# Optimizing a Trainium2 kernel written in Bass

```python
import numpy as np
import jax
import jax.numpy as jnp

def _softmax(x, axis=-1):
    return jax.nn.softmax(x, axis=axis)

def _gelu(x):
    return jax.nn.gelu(x, approximate=True)

def _silu(x):
    return jax.nn.silu(x)

def _sigmoid(x):
    return jax.nn.sigmoid(x)

def _layernorm(x, axis=-1, eps=1e-05):
    m = jnp.mean(x, axis=axis, keepdims=True)
    v = jnp.var(x, axis=axis, keepdims=True)
    return (x - m) / jnp.sqrt(v + eps)

def _scatter_add(tgt, idx, src, axis=0):
    return tgt.at[idx].add(src)

def _segment_sum(src, seg, n):
    return jax.ops.segment_sum(src, seg, n)
kernel_name = 'mk_gnn_ffn_d2_gnn_r64_fcb369'

def setup_inputs(seed: int=0):
    np.random.seed(seed)
    _w = jnp.asarray

    def _rec_inputs():
        import jax
        import jax.numpy as jnp
        _gk = jax.random.key(seed)
        x = -0.0003019 + 1 * jax.random.normal(jax.random.fold_in(_gk, 1), (10000, 1024), jnp.float32)
        src = jax.random.randint(jax.random.fold_in(_gk, 2), (5000,), 0, 10000, jnp.int32)
        dst = jnp.minimum((10000 * jax.random.uniform(jax.random.fold_in(_gk, 3), (5000,)) ** 2.0).astype(jnp.int32), 9999)
        _o = jnp.argsort(dst, stable=True)
        src = src[_o]
        dst = dst[_o]
        return (x, src, dst)
    x, src, dst = _rec_inputs()

    def _L0_gnn_setup():
        import jax, jax.numpy as jnp
        import numpy as np
        N = 20000
        E = 5000
        IN = 1024
        HID = 256
        H = 4
        D = HID // H
        OUT = 1024
        EPS = 1e-06
        NEG_SLOPE = 0.2
        key = jax.random.key(seed)
        ks = jax.random.split(key, 8)
        x = jax.random.normal(ks[0], (N, IN), dtype=jnp.float32)
        edge_index = jax.random.randint(ks[1], (2, E), 0, N, dtype=jnp.int64)
        s = 0.02
        return {'x': x, 'edge_index': edge_index, 'rms_w': jnp.ones((IN,), dtype=jnp.float32), 'W_down': jax.random.normal(ks[2], (IN, HID), dtype=jnp.float32) * s, 'Wl': jax.random.normal(ks[3], (HID, HID), dtype=jnp.float32) * s, 'Wr': jax.random.normal(ks[4], (HID, HID), dtype=jnp.float32) * s, 'att': jax.random.normal(ks[5], (H, D), dtype=jnp.float32) * s, 'W_up': jax.random.normal(ks[6], (HID, OUT), dtype=jnp.float32) * s}
    _L0_gnn_all = _L0_gnn_setup()
    _L0_gnn_in = {k: v for k, v in _L0_gnn_all.items() if k in ('rms_w', 'W_down', 'Wl', 'Wr', 'att', 'W_up')}
    del _L0_gnn_all

    def _L0_ffn_setup():
        import jax, jax.numpy as jnp
        import numpy as np
        QP = 127.0
        MIN_RANGE = 1e-06

        def _ste_round(x):
            return x + jax.lax.stop_gradient(jnp.round(x) - x)

        def _quant_per_tensor(x):
            scale = jnp.maximum(jnp.max(jnp.abs(x)), MIN_RANGE) / QP
            return (_ste_round(x / scale), scale)

        def _qlinear(x2d, w, b):
            xq, sx = _quant_per_tensor(x2d)
            wq, sw = _quant_per_tensor(w)
            out = jnp.matmul(xq, wq.T) + b[None, :]
            return out * (sw * sx)
        key = jax.random.key(seed)
        k = jax.random.split(key, 5)
        B, N, D, H = (8, 1024, 1024, 64)
        return {'x': jax.random.normal(k[0], (B, N, D), dtype=jnp.float32), 'w1': jax.random.normal(k[1], (H, D), dtype=jnp.float32) * 0.02, 'b1': jax.random.normal(k[2], (H,), dtype=jnp.float32) * 0.02, 'w2': jax.random.normal(k[3], (D, H), dtype=jnp.float32) * 0.02, 'b2': jax.random.normal(k[4], (D,), dtype=jnp.float32) * 0.02}
    _L0_ffn_all = _L0_ffn_setup()
    _L0_ffn_in = {k: v for k, v in _L0_ffn_all.items() if k in ('w1', 'b1', 'w2', 'b2')}
    del _L0_ffn_all

    def _L1_gnn_setup():
        import jax, jax.numpy as jnp
        import numpy as np
        N = 20000
        E = 5000
        D_IN = 1024
        D_OUT = 1024
        key = jax.random.key(seed)
        k1, k2, k3, k4 = jax.random.split(key, 4)
        x = jax.random.normal(k1, (N, D_IN), dtype=jnp.float32)
        edge_index = jax.random.randint(k2, (2, E), 0, N, dtype=jnp.int64)
        W = jax.random.normal(k3, (D_OUT, D_IN), dtype=jnp.float32) * (1.0 / np.sqrt(D_IN))
        b = jax.random.normal(k4, (D_OUT,), dtype=jnp.float32) * 0.01
        return {'x': x, 'edge_index': edge_index, 'W': W, 'b': b}
    _L1_gnn_all = _L1_gnn_setup()
    _L1_gnn_in = {k: v for k, v in _L1_gnn_all.items() if k in ('W', 'b')}
    del _L1_gnn_all

    def _L1_ffn_setup():
        import jax, jax.numpy as jnp
        import numpy as np
        DIM = 1024
        HIDDEN = 48
        SCALE = 1.0 / 127.0

        def _dequant(w_int, dtype):
            return w_int.astype(dtype) * jnp.asarray(SCALE, dtype)
        key = jax.random.key(seed)
        k_x, k_g, k_u, k_d = jax.random.split(key, 4)
        x = jax.random.normal(k_x, (4, 32, DIM), dtype=jnp.float32)
        w_gate = jax.random.randint(k_g, (HIDDEN, DIM), -127, 128, dtype=jnp.int32)
        w_up = jax.random.randint(k_u, (HIDDEN, DIM), -127, 128, dtype=jnp.int32)
        w_down = jax.random.randint(k_d, (DIM, HIDDEN), -127, 128, dtype=jnp.int32)
        return {'x': x, 'w_gate': w_gate, 'w_up': w_up, 'w_down': w_down}
    _L1_ffn_all = _L1_ffn_setup()
    _L1_ffn_in = {k: v for k, v in _L1_ffn_all.items() if k in ('w_gate', 'w_up', 'w_down')}
    del _L1_ffn_all
    return {'x': x, 'src': src, 'dst': dst, 'L0_gnn_rms_w': _L0_gnn_in['rms_w'], 'L0_gnn_W_down': _L0_gnn_in['W_down'], 'L0_gnn_Wl': _L0_gnn_in['Wl'], 'L0_gnn_Wr': _L0_gnn_in['Wr'], 'L0_gnn_att': _L0_gnn_in['att'], 'L0_gnn_W_up': _L0_gnn_in['W_up'], 'L0_ffn_w1': _L0_ffn_in['w1'], 'L0_ffn_b1': _L0_ffn_in['b1'], 'L0_ffn_w2': _L0_ffn_in['w2'], 'L0_ffn_b2': _L0_ffn_in['b2'], 'L1_gnn_W': _L1_gnn_in['W'], 'L1_gnn_b': _L1_gnn_in['b'], 'L1_ffn_w_gate': _L1_ffn_in['w_gate'], 'L1_ffn_w_up': _L1_ffn_in['w_up'], 'L1_ffn_w_down': _L1_ffn_in['w_down']}

def reference(x, src, dst, L0_gnn_rms_w, L0_gnn_W_down, L0_gnn_Wl, L0_gnn_Wr, L0_gnn_att, L0_gnn_W_up, L0_ffn_w1, L0_ffn_b1, L0_ffn_w2, L0_ffn_b2, L1_gnn_W, L1_gnn_b, L1_ffn_w_gate, L1_ffn_w_up, L1_ffn_w_down):
    import jax
    import jax.numpy as jnp

    def _L0_gnn_ref(x, edge_index, rms_w, W_down, Wl, Wr, att, W_up):
        import jax, jax.numpy as jnp
        import numpy as np
        N = 20000
        E = 5000
        IN = 1024
        HID = 256
        H = 4
        D = HID // H
        OUT = 1024
        EPS = 1e-06
        NEG_SLOPE = 0.2
        n = x.shape[0]
        ms = jnp.mean(jnp.square(x), axis=-1, keepdims=True)
        x = x * jax.lax.rsqrt(ms + EPS) * rms_w
        x = x @ W_down
        loop = jnp.arange(n, dtype=edge_index.dtype)
        src = jnp.concatenate([edge_index[0], loop])
        dst = jnp.concatenate([edge_index[1], loop])
        xl = (x @ Wl).reshape(n, H, D)
        xr = (x @ Wr).reshape(n, H, D)
        msg = xl[src] + xr[dst]
        act = jnp.where(msg > 0, msg, NEG_SLOPE * msg)
        e = jnp.einsum('ehd,hd->eh', act, att)
        m = jax.ops.segment_max(e, dst, num_segments=n)
        p = jnp.exp(e - m[dst])
        denom = jax.ops.segment_sum(p, dst, num_segments=n)
        alpha = p / (denom[dst] + 1e-16)
        out = jax.ops.segment_sum(alpha[..., None] * xl[src], dst, num_segments=n)
        out = out.reshape(n, HID)
        return out @ W_up

    def _L0_ffn_ref(x, w1, b1, w2, b2):
        import jax, jax.numpy as jnp
        import numpy as np
        QP = 127.0
        MIN_RANGE = 1e-06

        def _ste_round(x):
            return x + jax.lax.stop_gradient(jnp.round(x) - x)

        def _quant_per_tensor(x):
            scale = jnp.maximum(jnp.max(jnp.abs(x)), MIN_RANGE) / QP
            return (_ste_round(x / scale), scale)

        def _qlinear(x2d, w, b):
            xq, sx = _quant_per_tensor(x2d)
            wq, sw = _quant_per_tensor(w)
            out = jnp.matmul(xq, wq.T) + b[None, :]
            return out * (sw * sx)
        B, N, D = x.shape
        h = _qlinear(x.reshape(-1, D), w1, b1)
        h = jax.nn.gelu(h, approximate=False)
        o = _qlinear(h, w2, b2)
        return o.reshape(B, N, -1)

    def _L1_gnn_ref(x, edge_index, W, b):
        import jax, jax.numpy as jnp
        import numpy as np
        N = 20000
        E = 5000
        D_IN = 1024
        D_OUT = 1024
        num_nodes = x.shape[0]
        self_idx = jnp.arange(num_nodes, dtype=edge_index.dtype)
        ei = jnp.concatenate([edge_index, jnp.stack([self_idx, self_idx], axis=0)], axis=1)
        row, col = (ei[0], ei[1])
        h = jnp.einsum('nd,od->no', x, W) + b
        deg = jnp.zeros((num_nodes,), dtype=h.dtype).at[row].add(1.0)
        deg_inv_sqrt = deg ** (-0.5)
        norm = deg_inv_sqrt[row] * deg_inv_sqrt[col]
        msg = norm[:, None] * h[col]
        out = jax.ops.segment_sum(msg, row, num_segments=num_nodes)
        return out

    def _L1_ffn_ref(x, w_gate, w_up, w_down):
        import jax, jax.numpy as jnp
        import numpy as np
        DIM = 1024
        HIDDEN = 48
        SCALE = 1.0 / 127.0

        def _dequant(w_int, dtype):
            return w_int.astype(dtype) * jnp.asarray(SCALE, dtype)
        wg = _dequant(w_gate, x.dtype)
        wu = _dequant(w_up, x.dtype)
        wd = _dequant(w_down, x.dtype)
        gate = jnp.einsum('bsd,hd->bsh', x, wg)
        up = jnp.einsum('bsd,hd->bsh', x, wu)
        h = jax.nn.silu(gate) * up
        return jnp.einsum('bsh,dh->bsd', h, wd)
    edge_index = jnp.stack([src, dst])
    x = x + _L0_gnn_ref(_layernorm(x, axis=-1), edge_index, L0_gnn_rms_w, L0_gnn_W_down, L0_gnn_Wl, L0_gnn_Wr, L0_gnn_att, L0_gnn_W_up)
    x = x + _L0_ffn_ref(_layernorm(x, axis=-1)[None], L0_ffn_w1, L0_ffn_b1, L0_ffn_w2, L0_ffn_b2)[0]
    x = x + _L1_gnn_ref(_layernorm(x, axis=-1), edge_index, L1_gnn_W, L1_gnn_b)
    x = x + _L1_ffn_ref(_layernorm(x, axis=-1)[None], L1_ffn_w_gate, L1_ffn_w_up, L1_ffn_w_down)[0]
    return x

_drawn_inputs = setup_inputs


def setup_inputs(seed=0):
    import zlib

    import numpy as np

    out = dict(_drawn_inputs(seed))
    spreads = {'L0_gnn_rms_w': (1.0, 0.6)}
    factors = {'L0_gnn_Wr': 63.54, 'L0_gnn_att': 35.962, 'L0_ffn_b2': 64.0, 'L1_gnn_b': 4.807}
    for name, (base, spread) in spreads.items():
        noise = np.random.default_rng([zlib.crc32(name.encode()), seed]).standard_normal(out[name].shape)
        drawn = base * np.exp(spread * noise) if base else spread * noise
        out[name] = jnp.asarray(drawn.astype(out[name].dtype))
    for name, factor in factors.items():
        out[name] = (out[name] * factor).astype(out[name].dtype)
    return out
```

```python
from contextlib import ExitStack

import concourse.bass as bass
from concourse import mybir

FP32 = mybir.dt.float32
BF16 = mybir.dt.bfloat16
I32 = mybir.dt.int32
ALU = mybir.AluOpType
ACT = mybir.ActivationFunctionType
AX = mybir.AxisListType
RMAX = bass.bass_isa.ReduceOp.absmax

P = 128
N, D, E = 10000, 1024, 5000
HID, HEADS, FFN1, FFN2 = 256, 4, 64, 48
HD = HID // HEADS
KT = D // P
TPB = 4
BLK = TPB * P
NB = -(-N // BLK)
NP = NB * BLK
NT = NP // P
ET = -(-E // P)
EP = ET * P
UPROW = 64
LN_EPS, RMS_EPS, DEN_EPS = 1e-5, 1e-6, 1e-16
SLOPE, QP, MIN_RANGE = 0.2, 127.0, 1e-6
MAGIC = 1.5 * 2.0 ** 23
SKIP = float(2 ** 20)
FAR = -1.0e30
LEAD = 16


class Chain:

    def __init__(self, eng, sem, base=0):
        self.eng, self.sem, self.base, self.n = eng, sem, base, 0

    def link(self, ins):
        self.n += 1
        ins.then_inc(self.sem, 1)
        self.eng.wait_ge(self.sem, self.base + self.n)


def rsqrt_rest(nc, ch, var, sd, r, tmp):
    ch.link(nc.vector.reciprocal(r, sd))
    ch.link(nc.vector.tensor_tensor(tmp, r, r, ALU.mult))
    ch.link(nc.vector.tensor_tensor(tmp, tmp, var, ALU.mult))
    ch.link(nc.vector.tensor_scalar(tmp, tmp, -0.5, 1.5, ALU.mult, ALU.add))
    ch.link(nc.vector.tensor_tensor(r, r, tmp, ALU.mult))


def build(nc, x, xT, src_row, dst_row, src_col, dst_col, rms_w, W_down, Wl, Wr, att, W_up,
          w1T, b1, w2T, b2, gcnT, gcn_b, w_gateT, w_upT, w_downT, ident_in, out):
    T = nc.dram_tensor("node_rows", [NP, 2 * HID], FP32).ap()
    X1 = nc.dram_tensor("x1_rows", [NP, D], FP32).ap()
    X3 = nc.dram_tensor("x3_rows", [NP, D], FP32).ap()
    HP = nc.dram_tensor("h_rows", [NP, D], FP32).ap()
    DIS_D = nc.dram_tensor("dis_rows", [NP, 1], FP32).ap()
    by_src = [nc.dram_tensor(f"by_src_{n}", [EP, 1], FP32).ap() for n in ("src", "dst")]
    by_dst = [nc.dram_tensor(f"by_dst_{n}", [EP, 1], FP32).ap() for n in ("dst", "src")]
    T_half = T.rearrange("n (h c) -> (n h) c", h=2)

    keep = ExitStack()
    n_sem = [0]

    def maker(ctx):
        def sb(name, shape, dt=FP32):
            return ctx.enter_context(nc.sbuf_tensor(name, shape, dt))

        def ps(name, shape, dt=FP32):
            return ctx.enter_context(nc.psum_tensor(name, shape, dt))

        def sem(name):
            n_sem[0] += 1
            return ctx.enter_context(nc.semaphore(name))
        return sb, ps, sem

    def rows(ap, i, b, width):
        return ap[bass.ds(i * (2 * BLK) + b * BLK, BLK), 0:width].rearrange("(j p) d -> p j d", p=P)

    with keep:
        sbk, _, _ = maker(keep)
        ident = sbk("ident", [P, P])
        identb = sbk("identb", [P, P], BF16)
        dis = sbk("dis", [P, NT])
        e127 = sbk("e127", [P, 1])
        scal = sbk("scal", [P, 16])
        w1q = sbk("w1q", [P, KT, FFN1], BF16)
        w2q = sbk("w2q", [FFN1 + 3, D], BF16)
        b1c = sbk("b1c", [FFN1, 2])

        with ExitStack() as ctx:
            sb, ps, sem = maker(ctx)
            key_int = [sb(f"key_int{k}", [P, EP], I32) for k in range(2)]
            key = [sb(f"key{k}", [P, EP]) for k in range(2)]
            col_int = [sb(f"col_int{k}", [P, ET], I32) for k in range(2)]
            col = [sb(f"col{k}", [P, ET]) for k in range(2)]
            colq = [sb(f"colq{k}", [P, ET]) for k in range(2)]
            junk = sb("junk", [P, EP], BF16)
            junk_act = sb("junk_act", [P, EP], BF16)
            junk_diag = sb("junk_diag", [P, P], BF16)
            count = [sb(f"count{k}", [P, ET]) for k in range(2)]
            ties = [sb(f"ties{k}", [P, ET]) for k in range(2)]
            pos = [sb(f"pos{k}", [P, ET], I32) for k in range(2)]
            tri = sb("tri", [P, P])
            iota = sb("iota", [P, P])
            hi_int = sb("hi_int", [P, ET], I32)
            lo_int = sb("lo_int", [P, ET], I32)
            hi = sb("hi", [P, ET])
            lo = sb("lo", [P, ET])
            one_lo = sb("one_lo", [P, 2, P], BF16)
            one_hi = sb("one_hi", [P, 2, NT], BF16)
            zero = sb("zero", [P, P], BF16)
            deg = sb("deg", [P, 3, NT])
            w1 = sb("w1", [P, KT, FFN1])
            w2 = sb("w2", [FFN1, D])
            b2r = sb("b2r", [1, 2, D])
            b2p = sb("b2p", [1, 3, D], BF16)
            wmax = sb("wmax", [P, 2])
            hist = ps("hist", [P, NT])

            loaded = [sem(f"keys_loaded{k}") for k in range(2)]
            s_w = sem("small_weights")
            s_const = sem("constants")
            s_chain = sem("sort_dve_chain")
            s_key = sem("keys_ready")
            s_sign = sem("dst_counted")
            s_shift = sem("dst_shifted")
            s_hot = sem("onehots_ready")
            s_hist = sem("hist_step")
            s_pos = sem("ranks_ready")
            s_scat = sem("scattered")
            s_deg = sem("degree_ready")
            s_sd = sem("degree_sqrt")
            s_wmax = sem("weight_max")
            s_wall = sem("weight_max_all")
            s_b2 = sem("b2_parts")
            s_b2in = sem("b2_in")
            s_dis = sem("dis_ready")
            s_end = sem("sort_stores")

            with nc.Block() as block:
                @block.sync
                def _(sp):
                    for s in (s_shift, s_hist):
                        sp.sem_inc(s, LEAD)
                    for k, (r, c) in enumerate(((src_row, src_col), (dst_row, dst_col))):
                        sp.dma_start(key_int[k][:, :], r.partition_broadcast(P)).then_inc(loaded[k], 16)
                        sp.dma_start(col_int[k][:, :], c).then_inc(loaded[k], 16)
                    for dst, s in ((ident[:, :], ident_in), (w2[:, :], w2T), (b2r[:, 0, :], b2), (b1c[:, 0:1], b1)):
                        sp.dma_start(dst, s).then_inc(s_w, 16)
                    sp.dma_start(w1[:, :, :], w1T.rearrange("(k p) h -> p k h", p=P)).then_inc(s_w, 16)
                    sp.wait_ge(s_b2, 1)
                    for k in range(3):
                        sp.dma_start(w2q[FFN1 + k:FFN1 + k + 1, :], b2p[:, k, :]).then_inc(s_b2in, 16)
                    sp.wait_ge(s_b2in, 48)
                    sp.wait_ge(s_dis, 1)
                    with nc.allow_non_contiguous_dma(reason="one value of every node"):
                        sp.dma_start(DIS_D.rearrange("(t p) o -> p (t o)", p=P), dis[:, :]).then_inc(s_end, 16)
                    sp.wait_ge(s_end, 16)

                @block.gpsimd
                def _(pool):
                    nc.gpsimd.memset(tri[:, :], 1.0).then_inc(s_const, 1)
                    nc.gpsimd.memset(e127[:, :], 0.0).then_inc(s_const, 1)
                    nc.gpsimd.iota(iota[:, :], [[1, P]], base=0, channel_multiplier=0,
                                   allow_small_or_imprecise_dtypes=True).then_inc(s_const, 1)
                    nc.gpsimd.memset(zero[:, :], 0.0).then_inc(s_const, 1)
                    nc.gpsimd.memset(wmax[:, :], 0.0).then_inc(s_const, 1)
                    pool.wait_ge(s_const, 5)
                    nc.gpsimd.affine_select(tri[:, :], tri[:, :], [[-1, P]], ALU.is_gt, 0.0, base=0,
                                            channel_multiplier=1).then_inc(s_const, 1)
                    nc.gpsimd.affine_select(e127[:, :], e127[:, :], [[0, 1]], ALU.not_equal, 1.0, base=-(P - 1),
                                            channel_multiplier=1).then_inc(s_const, 1)
                    pool.wait_ge(s_wmax, 1)
                    nc.gpsimd.partition_all_reduce(wmax[:, :], wmax[:, :], P, RMAX).then_inc(s_wall, 1)
                    pool.wait_ge(s_pos, 1)
                    for k, table in enumerate((by_src, by_dst)):
                        for t in range(ET):
                            for j in range(2):
                                nc.gpsimd.indirect_dma_start(
                                    table[j], bass.IndirectOffsetOnAxis(ap=pos[k][:, t:t + 1], axis=0),
                                    col[k ^ j][:, t:t + 1], None).then_inc(s_scat, 16)
                    pool.wait_ge(s_scat, 16 * 4 * ET)

                @block.scalar
                def _(act):
                    act.wait_ge(s_key, 1)
                    with act.Fori(0, ET) as t:
                        act.wait_ge(s_shift, LEAD + t)
                        nc.scalar.activation(junk_act[:, :], key[1][:, :], ACT.Sign, bias=col[1][:, bass.ds(t, 1)],
                                             scale=-1.0, accum_out=count[1][:, bass.ds(t, 1)]).then_inc(s_sign, 1)
                    act.wait_ge(s_deg, 1)
                    nc.scalar.activation(deg[:, 1, :], deg[:, 0, :], ACT.Sqrt).then_inc(s_sd, 1)

                @block.vector
                def _(dve):
                    ch = Chain(dve, s_chain)
                    for k in range(2):
                        dve.wait_ge(loaded[k], 32)
                        ch.link(nc.vector.tensor_scalar(key[k][:, :], key_int[k][:, :], 0.25, None, ALU.add))
                        ch.link(nc.vector.tensor_copy(col[k][:, :], col_int[k][:, :]))
                        ch.link(nc.vector.tensor_scalar(colq[k][:, :], col_int[k][:, :], 0.25, None, ALU.add))
                    ch.link(nc.vector.tensor_scalar(lo_int[:, :], col_int[0][:, :], P - 1, None, ALU.bitwise_and))
                    ch.link(nc.vector.tensor_scalar(hi_int[:, :], col_int[0][:, :], 7, None, ALU.arith_shift_right))
                    ch.link(nc.vector.tensor_copy(lo[:, :], lo_int[:, :]))
                    ch.link(nc.vector.tensor_copy(hi[:, :], hi_int[:, :]))
                    dve.wait_ge(s_w, 16 * 5)
                    dve.wait_ge(s_const, 7)
                    ch.link(nc.vector.tensor_reduce(wmax[:, 0:1], w1[:, :, :], AX.XY, ALU.max, apply_absolute_value=True))
                    nc.vector.tensor_reduce(wmax[0:FFN1, 1:2], w2[:, :], AX.X, ALU.max,
                                            apply_absolute_value=True).then_inc(s_wmax, 1)
                    ch.link(nc.vector.tensor_copy(identb[:, :], ident[:, :]))
                    dve.wait_ge(s_wall, 1)
                    ch.link(nc.vector.tensor_scalar(scal[:, 0:2], wmax[:, :], MIN_RANGE, 1.0 / QP, ALU.max, ALU.mult))
                    ch.link(nc.vector.reciprocal(scal[:, 2:4], scal[:, 0:2]))
                    ch.link(nc.vector.tensor_scalar(w1[:, :, :], w1[:, :, :], scal[:, 2:3], MAGIC, ALU.mult, ALU.add))
                    ch.link(nc.vector.tensor_scalar(w1q[:, :, :], w1[:, :, :], -MAGIC, None, ALU.add))
                    ch.link(nc.vector.tensor_scalar(w2[:, :], w2[:, :], scal[0:FFN1, 3:4], MAGIC, ALU.mult, ALU.add))
                    ch.link(nc.vector.tensor_scalar(w2q[0:FFN1, :], w2[:, :], -MAGIC, None, ALU.add))
                    for k in range(3):
                        ch.link(nc.vector.tensor_copy(b2p[:, k, :], b2r[:, k % 2, :]))
                        if k < 2:
                            ch.link(nc.vector.tensor_tensor(b2r[:, (k + 1) % 2, :], b2r[:, k % 2, :], b2p[:, k, :],
                                                            ALU.subtract))
                    dve.sem_inc(s_b2, 1)
                    dve.sem_inc(s_key, 1)
                    base = ch.n
                    STEPS = 5
                    with dve.Fori(0, ET // 2) as i:
                        for u in range(2):
                            t = i * 2 + u
                            c1 = bass.ds(t, 1)
                            here = bass.ds(t * P, P)
                            ch = Chain(dve, s_chain, t * STEPS + base)
                            if u == 0:
                                dve.wait_ge(s_hist, LEAD + i * 2)
                            nc.vector.tensor_scalar(one_lo[:, u, :], iota[:, :], lo[:, c1], None, ALU.is_equal)
                            nc.vector.tensor_scalar(one_hi[:, u, :], iota[:, 0:NT], hi[:, c1], None,
                                                    ALU.is_equal).then_inc(s_hot, 1)
                            ch.link(nc.vector.tensor_scalar(junk[:, :], key[0][:, :], col[0][:, c1], None, ALU.is_lt,
                                                            ALU.add, accum_out=count[0][:, c1]))
                            for k in range(2):
                                ch.link(nc.vector.scalar_tensor_tensor(
                                    junk_diag[:, :], key[k][:, here], colq[k][:, c1], tri[:, :], ALU.is_equal,
                                    ALU.mult, accum_out=ties[k][:, c1]))
                            ch.link(nc.vector.tensor_scalar(key[0][:, here], key[0][:, here], -0.5, None, ALU.add))
                            dve.wait_ge(s_sign, t + 1)
                            ch.link(nc.vector.tensor_scalar(key[1][:, here], key[1][:, here], -0.5, None, ALU.add))
                            dve.sem_inc(s_shift, 1)
                            assert ch.n == STEPS
                    ch = Chain(dve, s_chain, base + STEPS * ET)
                    ch.link(nc.vector.tensor_scalar(count[1][:, :], count[1][:, :], float(EP), 0.5, ALU.add, ALU.mult))
                    for k in range(2):
                        ch.link(nc.vector.tensor_tensor(ties[k][:, :], ties[k][:, :], count[k][:, :], ALU.add))
                        ch.link(nc.vector.tensor_copy(pos[k][:, :], ties[k][:, :]))
                    dve.sem_inc(s_pos, 1)
                    dve.wait_ge(s_hist, LEAD + ET + 1)
                    nc.vector.tensor_scalar(deg[:, 0, :], hist[:, :], 1.0, None, ALU.add).then_inc(s_deg, 1)
                    dve.wait_ge(s_sd, 1)
                    rsqrt_rest(nc, ch, deg[:, 0, :], deg[:, 1, :], dis[:, :], deg[:, 2, :])
                    dve.sem_inc(s_dis, 1)

                @block.tensor
                def _(pe):
                    pe.wait_ge(s_const, 7)
                    nc.tensor.matmul(hist[:, :], zero[:, :], zero[:, 0:NT], start=True, stop=False)
                    with pe.Fori(0, ET // 2) as i:
                        for u in range(2):
                            pe.wait_ge(s_hot, i * 2 + u + 1)
                            nc.tensor.matmul(hist[:, :], one_lo[:, u, :], one_hi[:, u, :], start=False,
                                             stop=False).then_inc(s_hist, 1)
                    nc.tensor.matmul(hist[:, :], zero[:, :], zero[:, 0:NT], start=False, stop=True).then_inc(s_hist, 1)

        with ExitStack() as ctx:
            sb, ps, sem = maker(ctx)
            wd = sb("wd", [P, KT, HID])
            wlr = sb("wlr", [P, 2, 2 * HID])
            rms = sb("rms", [P, KT])
            mean_of = sb("mean_of", [P, P])
            xt = sb("xt", [P, 2, KT, BLK])
            xb = sb("xb", [P, 2, TPB, D])
            xdT = sb("xdT", [P, 2, 2, BLK])
            lr = sb("lr", [P, 2, TPB, 2 * HID])
            st = sb("st", [P, 2, TPB, 2, 6])
            mv = sb("mv", [P, 2, TPB, 2])
            small = sb("small", [P, 2, 4, TPB])
            p_xd = ps("p_xd", [P, 2, 2, BLK])
            p_lr = ps("p_lr", [P, TPB, 2 * HID])

            s_w = sem("project_weights")
            s_chain = sem("project_chain")
            s_wf = sem("wd_folded")
            s_mean = sem("wd_mean")
            s_wc = sem("wd_centred")
            s_xt = [sem(f"xT_loaded{s}") for s in range(2)]
            s_xb = [sem(f"x_loaded{s}") for s in range(2)]
            s_xt_free = sem("xT_used")
            s_xb_free = sem("x_used")
            s_xd = sem("xd_in_psum")
            s_xde = sem("xd_copied")
            s_lr = sem("lr_in_psum")
            s_lre = sem("lr_copied")
            s_var = sem("var_ready")
            s_sd = sem("sd_ready")
            s_r = sem("scale_ready")
            s_lrfree = [sem(f"lr_stored{s}") for s in range(2)]
            with nc.Block() as block:
                @block.sync
                def _(sp):
                    for s in (s_xde, s_lre, *s_lrfree):
                        sp.sem_inc(s, LEAD)
                    sp.dma_start(wd[:, :, :], W_down.rearrange("(k p) h -> p k h", p=P)).then_inc(s_w, 16)
                    sp.dma_start(rms[:, :], rms_w).then_inc(s_w, 16)
                    for k, w in enumerate((Wl, Wr)):
                        sp.dma_start(wlr[:, :, k * HID:(k + 1) * HID],
                                     w.rearrange("(k p) h -> p k h", p=P)).then_inc(s_w, 16)
                    with sp.Fori(0, NB // 2) as i:
                        for s in range(2):
                            b = i * 2 + s
                            sp.wait_ge(s_xt_free, b + 1)
                            sp.dma_start(xt[:, s], xT[:, bass.ds(b * BLK, BLK)].rearrange(
                                "(k p) n -> p k n", p=P)).then_inc(s_xt[s], 16)
                            sp.wait_ge(s_xb_free, b + 1)
                            sp.dma_start(xb[:, s], rows(x, i, s, D)).then_inc(s_xb[s], 16)

                @block.tensor
                def _(pe):
                    pe.wait_ge(s_wf, 1)
                    for k in range(KT):
                        last = nc.tensor.matmul(p_lr[:, 0, 0:HID], mean_of[:, :], wd[:, k, :], start=(k == 0),
                                                stop=(k == KT - 1))
                    last.then_inc(s_mean, 1)
                    pe.wait_ge(s_wc, 1)
                    pe.sem_inc(s_xt_free, 2)
                    with pe.Fori(0, NB // 2) as i:
                        for s in range(2):
                            b = i * 2 + s
                            pe.wait_ge(s_xt[s], i * 16 + 16)
                            pe.wait_ge(s_xde, LEAD + b * 2)
                            for m in range(2):
                                for k in range(KT):
                                    last = nc.tensor.matmul(p_xd[:, s, m, :], wd[:, k, m * P:(m + 1) * P],
                                                            xt[:, s, k, :], start=(k == 0), stop=(k == KT - 1))
                                last.then_inc(s_xd, 1)
                            pe.wait_ge(s_xde, LEAD + b * 2 + 2)
                            for j in range(TPB):
                                pe.wait_ge(s_lre, LEAD + b * TPB + j)
                                for m in range(2):
                                    last = nc.tensor.matmul(p_lr[:, j, :], xdT[:, s, m, j * P:(j + 1) * P],
                                                            wlr[:, m, :], start=(m == 0), stop=(m == 1))
                                last.then_inc(s_lr, 1)

                @block.scalar
                def _(act):
                    with act.Fori(0, NB // 2) as i:
                        for s in range(2):
                            b = i * 2 + s
                            act.wait_ge(s_var, b + 1)
                            nc.scalar.activation(small[:, s, 1, :], small[:, s, 0, :], ACT.Sqrt).then_inc(s_sd, 1)
                            for m in range(2):
                                act.wait_ge(s_xd, b * 2 + m + 1)
                                ins = nc.scalar.activation(xdT[:, s, m, :], p_xd[:, s, m, :], ACT.Copy)
                                ins.then_inc(s_xde, 1)
                            act.sem_inc(s_xt_free, 1)
                            act.wait_ge(s_r, b + 1)
                            act.wait_ge(s_lrfree[s], LEAD + i * 16)
                            for j in range(TPB):
                                act.wait_ge(s_lr, b * TPB + j + 1)
                                nc.scalar.activation(lr[:, s, j, :], p_lr[:, j, :], ACT.Copy,
                                                     scale=small[:, s, 2, j:j + 1]).then_inc(s_lre, 1)
                            act.wait_ge(s_lre, LEAD + b * TPB + TPB)
                            act.dma_start(rows(T, i, s, 2 * HID), lr[:, s]).then_inc(s_lrfree[s], 16)
                    for s in range(2):
                        act.wait_ge(s_lrfree[s], LEAD + NB // 2 * 16)

                @block.vector
                def _(dve):
                    ch = Chain(dve, s_chain)
                    nc.vector.memset(mean_of[:, :], 1.0 / D)
                    dve.wait_ge(s_w, 64)
                    for k in range(KT):
                        last = nc.vector.tensor_scalar(wd[:, k, :], wd[:, k, :], rms[:, k:k + 1], None, ALU.mult)
                    ch.link(last)
                    dve.sem_inc(s_wf, 1)
                    dve.wait_ge(s_mean, 1)
                    for k in range(KT):
                        last = nc.vector.tensor_tensor(wd[:, k, :], wd[:, k, :], p_lr[:, 0, 0:HID], ALU.subtract)
                    ch.link(last)
                    dve.sem_inc(s_wc, 1)
                    dve.sem_inc(s_xb_free, 2)
                    base = ch.n
                    STEPS = 8
                    with dve.Fori(0, NB // 2) as i:
                        for s in range(2):
                            b = i * 2 + s
                            ch = Chain(dve, s_chain, b * STEPS + base)
                            dve.wait_ge(s_xb[s], i * 16 + 16)
                            for j in range(TPB):
                                for h in range(2):
                                    last = nc.vector.bn_stats(st[:, s, j, h, :], xb[:, s, j, h * 512:(h + 1) * 512])
                            ch.link(last)
                            dve.sem_inc(s_xb_free, 1)
                            dve.wait_ge(s_lre, LEAD + b * TPB)
                            nc.vector.memset(small[:, s, 3, :], 0.0)
                            for j in range(TPB):
                                last = nc.vector.bn_aggr(mv[:, s, j, :], st[:, s, j])
                            ch.link(last)
                            ch.link(nc.vector.tensor_scalar(small[:, s, 0, :], mv[:, s, :, 1], 1.0 + RMS_EPS,
                                                            LN_EPS * RMS_EPS, ALU.mult, ALU.add))
                            dve.sem_inc(s_var, 1)
                            dve.wait_ge(s_sd, b + 1)
                            rsqrt_rest(nc, ch, small[:, s, 0, :], small[:, s, 1, :], small[:, s, 2, :],
                                       small[:, s, 3, :])
                            assert ch.n == STEPS, ch.n
                            dve.sem_inc(s_r, 1)

        with ExitStack() as ctx:
            sb, ps, sem = maker(ctx)
            XS = sb("XS", [P, ET, HID])
            XLD = sb("XLD", [P, ET, HID])
            KB = sb("KB", [P, EP])
            a_row = sb("a_row", [P, HID])
            lg = [sb(f"lg{k}", [HEADS, EP]) for k in range(4)]
            step = sb("step", [HEADS, EP + 1], BF16)
            cols = sb("cols", [P, 4, ET])
            prev = sb("prev", [P, 1 + ET])
            idx = sb("idx", [P, 4, ET], I32)
            msg = sb("msg", [P, 2, 2 * HID])
            lgc = sb("lgc", [P, 2, 2 * HEADS])
            pw = sb("pw", [P, 3, ET * HEADS])
            SM = sb("SM", [P, 2, 2, P])
            OS = sb("OS", [P, 2, HID])
            p_lg = ps("p_lg", [HEADS, 2, 4, P])
            p_w = ps("p_w", [P, 3, ET * HEADS])
            p_o = ps("p_o", [P, 2, 512])
            s_in = sem("edges_loaded")
            s_chain = sem("attend_chain")
            s_idx = sem("attend_indices")
            s_g = [sem(f"edge_rows{t}") for t in range(2)]
            s_gx = sem("self_rows")
            s_lgc = sem("logits_ready")
            s_lgt = sem("logits_turned")
            s_lge = sem("logits_copied")
            s_dif = sem("shifted_logits")
            s_exp = sem("exps_ready")
            s_sc = sem("scans_ready")
            s_pt = sem("weights_turned")
            s_v = sem("weighted_rows")
            s_o = sem("sums_in_psum")
            s_oe = sem("sums_copied")
            s_res = sem("rows_ready")
            s_sct = sem("rows_scattered")
            NE = ET // 2
            with nc.Block() as block:
                @block.sync
                def _(sp):
                    for s in (s_lgt, s_lge, s_oe, s_res, s_o):
                        sp.sem_inc(s, LEAD)
                    sp.dma_start(KB[:, :], by_dst[0][:, 0].partition_broadcast(P)).then_inc(s_in, 16)
                    with nc.allow_non_contiguous_dma(reason="one value of every edge"):
                        sp.dma_start(cols[:, 0, :], by_dst[0].rearrange("(t p) o -> p (t o)", p=P)).then_inc(s_in, 16)
                        sp.dma_start(cols[:, 1, :], by_dst[1].rearrange("(t p) o -> p (t o)", p=P)).then_inc(s_in, 16)
                        sp.dma_start(cols[:, 2, 0:ET - 1], by_dst[0][1:EP - P + 1].rearrange(
                            "(t p) o -> p (t o)", p=P)).then_inc(s_in, 16)
                        sp.dma_start(cols[0:P - 1, 2, ET - 1:ET], by_dst[0][EP - P + 1:EP]).then_inc(s_in, 16)
                        sp.dma_start(cols[P - 1:P, 2, ET - 1:ET], by_dst[0][0:1]).then_inc(s_in, 16)
                    sp.dma_start(a_row[:, :], att.partition_broadcast(P)).then_inc(s_in, 16)

                @block.gpsimd
                def _(pool):
                    pool.wait_ge(s_idx, 1)
                    for t in range(ET):
                        s = t % 2
                        if t >= 2:
                            pool.wait_ge(s_lgc, t - 1)
                        nc.gpsimd.indirect_dma_start(XS[:, t, :], None, T_half, bass.IndirectOffsetOnAxis(
                            ap=idx[:, 1, t:t + 1], axis=0)).then_inc(s_g[s], 16)
                        nc.gpsimd.indirect_dma_start(XLD[:, t, :], None, T_half, bass.IndirectOffsetOnAxis(
                            ap=idx[:, 0, t:t + 1], axis=0)).then_inc(s_g[s], 16)
                        nc.gpsimd.indirect_dma_start(msg[:, s, HID:2 * HID], None, T_half, bass.IndirectOffsetOnAxis(
                            ap=idx[:, 2, t:t + 1], axis=0)).then_inc(s_g[s], 16)
                    for t in range(ET):
                        pool.wait_ge(s_res, LEAD + t + 1)
                        nc.gpsimd.indirect_dma_start(
                            T_half, bass.IndirectOffsetOnAxis(ap=idx[:, 3, t:t + 1], axis=0),
                            XLD[:, t, :], None, bounds_check=2 * NP - 1, oob_is_err=False).then_inc(s_sct, 16)
                    pool.wait_ge(s_sct, 16 * ET)

                @block.scalar
                def _(act):
                    for k in range(2):
                        act.wait_ge(s_dif, k + 1)
                        nc.scalar.activation(lg[k][:, :], lg[k][:, :], ACT.Exp).then_inc(s_exp, 1)
                    with act.Fori(0, NE) as i:
                        for s in range(2):
                            act.wait_ge(s_o, LEAD + i * 2 + s + 1)
                            act.wait_ge(s_res, LEAD + i * 2 + s)
                            nc.scalar.activation(OS[:, s, :], p_o[:, s, 0:HID], ACT.Copy).then_inc(s_oe, 1)

                @block.vector
                def _(dve):
                    ch = Chain(dve, s_chain)
                    dve.wait_ge(s_in, 16 * 7)
                    ch.link(nc.vector.tensor_scalar(idx[:, 0, :], cols[:, 0, :], 2.0, None, ALU.mult))
                    ch.link(nc.vector.tensor_scalar(idx[:, 1, :], cols[:, 1, :], 2.0, None, ALU.mult))
                    ch.link(nc.vector.tensor_scalar(idx[:, 2, :], cols[:, 0, :], 2.0, 1.0, ALU.mult, ALU.add))
                    dve.sem_inc(s_idx, 1)
                    ch.link(nc.vector.memset(prev[:, 0:1], -1.0))
                    ch.link(nc.vector.tensor_copy(prev[:, 1:1 + ET], cols[:, 0, :]))
                    ch.link(nc.vector.memset(OS[:, :, :], 0.0))
                    ch.link(nc.vector.tensor_tensor(cols[:, 3, :], cols[:, 0, :], cols[:, 2, :], ALU.is_equal))
                    ch.link(nc.vector.tensor_scalar(cols[:, 3, :], cols[:, 3, :], SKIP, None, ALU.mult))
                    ch.link(nc.vector.tensor_tensor(cols[:, 3, :], cols[:, 3, :], cols[:, 0, :], ALU.add))
                    ch.link(nc.vector.tensor_scalar(idx[:, 3, :], cols[:, 3, :], 2.0, None, ALU.mult))
                    ch.link(nc.vector.memset(step[:, :], 0.0))
                    ch.link(nc.vector.tensor_tensor(step[:, 1:EP], KB[0:HEADS, 1:EP], KB[0:HEADS, 0:EP - 1],
                                                    ALU.is_equal))
                    ch.link(nc.vector.tensor_scalar(step[:, :], step[:, :], -FAR, FAR, ALU.mult, ALU.add))
                    base = ch.n
                    STEPS = 4
                    with dve.Fori(0, NE) as i:
                        for s in range(2):
                            t = i * 2 + s
                            ch = Chain(dve, s_chain, t * STEPS + base)
                            dve.wait_ge(s_g[s], i * 48 + 48)
                            ch.link(nc.vector.tensor_tensor(
                                msg[:, s, 0:HID], XS[:, bass.ds(t, 1), :].rearrange("p o c -> p (o c)"),
                                msg[:, s, HID:2 * HID], ALU.add))
                            ch.link(nc.vector.tensor_tensor(
                                msg[:, s, HID:2 * HID], XLD[:, bass.ds(t, 1), :].rearrange("p o c -> p (o c)"),
                                msg[:, s, HID:2 * HID], ALU.add))
                            ch.link(nc.vector.scalar_tensor_tensor(msg[:, s, :], msg[:, s, :], SLOPE, msg[:, s, :],
                                                                   ALU.mult, ALU.max))
                            ch.link(nc.vector.tensor_tensor(
                                msg[:, s, :].rearrange("p (a c) -> p a c", a=2),
                                msg[:, s, :].rearrange("p (a c) -> p a c", a=2),
                                a_row[:, None, :].broadcast_to([P, 2, HID]), ALU.mult))
                            dve.wait_ge(s_lgt, LEAD + t)
                            nc.vector.tensor_reduce(lgc[:, s, :], msg[:, s, :].rearrange("p (a c) -> p a c", c=HD),
                                                    AX.X, ALU.add).then_inc(s_lgc, 1)
                            if s == 1:
                                dve.wait_ge(s_lgt, LEAD + t + 1)
                                for k in range(2):
                                    last = nc.vector.tensor_copy(
                                        lg[k][:, bass.ds(i * 2 * P, 2 * P)],
                                        p_lg[:, k, 0:2, :].rearrange("h a e -> h (a e)"))
                                last.then_inc(s_lge, 1)
                    ch = Chain(dve, s_chain, base + STEPS * ET)
                    dve.wait_ge(s_lge, LEAD + NE)
                    ch.link(nc.vector.tensor_tensor_scan(lg[2][:, :], step[:, 0:EP], lg[0][:, :], FAR, ALU.add, ALU.max))
                    ch.link(nc.vector.tensor_tensor_scan(lg[3][:, ::-1], step[:, 1:EP + 1][:, ::-1], lg[0][:, ::-1],
                                                         FAR, ALU.add, ALU.max))
                    ch.link(nc.vector.tensor_tensor(lg[2][:, :], lg[2][:, :], lg[3][:, :], ALU.max))
                    ch.link(nc.vector.tensor_tensor(lg[2][:, :], lg[2][:, :], lg[1][:, :], ALU.max))
                    for k in range(2):
                        nc.vector.tensor_tensor(lg[k][:, :], lg[k][:, :], lg[2][:, :],
                                                ALU.subtract).then_inc(s_dif, 1)
                    ch.link(nc.vector.tensor_scalar(step[:, :], step[:, :], 0.0, None, ALU.is_ge))
                    dve.wait_ge(s_exp, 2)
                    ch.link(nc.vector.tensor_tensor_scan(lg[3][:, :], step[:, 0:EP], lg[0][:, :], 0.0, ALU.mult, ALU.add))
                    ch.link(nc.vector.tensor_tensor(lg[3][:, :], lg[3][:, :], lg[1][:, :], ALU.add))
                    ch.link(nc.vector.tensor_scalar(lg[3][:, :], lg[3][:, :], DEN_EPS, None, ALU.add))
                    ch.link(nc.vector.reciprocal(lg[3][:, :], lg[3][:, :]))
                    dve.sem_inc(s_sc, 1)
                    dve.wait_ge(s_pt, 1)
                    ch.link(nc.vector.tensor_copy(pw[:, :, :], p_w[:, :, :]))
                    base2 = ch.n + base + STEPS * ET
                    STEPS2 = 3

                    def per_head(k, t):
                        return pw[:, k, bass.ds(t * HEADS, HEADS)].unsqueeze(2).broadcast_to([P, HEADS, HD])

                    def heads(ap):
                        return ap.rearrange("p (h c) -> p h c", h=HEADS)

                    with dve.Fori(0, NE) as i:
                        for s in range(2):
                            t = i * 2 + s
                            ch = Chain(dve, s_chain, t * STEPS2 + base2)
                            xs = XS[:, bass.ds(t, 1), :].rearrange("p o c -> p (o c)")
                            xld = XLD[:, bass.ds(t, 1), :].rearrange("p o c -> p (o c)")
                            kb = KB[:, bass.ds(t * P, P)]
                            ch.link(nc.vector.tensor_tensor(heads(xs), heads(xs), per_head(0, t), ALU.mult))
                            dve.wait_ge(s_o, LEAD + t)
                            nc.vector.tensor_scalar(SM[:, s, 0, :], kb, cols[:, 0, bass.ds(t, 1)], None, ALU.is_equal)
                            nc.vector.tensor_scalar(SM[:, s, 1, :], kb, prev[:, bass.ds(t, 1)], e127[:, 0:1],
                                                    ALU.is_equal, ALU.mult).then_inc(s_v, 1)
                            ch.link(nc.vector.tensor_tensor(heads(xld), heads(xld), per_head(1, t), ALU.mult))
                            dve.wait_ge(s_oe, LEAD + t + 1)
                            ch.link(nc.vector.tensor_tensor(xld, xld, OS[:, s, :], ALU.add))
                            nc.vector.tensor_tensor(heads(xld), heads(xld), per_head(2, t), ALU.mult).then_inc(s_res, 1)

                @block.tensor
                def _(pe):
                    with pe.Fori(0, NE) as i:
                        for s in range(2):
                            pe.wait_ge(s_lgc, i * 2 + s + 1)
                            pe.wait_ge(s_lge, LEAD + i)
                            for k in range(2):
                                last = nc.tensor.transpose(p_lg[:, k, s, :], lgc[:, s, k * HEADS:(k + 1) * HEADS],
                                                           ident[:, :])
                            last.then_inc(s_lgt, 1)
                    pe.wait_ge(s_sc, 1)
                    for t in range(ET):
                        for j, k in enumerate((0, 1, 3)):
                            last = nc.tensor.transpose(p_w[:, j, t * HEADS:(t + 1) * HEADS],
                                                       lg[k][:, t * P:(t + 1) * P], ident[0:HEADS, 0:HEADS])
                    last.then_inc(s_pt, 1)
                    with pe.Fori(0, NE) as i:
                        for s in range(2):
                            t = i * 2 + s
                            pe.wait_ge(s_v, t + 1)
                            nc.tensor.matmul(p_o[:, s, 0:HID], SM[:, s, 0, :],
                                             XS[:, bass.ds(t, 1), :].rearrange("p o c -> p (o c)"),
                                             start=True, stop=False)
                            pe.wait_ge(s_oe, LEAD + t)
                            nc.tensor.matmul(p_o[:, s, 0:HID], SM[:, s, 1, :], OS[:, 1 - s, :],
                                             start=False, stop=True).then_inc(s_o, 1)

        with ExitStack() as node_ctx:
            sbn, _, _ = maker(node_ctx)
            mean1 = sbn("mean1", [P, NT])
            r1 = sbn("r1", [P, NT])
            far1 = sbn("far1", [P, NT])
            hT = sbn("hT", [FFN1, NP])
            hmax = sbn("hmax", [P, NB])
            with ExitStack() as ctx:
                mix(nc, maker(ctx), rows, T, x, X1, W_up, ident, mean1, r1, far1)
            with ExitStack() as ctx:
                quant1(nc, maker(ctx), rows, X1, identb, w1q, b1c, scal, mean1, r1, far1, hT, hmax)
            with ExitStack() as ctx:
                conv(nc, maker(ctx), rows, X1, X3, HP, gcnT, gcn_b, w2q, ident, dis, scal, hT, hmax)
        with ExitStack() as ctx:
            edges(nc, maker(ctx), X3, HP, DIS_D, by_src, e127)
        with ExitStack() as ctx:
            gated(nc, maker(ctx), rows, X3, w_gateT, w_upT, w_downT, ident, out)
    return n_sem


def block_stats(nc, ch, xs, st, mv, small, s_var, s_sd, want, dve, x_ready=None):
    for j in range(TPB):
        if x_ready is not None:
            dve.wait_ge(*x_ready(j))
        for h in range(2):
            last = nc.vector.bn_stats(st[:, j, h, :], xs[:, j, h * 512:(h + 1) * 512])
    ch.link(last)
    nc.vector.memset(small[:, 4, :], 0.0)
    for j in range(TPB):
        last = nc.vector.bn_aggr(mv[:, j, :], st[:, j])
    ch.link(last)
    ch.link(nc.vector.tensor_scalar(small[:, 0, :], mv[:, :, 1], LN_EPS, None, ALU.add))
    dve.sem_inc(s_var, 1)
    ch.link(nc.vector.tensor_scalar(small[:, 3, :], mv[:, :, 0], -1.0, None, ALU.mult))
    dve.wait_ge(s_sd, want)
    rsqrt_rest(nc, ch, small[:, 0, :], small[:, 1, :], small[:, 2, :], small[:, 4, :])


STAT_STEPS = 9


def mix(nc, made, rows, T, x, X1, W_up, ident, mean1, r1, far1):
    sb, ps, sem = made
    wu = sb("wu", [P, 2, D])
    g = sb("g", [P, 2, TPB, HID])
    gT = sb("gT", [P, 2, 2, BLK])
    xb = sb("xb_mix", [P, 2, TPB, D])
    x1 = sb("x1_mix", [P, 2, TPB, D])
    gap = sb("gap", [P, 2, D])
    st = sb("st_mix", [P, TPB, 2, 6])
    mv = sb("mv_mix", [P, TPB, 2])
    small = sb("small_mix", [P, 5, TPB])
    p_t = ps("p_t_mix", [P, 2, BLK])
    p_x = ps("p_x_mix", [P, 2, D])
    s_w = sem("mix_weights")
    s_chain = sem("mix_chain")
    s_g = [sem(f"g_loaded{s}") for s in range(2)]
    s_x = [sem(f"mix_x_loaded{s}") for s in range(2)]
    s_g_free = sem("g_used")
    s_x_free = sem("mix_x_used")
    s_t = sem("g_turned")
    s_te = sem("g_copied")
    s_p = sem("update_in_psum")
    s_x1 = sem("x1_ready")
    s_var = sem("mix_var")
    s_sd = sem("mix_sd")
    s_mean = sem("mix_mean")
    s_gap = sem("gap_ready")
    s_far = sem("gap_used")
    s_out = [sem(f"x1_stored{s}") for s in range(2)]
    with nc.Block() as block:
        @block.sync
        def _(sp):
            for s in (s_te, s_far, s_x1, *s_out):
                sp.sem_inc(s, LEAD)
            sp.dma_start(wu[:, :, :], W_up.rearrange("(k p) n -> p k n", p=P)).then_inc(s_w, 16)
            with sp.Fori(0, NB // 2) as i:
                for s in range(2):
                    b = i * 2 + s
                    sp.wait_ge(s_g_free, b + 1)
                    sp.dma_start(g[:, s], rows(T, i, s, HID)).then_inc(s_g[s], 16)
                    sp.wait_ge(s_x_free, b + 1)
                    sp.dma_start(xb[:, s], rows(x, i, s, D)).then_inc(s_x[s], 16)

        @block.tensor
        def _(pe):
            pe.wait_ge(s_w, 16)
            pe.sem_inc(s_g_free, 2)
            with pe.Fori(0, NB // 2) as i:
                for s in range(2):
                    b = i * 2 + s
                    pe.wait_ge(s_g[s], i * 16 + 16)
                    pe.wait_ge(s_te, LEAD + b * 2)
                    for m in range(2):
                        for j in range(TPB):
                            last = nc.tensor.transpose(p_t[:, m, j * P:(j + 1) * P], g[:, s, j, m * P:(m + 1) * P],
                                                       ident[:, :])
                        last.then_inc(s_t, 1)
                    pe.wait_ge(s_te, LEAD + b * 2 + 2)
                    for j in range(TPB):
                        t = b * TPB + j
                        pe.wait_ge(s_x1, LEAD + b * TPB + j - 1) if j > 0 else pe.wait_ge(s_far, LEAD + b)
                        for h in range(2):
                            for m in range(2):
                                last = nc.tensor.matmul(p_x[:, j % 2, h * 512:(h + 1) * 512],
                                                        gT[:, s, m, j * P:(j + 1) * P],
                                                        wu[:, m, h * 512:(h + 1) * 512], start=(m == 0), stop=(m == 1))
                        last.then_inc(s_p, 1)

        @block.scalar
        def _(act):
            with act.Fori(0, NB // 2) as i:
                for s in range(2):
                    b = i * 2 + s
                    for m in range(2):
                        act.wait_ge(s_t, b * 2 + m + 1)
                        nc.scalar.activation(gT[:, s, m, :], p_t[:, m, :], ACT.Copy).then_inc(s_te, 1)
                    act.sem_inc(s_g_free, 1)
                    act.wait_ge(s_x1, LEAD + b * TPB + TPB)
                    act.dma_start(rows(X1, i, s, D), x1[:, s]).then_inc(s_out[s], 16)
                    act.wait_ge(s_var, b + 1)
                    nc.scalar.activation(small[:, 1, :], small[:, 0, :], ACT.Sqrt).then_inc(s_sd, 1)
                    act.wait_ge(s_mean, b + 1)
                    for j in range(TPB):
                        t = b * TPB + j
                        act.wait_ge(s_far, LEAD + t - 1) if j > 1 else (act.wait_ge(s_far, LEAD + b * TPB) if j == 0 else None)
                        nc.scalar.activation(gap[:, j % 2, :], x1[:, s, j, :], ACT.Abs,
                                             bias=small[:, 3, j:j + 1]).then_inc(s_gap, 1)
            for s in range(2):
                act.wait_ge(s_out[s], LEAD + NB // 2 * 16)

        @block.vector
        def _(dve):
            dve.sem_inc(s_x_free, 2)
            STEPS = STAT_STEPS + 2
            with dve.Fori(0, NB // 2) as i:
                for s in range(2):
                    b = i * 2 + s
                    ch = Chain(dve, s_chain, b * STEPS)
                    dve.wait_ge(s_x[s], i * 16 + 16)
                    dve.wait_ge(s_out[s], LEAD + i * 16)
                    for j in range(TPB):
                        dve.wait_ge(s_p, b * TPB + j + 1)
                        nc.vector.tensor_tensor(x1[:, s, j, :], p_x[:, j % 2, :], xb[:, s, j, :],
                                                ALU.add).then_inc(s_x1, 1)
                    dve.wait_ge(s_x1, LEAD + b * TPB + TPB)
                    dve.sem_inc(s_x_free, 1)
                    block_stats(nc, ch, x1[:, s], st, mv, small, s_var, s_sd, b + 1, dve)
                    ch.link(nc.vector.tensor_copy(r1[:, bass.ds(b * TPB, TPB)], small[:, 2, :]))
                    ch.link(nc.vector.tensor_copy(mean1[:, bass.ds(b * TPB, TPB)], small[:, 3, :]))
                    dve.sem_inc(s_mean, 1)
                    for j in range(TPB):
                        dve.wait_ge(s_gap, b * TPB + j + 1)
                        nc.vector.tensor_reduce(far1[:, bass.ds(b * TPB + j, 1)], gap[:, j % 2, :], AX.X,
                                                ALU.max).then_inc(s_far, 1)
                    assert ch.n == STEPS, ch.n


def quant1(nc, made, rows, X1, identb, w1q, b1c, scal, mean1, r1, far1, hT, hmax):
    sb, ps, sem = made
    top = sb("top", [P, 1])
    a = sb("scale1", [P, NT])
    c = sb("shift1", [P, NT])
    xb = sb("xb_q", [P, 2, TPB, D])
    y = sb("y_q", [P, 2, D])
    yq = sb("yq", [P, 2, D], BF16)
    yT = sb("yT_q", [P, 2, KT, BLK], BF16)
    p_t = ps("p_t_q", [P, 2, D], BF16)
    p_h = ps("p_h_q", [P, 2, BLK])
    s_chain = sem("quant_chain")
    s_top = sem("top_ready")
    s_topall = sem("top_all")
    s_sc = sem("quant_scales")
    s_x = [sem(f"q_x1_loaded{s}") for s in range(2)]
    s_x_free = sem("q_x1_used")
    s_y = sem("scaled")
    s_yq = sem("rounded")
    s_t = sem("q_turned")
    s_te = sem("q_copied")
    s_h = sem("h_in_psum")
    s_hg = sem("h_gelu")
    s_hmax = sem("h_max")
    with nc.Block() as block:
        @block.sync
        def _(sp):
            for s in (s_yq, s_te, s_t, s_hg):
                sp.sem_inc(s, LEAD)
            with sp.Fori(0, NB // 2) as i:
                for s in range(2):
                    sp.wait_ge(s_x_free, (i * 2 + s) * TPB + TPB)
                    sp.dma_start(xb[:, s], rows(X1, i, s, D)).then_inc(s_x[s], 16)

        @block.gpsimd
        def _(pool):
            pool.wait_ge(s_top, 1)
            nc.gpsimd.partition_all_reduce(top[:, :], top[:, :], P, RMAX).then_inc(s_topall, 1)

        @block.scalar
        def _(act):
            act.sem_inc(s_x_free, 2 * TPB)
            act.wait_ge(s_sc, 1)
            with act.Fori(0, NB // 2) as i:
                for s in range(2):
                    b = i * 2 + s
                    act.wait_ge(s_x[s], i * 16 + 16)
                    for j in range(TPB):
                        t = b * TPB + j
                        act.wait_ge(s_yq, LEAD + t)
                        nc.scalar.activation(y[:, j % 2, :], xb[:, s, j, :], ACT.Identity,
                                             bias=c[:, bass.ds(t, 1)], scale=a[:, bass.ds(t, 1)]).then_inc(s_y, 1)
                        if j > 0:
                            act.wait_ge(s_t, LEAD + t)
                            nc.scalar.activation(yT[:, s, :, (j - 1) * P:j * P],
                                                 p_t[:, (j - 1) % 2, :].rearrange("p (k n) -> p k n", k=KT),
                                                 ACT.Copy).then_inc(s_te, 1)
                    act.wait_ge(s_t, LEAD + b * TPB + TPB)
                    nc.scalar.activation(yT[:, s, :, 3 * P:4 * P], p_t[:, 1, :].rearrange("p (k n) -> p k n", k=KT),
                                         ACT.Copy).then_inc(s_te, 1)
                    act.wait_ge(s_y, b * TPB + TPB)
                    act.sem_inc(s_x_free, TPB)
                    act.wait_ge(s_h, b + 1)
                    nc.scalar.activation(hT[:, bass.ds(b * BLK, BLK)], p_h[0:FFN1, s, :], ACT.Gelu,
                                         bias=b1c[:, 1:2], scale=scal[0:FFN1, 5:6]).then_inc(s_hg, 1)

        @block.vector
        def _(dve):
            ch = Chain(dve, s_chain)
            ch.link(nc.vector.tensor_tensor(a[:, :], far1[:, :], r1[:, :], ALU.mult))
            nc.vector.tensor_reduce(top[:, :], a[:, :], AX.X, ALU.max).then_inc(s_top, 1)
            dve.wait_ge(s_topall, 1)
            ch.link(nc.vector.tensor_scalar(scal[:, 4:5], top[:, :], MIN_RANGE, 1.0 / QP, ALU.max, ALU.mult))
            ch.link(nc.vector.tensor_tensor(scal[:, 5:6], scal[:, 4:5], scal[:, 0:1], ALU.mult))
            ch.link(nc.vector.reciprocal(scal[:, 6:7], scal[:, 4:5]))
            ch.link(nc.vector.tensor_tensor(b1c[:, 1:2], b1c[:, 0:1], scal[0:FFN1, 5:6], ALU.mult))
            ch.link(nc.vector.tensor_scalar(a[:, :], r1[:, :], scal[:, 6:7], None, ALU.mult))
            ch.link(nc.vector.tensor_tensor(c[:, :], a[:, :], mean1[:, :], ALU.mult))
            ch.link(nc.vector.memset(hmax[:, :], 0.0))
            dve.sem_inc(s_sc, 1)
            base = ch.n
            with dve.Fori(0, NB // 2) as i:
                for s in range(2):
                    b = i * 2 + s
                    for j in range(TPB):
                        t = b * TPB + j
                        ch = Chain(dve, s_chain, t + base)
                        dve.wait_ge(s_y, t + 1)
                        dve.wait_ge(s_t, LEAD + t)
                        ch.link(nc.vector.tensor_scalar(yq[:, j % 2, :], y[:, j % 2, :], MAGIC, -MAGIC, ALU.add, ALU.add))
                        dve.sem_inc(s_yq, 1)
                    dve.wait_ge(s_hg, LEAD + b + 1)
                    nc.vector.tensor_reduce(hmax[0:FFN1, bass.ds(b, 1)], hT[:, bass.ds(b * BLK, BLK)], AX.X, ALU.max,
                                            apply_absolute_value=True).then_inc(s_hmax, 1)
            dve.wait_ge(s_hmax, NB)
            nc.vector.tensor_reduce(hmax[0:FFN1, NB - 1:NB], hT[:, (NB - 1) * BLK:N], AX.X, ALU.max,
                                    apply_absolute_value=True)

        @block.tensor
        def _(pe):
            with pe.Fori(0, NB // 2) as i:
                for s in range(2):
                    b = i * 2 + s
                    for j in range(TPB):
                        t = b * TPB + j
                        pe.wait_ge(s_yq, LEAD + t + 1)
                        pe.wait_ge(s_te, LEAD + t)
                        for k in range(KT):
                            last = nc.tensor.transpose(p_t[:, j % 2, k * P:(k + 1) * P],
                                                       yq[:, j % 2, k * P:(k + 1) * P], identb[:, :])
                        last.then_inc(s_t, 1)
                    pe.wait_ge(s_te, LEAD + b * TPB + TPB)
                    pe.wait_ge(s_hg, LEAD + b)
                    for k in range(KT):
                        last = nc.tensor.matmul(p_h[0:FFN1, s, :], w1q[:, k, :], yT[:, s, k, :], start=(k == 0),
                                                stop=(k == KT - 1))
                    last.then_inc(s_h, 1)


def conv(nc, made, rows, X1, X3, HP, gcnT, gcn_b, w2q, ident, dis, scal, hT, hmax):
    sb, ps, sem = made
    w = sb("w_gcn", [P, KT, D])
    brow = sb("b_gcn", [P, D])
    top = sb("top_c", [P, 1])
    hs = sb("hs", [FFN1, BLK])
    hq = sb("hq", [FFN1 + 3, 2, BLK], BF16)
    ones = sb("ones3", [3, BLK], BF16)
    xb = sb("xb_c", [P, 2, TPB, D])
    ub = sb("ub_c", [P, 2, D])
    y = sb("y_c", [P, 2, D])
    yT = sb("yT_c", [P, 2, D])
    hb = sb("hb_c", [P, 4, D])
    st = sb("st_c", [P, TPB, 2, 6])
    mv = sb("mv_c", [P, TPB, 2])
    small = sb("small_c", [P, 5, TPB])
    p_u = ps("p_u", [P, D])
    p_t = ps("p_t_c", [P, D])
    p_h = ps("p_h_c", [P, 2, D])
    s_w = sem("conv_weights")
    s_ones = sem("conv_ones")
    s_onesin = sem("conv_ones_in")
    s_chain = sem("conv_chain")
    s_top = sem("hmax_ready")
    s_topall = sem("hmax_all")
    s_x = [sem(f"c_x1_loaded{s}") for s in range(2)]
    s_x3 = [sem(f"x3_stored{s}") for s in range(2)]
    s_hp = [sem(f"h_stored{s}") for s in range(4)]
    s_hq = sem("hq_ready")
    s_u = sem("ffn_in_psum")
    s_x2 = sem("x2_ready")
    s_var = sem("c_var")
    s_sd = sem("c_sd")
    s_mean = sem("c_mean")
    s_y = sem("c_normed")
    s_t = sem("c_turned")
    s_te = sem("c_copied")
    s_h = sem("c_h_in_psum")
    s_hb = sem("c_bias_added")
    s_hd = sem("c_h_scaled")
    s_fin = sem("x3_ready")
    with nc.Block() as block:
        @block.sync
        def _(sp):
            for s in (*s_x3, s_x2, s_te, s_hb, s_t, s_h, *s_hp):
                sp.sem_inc(s, LEAD)
            sp.dma_start(w[:, :, :], gcnT.rearrange("(k p) n -> p k n", p=P)).then_inc(s_w, 16)
            sp.dma_start(brow[:, :], gcn_b.partition_broadcast(P)).then_inc(s_w, 16)
            sp.wait_ge(s_ones, 1)
            for s in range(2):
                sp.dma_start(hq[FFN1:FFN1 + 3, s, :], ones[:, :]).then_inc(s_onesin, 16)
            with sp.Fori(0, NB // 2) as i:
                for s in range(2):
                    b = i * 2 + s
                    sp.wait_ge(s_x3[s], LEAD + i * 16)
                    sp.dma_start(xb[:, s], rows(X1, i, s, D)).then_inc(s_x[s], 16)

        @block.gpsimd
        def _(pool):
            nc.gpsimd.memset(ones[:, :], 1.0).then_inc(s_ones, 1)
            pool.wait_ge(s_top, 1)
            nc.gpsimd.partition_all_reduce(top[:, :], top[:, :], P, RMAX).then_inc(s_topall, 1)

        @block.tensor
        def _(pe):
            pe.wait_ge(s_w, 32)
            pe.wait_ge(s_onesin, 32)
            with pe.Fori(0, NB // 2) as i:
                for s in range(2):
                    b = i * 2 + s
                    pe.wait_ge(s_hq, b + 1)
                    for j in range(TPB):
                        pe.wait_ge(s_x2, LEAD + b * TPB + j)
                        for h in range(2):
                            last = nc.tensor.matmul(p_u[:, h * 512:(h + 1) * 512], hq[:, s, j * P:(j + 1) * P],
                                                    w2q[:, h * 512:(h + 1) * 512], start=True, stop=True)
                        last.then_inc(s_u, 1)
                    for j in range(TPB):
                        t = b * TPB + j
                        pe.wait_ge(s_y, t + 1)
                        pe.wait_ge(s_te, LEAD + t)
                        for k in range(KT):
                            last = nc.tensor.transpose(p_t[:, k * P:(k + 1) * P], y[:, j % 2, k * P:(k + 1) * P],
                                                       ident[:, :])
                        last.then_inc(s_t, 1)
                        pe.wait_ge(s_te, LEAD + t + 1)
                        if j == 0:
                            pe.wait_ge(s_hb, LEAD + b * TPB)
                        elif j > 1:
                            pe.wait_ge(s_hb, LEAD + t - 1)
                        for h in range(2):
                            for k in range(KT):
                                last = nc.tensor.matmul(p_h[:, j % 2, h * 512:(h + 1) * 512],
                                                        yT[:, j % 2, k * P:(k + 1) * P],
                                                        w[:, k, h * 512:(h + 1) * 512], start=(k == 0),
                                                        stop=(k == KT - 1))
                        last.then_inc(s_h, 1)

        @block.scalar
        def _(act):
            with act.Fori(0, NB // 2) as i:
                for s in range(2):
                    b = i * 2 + s
                    act.wait_ge(s_var, b + 1)
                    nc.scalar.activation(small[:, 1, :], small[:, 0, :], ACT.Sqrt).then_inc(s_sd, 1)
                    act.wait_ge(s_mean, b + 1)
                    for j in range(TPB):
                        t = b * TPB + j
                        act.wait_ge(s_t, LEAD + t)
                        nc.scalar.activation(y[:, j % 2, :], xb[:, s, j, :], ACT.Identity, bias=small[:, 3, j:j + 1],
                                             scale=small[:, 2, j:j + 1]).then_inc(s_y, 1)
                        act.wait_ge(s_t, LEAD + t + 1)
                        act.wait_ge(s_h, LEAD + t)
                        nc.scalar.activation(yT[:, j % 2, :], p_t[:, :], ACT.Copy).then_inc(s_te, 1)
                        act.wait_ge(s_hb, LEAD + t + 1)
                        nc.scalar.activation(hb[:, j, :], hb[:, j, :], ACT.Copy,
                                             scale=dis[:, bass.ds(t, 1)]).then_inc(s_hd, 1)
                        act.wait_ge(s_hd, t + 1)
                        act.dma_start(HP[bass.ds(t * P, P), :], hb[:, j, :]).then_inc(s_hp[j], 16)
                    act.wait_ge(s_fin, b * TPB + TPB)
                    act.dma_start(rows(X3, i, s, D), xb[:, s]).then_inc(s_x3[s], 16)
            for s in range(2):
                act.wait_ge(s_x3[s], LEAD + NB // 2 * 16)
            for j in range(4):
                act.wait_ge(s_hp[j], LEAD + NB * 16)

        @block.vector
        def _(dve):
            ch = Chain(dve, s_chain)
            nc.vector.tensor_reduce(top[:, :], hmax[:, :], AX.X, ALU.max).then_inc(s_top, 1)
            dve.wait_ge(s_topall, 1)
            ch.link(nc.vector.tensor_scalar(scal[:, 7:8], top[:, :], MIN_RANGE, 1.0 / QP, ALU.max, ALU.mult))
            ch.link(nc.vector.tensor_tensor(scal[:, 8:9], scal[:, 7:8], scal[:, 1:2], ALU.mult))
            ch.link(nc.vector.reciprocal(scal[:, 9:10], scal[:, 7:8]))
            dve.wait_ge(s_w, 32)
            base = ch.n
            STEPS = STAT_STEPS + 3
            with dve.Fori(0, NB // 2) as i:
                for s in range(2):
                    b = i * 2 + s
                    ch = Chain(dve, s_chain, b * STEPS + base)
                    ch.link(nc.vector.tensor_scalar(hs[:, :], hT[:, bass.ds(b * BLK, BLK)], scal[0:FFN1, 9:10], MAGIC,
                                                    ALU.mult, ALU.add))
                    ch.link(nc.vector.tensor_scalar(hq[0:FFN1, s, :], hs[:, :], -MAGIC, None, ALU.add))
                    dve.sem_inc(s_hq, 1)
                    dve.wait_ge(s_x[s], i * 16 + 16)
                    for j in range(TPB):
                        dve.wait_ge(s_u, b * TPB + j + 1)
                        nc.vector.scalar_tensor_tensor(xb[:, s, j, :], p_u[:, :], scal[:, 8:9], xb[:, s, j, :],
                                                       ALU.mult, ALU.add).then_inc(s_x2, 1)
                    dve.wait_ge(s_x2, LEAD + b * TPB + TPB)
                    block_stats(nc, ch, xb[:, s], st, mv, small, s_var, s_sd, b + 1, dve)
                    ch.link(nc.vector.tensor_tensor(small[:, 3, :], small[:, 3, :], small[:, 2, :], ALU.mult))
                    dve.sem_inc(s_mean, 1)
                    for j in range(TPB):
                        t = b * TPB + j
                        dve.wait_ge(s_h, LEAD + t + 1)
                        dve.wait_ge(s_hp[j], LEAD + b * 16)
                        nc.vector.tensor_tensor(hb[:, j, :], p_h[:, j % 2, :], brow[:, :], ALU.add).then_inc(s_hb, 1)
                        dve.wait_ge(s_hd, t + 1)
                        nc.vector.scalar_tensor_tensor(xb[:, s, j, :], hb[:, j, :], dis[:, bass.ds(t, 1)],
                                                       xb[:, s, j, :], ALU.mult, ALU.add).then_inc(s_fin, 1)
                    assert ch.n == STEPS, ch.n


def edges(nc, made, X3, HP, DIS_D, by_src, e127):
    sb, ps, sem = made
    KB = sb("KB_e", [P, EP])
    cols = sb("cols_e", [P, 4, ET])
    prev = sb("prev_e", [P, 1 + ET])
    idx = sb("idx_e", [P, 3, ET], I32)
    de = sb("dis_e", [P, ET])
    H = sb("H_e", [P, 4, D])
    X = sb("X_e", [P, 4, D])
    OS = sb("OS_e", [P, 2, D])
    SM = sb("SM_e", [P, 2, 2, P])
    p_o = ps("p_o_e", [P, 2, D])
    s_in = sem("e_loaded")
    s_chain = sem("e_chain")
    s_idx = sem("e_indices")
    s_de = sem("e_dis")
    s_g = [sem(f"e_rows{t}") for t in range(4)]
    s_sm = sem("e_masks")
    s_o = sem("e_sums")
    s_oe = sem("e_sums_copied")
    s_res = sem("e_rows_ready")
    s_sct = [sem(f"e_scattered{t}") for t in range(4)]
    with nc.Block() as block:
        @block.sync
        def _(sp):
            for s in (s_oe, s_res):
                sp.sem_inc(s, LEAD)
            sp.dma_start(KB[:, :], by_src[0][:, 0].partition_broadcast(P)).then_inc(s_in, 16)
            with nc.allow_non_contiguous_dma(reason="one value of every edge"):
                sp.dma_start(cols[:, 0, :], by_src[0].rearrange("(t p) o -> p (t o)", p=P)).then_inc(s_in, 16)
                sp.dma_start(cols[:, 1, :], by_src[1].rearrange("(t p) o -> p (t o)", p=P)).then_inc(s_in, 16)
                sp.dma_start(cols[:, 2, 0:ET - 1], by_src[0][1:EP - P + 1].rearrange(
                    "(t p) o -> p (t o)", p=P)).then_inc(s_in, 16)
                sp.dma_start(cols[0:P - 1, 2, ET - 1:ET], by_src[0][EP - P + 1:EP]).then_inc(s_in, 16)
                sp.dma_start(cols[P - 1:P, 2, ET - 1:ET], by_src[0][0:1]).then_inc(s_in, 16)

        @block.gpsimd
        def _(pool):
            def scatter(t):
                s = t % 4
                pool.wait_ge(s_res, LEAD + t + 1)
                nc.gpsimd.indirect_dma_start(X3, bass.IndirectOffsetOnAxis(ap=idx[:, 2, t:t + 1], axis=0),
                                             X[:, s, :], None, bounds_check=NP - 1, oob_is_err=False
                                             ).then_inc(s_sct[s], 16)

            pool.wait_ge(s_idx, 1)
            for t in range(ET):
                nc.gpsimd.indirect_dma_start(de[:, t:t + 1], None, DIS_D, bass.IndirectOffsetOnAxis(
                    ap=idx[:, 0, t:t + 1], axis=0)).then_inc(s_de, 16)
            for t in range(ET):
                s = t % 4
                if t >= 4:
                    pool.wait_ge(s_o, t - 3)
                    pool.wait_ge(s_sct[s], t // 4 * 16)
                nc.gpsimd.indirect_dma_start(H[:, s, :], None, HP, bass.IndirectOffsetOnAxis(
                    ap=idx[:, 1, t:t + 1], axis=0)).then_inc(s_g[s], 16)
                nc.gpsimd.indirect_dma_start(X[:, s, :], None, X3, bass.IndirectOffsetOnAxis(
                    ap=idx[:, 0, t:t + 1], axis=0)).then_inc(s_g[s], 16)
                if t >= 2:
                    scatter(t - 2)
            for t in range(ET - 2, ET):
                scatter(t)
            for s in range(4):
                pool.wait_ge(s_sct[s], ET // 4 * 16)

        @block.vector
        def _(dve):
            ch = Chain(dve, s_chain)
            dve.wait_ge(s_in, 16 * 6)
            ch.link(nc.vector.tensor_copy(idx[:, 0, :], cols[:, 0, :]))
            ch.link(nc.vector.tensor_copy(idx[:, 1, :], cols[:, 1, :]))
            ch.link(nc.vector.tensor_tensor(cols[:, 3, :], cols[:, 0, :], cols[:, 2, :], ALU.is_equal))
            ch.link(nc.vector.tensor_scalar(cols[:, 3, :], cols[:, 3, :], SKIP, None, ALU.mult))
            ch.link(nc.vector.tensor_tensor(cols[:, 3, :], cols[:, 3, :], cols[:, 0, :], ALU.add))
            ch.link(nc.vector.tensor_copy(idx[:, 2, :], cols[:, 3, :]))
            ch.link(nc.vector.memset(prev[:, 0:1], -1.0))
            ch.link(nc.vector.tensor_copy(prev[:, 1:1 + ET], cols[:, 0, :]))
            ch.link(nc.vector.memset(OS[:, :, :], 0.0))
            dve.sem_inc(s_idx, 1)
            dve.wait_ge(s_de, 16 * ET)

            def masks(t, s):
                kb = KB[:, bass.ds(t * P, P)]
                nc.vector.tensor_scalar(SM[:, s, 0, :], kb, cols[:, 0, bass.ds(t, 1)], None, ALU.is_equal)
                nc.vector.tensor_scalar(SM[:, s, 1, :], kb, prev[:, bass.ds(t, 1)], e127[:, 0:1],
                                        ALU.is_equal, ALU.mult).then_inc(s_sm, 1)

            with dve.Fori(0, ET // 4) as i:
                for s in range(4):
                    t = i * 4 + s
                    masks(t, s % 2)
                    dve.wait_ge(s_g[s], i * 32 + 32)
                    dve.wait_ge(s_oe, LEAD + t + 1)
                    nc.vector.scalar_tensor_tensor(X[:, s, :], OS[:, s % 2, :], de[:, bass.ds(t, 1)], X[:, s, :],
                                                   ALU.mult, ALU.add).then_inc(s_res, 1)

        @block.scalar
        def _(act):
            with act.Fori(0, ET // 4) as i:
                for s in range(4):
                    t = i * 4 + s
                    act.wait_ge(s_o, t + 1)
                    act.wait_ge(s_res, LEAD + t)
                    nc.scalar.activation(OS[:, s % 2, :], p_o[:, s % 2, :], ACT.Copy).then_inc(s_oe, 1)

        @block.tensor
        def _(pe):
            pe.wait_ge(s_idx, 1)
            with pe.Fori(0, ET // 4) as i:
                for s in range(4):
                    t = i * 4 + s
                    pe.wait_ge(s_sm, t + 1)
                    pe.wait_ge(s_g[s], i * 32 + 32)
                    pe.wait_ge(s_oe, LEAD + t)
                    for h in range(2):
                        c = slice(h * 512, (h + 1) * 512)
                        nc.tensor.matmul(p_o[:, s % 2, c], SM[:, s % 2, 0, :], H[:, s, c], start=True, stop=False)
                        last = nc.tensor.matmul(p_o[:, s % 2, c], SM[:, s % 2, 1, :], OS[:, 1 - s % 2, c],
                                                start=False, stop=True)
                    last.then_inc(s_o, 1)


def gated(nc, made, rows, X3, w_gateT, w_upT, w_downT, ident, out):
    sb, ps, sem = made
    M = UPROW + FFN2
    wi = sb("wi", [P, KT, M], I32)
    wf = sb("wf", [P, KT, M])
    di = sb("di", [FFN2, D], I32)
    wd = sb("wd_g", [FFN2, D])
    xb = sb("xb_g", [P, 3, TPB, D])
    y = sb("y_g", [P, 2, D])
    yT = sb("yT_g", [P, KT, BLK])
    hh = sb("hh_g", [FFN2, 2, BLK])
    st = sb("st_g", [P, TPB, 2, 6])
    mv = sb("mv_g", [P, TPB, 2])
    small = sb("small_g", [P, 5, TPB])
    p_t = ps("p_t_g", [P, D])
    p_g = ps("p_g", [P, 2, BLK])
    p_o = ps("p_o_g", [P, 2, D])
    s_w = sem("gated_weights")
    s_wz = sem("gated_zeros")
    s_wf = sem("gated_weights_ready")
    s_chain = sem("gated_chain")
    s_x = [sem(f"g_x3_loaded{s}") for s in range(2)]
    s_out = [sem(f"out_stored{s}") for s in range(2)]
    s_var = sem("g_var")
    s_sd = sem("g_sd")
    s_mean = sem("g_mean")
    s_y = sem("g_normed")
    s_t = sem("g_y_turned")
    s_te = sem("g_y_copied")
    s_gu = sem("gate_up_in_psum")
    s_si = sem("silu_ready")
    s_hh = sem("hidden_ready")
    s_o = sem("g_out_in_psum")
    s_fin = sem("g_out_ready")
    with nc.Block() as block:
        @block.sync
        def _(sp):
            for s in (*s_out, s_te, s_hh, s_fin, s_t, s_gu):
                sp.sem_inc(s, LEAD)
            sp.wait_ge(s_wz, 1)
            sp.dma_start(wi[:, :, 0:FFN2], w_gateT.rearrange("(k p) h -> p k h", p=P)).then_inc(s_w, 16)
            sp.dma_start(wi[:, :, UPROW:M], w_upT.rearrange("(k p) h -> p k h", p=P)).then_inc(s_w, 16)
            sp.dma_start(di[:, :], w_downT).then_inc(s_w, 16)
            with sp.Fori(0, NB // 2) as i:
                for s in range(2):
                    sp.wait_ge(s_out[s], LEAD + i * 16)
                    sp.dma_start(xb[:, s], rows(X3, i, s, D)).then_inc(s_x[s], 16)

        @block.gpsimd
        def _(pool):
            nc.gpsimd.memset(wi[:, :, :], 0).then_inc(s_wz, 1)

        @block.tensor
        def _(pe):
            pe.wait_ge(s_wf, 1)
            with pe.Fori(0, NB // 2) as i:
                for s in range(2):
                    b = i * 2 + s
                    for j in range(TPB):
                        t = b * TPB + j
                        pe.wait_ge(s_y, t + 1)
                        pe.wait_ge(s_te, LEAD + t)
                        for k in range(KT):
                            last = nc.tensor.transpose(p_t[:, k * P:(k + 1) * P], y[:, j % 2, k * P:(k + 1) * P],
                                                       ident[:, :])
                        last.then_inc(s_t, 1)
                    pe.wait_ge(s_te, LEAD + b * TPB + TPB)
                    pe.wait_ge(s_hh, LEAD + b)
                    for k in range(KT):
                        last = nc.tensor.matmul(p_g[0:M, s, :], wf[:, k, :], yT[:, k, :], start=(k == 0),
                                                stop=(k == KT - 1))
                    last.then_inc(s_gu, 1)
                    pe.wait_ge(s_hh, LEAD + b + 1)
                    for j in range(TPB):
                        t = b * TPB + j
                        if j == 0:
                            pe.wait_ge(s_fin, LEAD + b * TPB)
                        elif j > 1:
                            pe.wait_ge(s_fin, LEAD + t - 1)
                        for h in range(2):
                            last = nc.tensor.matmul(p_o[:, j % 2, h * 512:(h + 1) * 512], hh[:, s, j * P:(j + 1) * P],
                                                    wd[:, h * 512:(h + 1) * 512], start=True, stop=True)
                        last.then_inc(s_o, 1)

        @block.scalar
        def _(act):
            with act.Fori(0, NB // 2) as i:
                for s in range(2):
                    b = i * 2 + s
                    act.wait_ge(s_var, b + 1)
                    nc.scalar.activation(small[:, 1, :], small[:, 0, :], ACT.Sqrt).then_inc(s_sd, 1)
                    act.wait_ge(s_mean, b + 1)
                    act.wait_ge(s_gu, LEAD + b)
                    for j in range(TPB):
                        t = b * TPB + j
                        act.wait_ge(s_t, LEAD + t)
                        nc.scalar.activation(y[:, j % 2, :], xb[:, s, j, :], ACT.Identity, bias=small[:, 3, j:j + 1],
                                             scale=small[:, 2, j:j + 1]).then_inc(s_y, 1)
                        act.wait_ge(s_t, LEAD + t + 1)
                        nc.scalar.activation(yT[:, :, j * P:(j + 1) * P], p_t[:, :].rearrange("p (k n) -> p k n", k=KT),
                                             ACT.Copy).then_inc(s_te, 1)
                    act.wait_ge(s_gu, LEAD + b + 1)
                    nc.scalar.activation(hh[:, s, :], p_g[0:FFN2, s, :], ACT.Silu).then_inc(s_si, 1)
                    act.wait_ge(s_fin, LEAD + b * TPB + TPB)
                    act.dma_start(rows(out, i, s, D), xb[:, s]).then_inc(s_out[s], 16)
            for s in range(2):
                act.wait_ge(s_out[s], LEAD + NB // 2 * 16)

        @block.vector
        def _(dve):
            ch = Chain(dve, s_chain)
            dve.wait_ge(s_w, 48)
            ch.link(nc.vector.tensor_copy(wf[:, :, :], wi[:, :, :]))
            ch.link(nc.vector.tensor_copy(wd[:, :], di[:, :]))
            ch.link(nc.vector.tensor_scalar(wf[:, :, :], wf[:, :, :], 1.0 / QP, None, ALU.mult))
            ch.link(nc.vector.tensor_scalar(wd[:, :], wd[:, :], 1.0 / QP, None, ALU.mult))
            dve.sem_inc(s_wf, 1)
            base = ch.n
            STEPS = STAT_STEPS + 1
            with dve.Fori(0, NB // 2) as i:
                for s in range(2):
                    b = i * 2 + s
                    ch = Chain(dve, s_chain, b * STEPS + base)
                    dve.wait_ge(s_x[s], i * 16 + 16)
                    block_stats(nc, ch, xb[:, s], st, mv, small, s_var, s_sd, b + 1, dve)
                    ch.link(nc.vector.tensor_tensor(small[:, 3, :], small[:, 3, :], small[:, 2, :], ALU.mult))
                    dve.sem_inc(s_mean, 1)
                    dve.wait_ge(s_si, b + 1)
                    nc.vector.tensor_tensor(hh[:, s, :], hh[:, s, :], p_g[UPROW:M, s, :], ALU.mult).then_inc(s_hh, 1)
                    for j in range(TPB):
                        t = b * TPB + j
                        dve.wait_ge(s_o, t + 1)
                        nc.vector.tensor_tensor(xb[:, s, j, :], xb[:, s, j, :], p_o[:, j % 2, :],
                                                ALU.add).then_inc(s_fin, 1)
                    assert ch.n == STEPS, ch.n


def kernel(x, src, dst, L0_gnn_rms_w, L0_gnn_W_down, L0_gnn_Wl, L0_gnn_Wr, L0_gnn_att, L0_gnn_W_up, L0_ffn_w1,
           L0_ffn_b1, L0_ffn_w2, L0_ffn_b2, L1_gnn_W, L1_gnn_b, L1_ffn_w_gate, L1_ffn_w_up, L1_ffn_w_down):
    import numpy as np
    import concourse.bacc as bacc
    from concourse import mybir as mb
    from concourse.bass_utils import run_bass_kernel_spmd

    def lay(a):
        return np.ascontiguousarray(np.asarray(a))

    xp = np.zeros((NP, D), np.float32)
    xp[:N] = np.asarray(x)
    ends = []
    for e in (src, dst):
        p = np.full((EP,), NP - 1, np.int32)
        p[:E] = np.asarray(e)
        ends.append(p)
    arrays = {
        "x": xp, "xT": lay(xp.T),
        "src_row": ends[0], "dst_row": ends[1],
        "src_col": lay(ends[0].reshape(ET, P).T), "dst_col": lay(ends[1].reshape(ET, P).T),
        "rms_w": lay(np.asarray(L0_gnn_rms_w).reshape(KT, P).T),
        "W_down": lay(L0_gnn_W_down), "Wl": lay(L0_gnn_Wl), "Wr": lay(L0_gnn_Wr),
        "att": lay(L0_gnn_att).reshape(HID), "W_up": lay(L0_gnn_W_up),
        "w1T": lay(np.asarray(L0_ffn_w1).T), "b1": lay(L0_ffn_b1).reshape(FFN1, 1),
        "w2T": lay(np.asarray(L0_ffn_w2).T), "b2": lay(L0_ffn_b2).reshape(1, D),
        "gcnT": lay(np.asarray(L1_gnn_W).T), "gcn_b": lay(L1_gnn_b).reshape(D),
        "w_gateT": lay(np.asarray(L1_ffn_w_gate).T), "w_upT": lay(np.asarray(L1_ffn_w_up).T),
        "w_downT": lay(np.asarray(L1_ffn_w_down).T),
        "ident_in": np.eye(P, dtype=np.float32),
    }
    nc = bacc.Bacc("TRN2", target_bir_lowering=False, num_devices=1)
    feeds, args = {}, {}
    for name, a in arrays.items():
        feeds[f"in_{name}"] = a
        args[name] = nc.dram_tensor(f"in_{name}", a.shape, mb.dt.from_np(a.dtype), kind="ExternalInput").ap()
    args["out"] = nc.dram_tensor("out_rows", [NP, D], mb.dt.float32, kind="ExternalOutput").ap()
    build(nc, **args)
    r = run_bass_kernel_spmd(nc, [feeds], core_ids=[0])
    return r.results[0]["out_rows"][:N]
```

```python
from contextlib import ExitStack

import concourse.bass as bass
from concourse import mybir

FP32 = mybir.dt.float32
BF16 = mybir.dt.bfloat16
FP16 = mybir.dt.float16
I32 = mybir.dt.int32
ALU = mybir.AluOpType
ACT = mybir.ActivationFunctionType
AX = mybir.AxisListType
RMAX = bass.bass_isa.ReduceOp.absmax

P = 128
N, D, E = 10000, 1024, 5000
HID, HEADS, FFN1, FFN2 = 256, 4, 64, 48
HD = HID // HEADS
KT = D // P
TPB = 4
BLK = TPB * P
NB = -(-N // BLK)
NP = NB * BLK
NT = NP // P
ET = -(-E // P)
EP = ET * P
UPROW = 64
LN_EPS, RMS_EPS, DEN_EPS = 1e-5, 1e-6, 1e-16
SLOPE, QP, MIN_RANGE = 0.2, 127.0, 1e-6
MAGIC = 1.5 * 2.0 ** 23
SKIP = float(2 ** 20)
FAR = -1.0e30
YSCALE, WMAX = 2.0 ** 10, 2.0 ** 12
LEAD = 16


class Chain:

    def __init__(self, eng, sem, base=0):
        self.eng, self.sem, self.base, self.n = eng, sem, base, 0

    def link(self, ins):
        self.n += 1
        ins.then_inc(self.sem, 1)
        self.eng.wait_ge(self.sem, self.base + self.n)


def rsqrt_rest(nc, ch, var, sd, r, tmp):
    ch.link(nc.vector.reciprocal(r, sd))
    ch.link(nc.vector.tensor_tensor(tmp, r, r, ALU.mult))
    ch.link(nc.vector.tensor_tensor(tmp, tmp, var, ALU.mult))
    ch.link(nc.vector.tensor_scalar(tmp, tmp, -0.5, 1.5, ALU.mult, ALU.add))
    ch.link(nc.vector.tensor_tensor(r, r, tmp, ALU.mult))


def build(nc, x, xT, src_row, dst_row, src_col, dst_col, rms_w, W_down, Wl, Wr, att, W_up,
          w1T, b1, w2T, b2, gcnT, gcn_b, w_gateT, w_upT, w_downT, ident_in, out):
    T = nc.dram_tensor("node_rows", [NP, 2 * HID], FP32).ap()
    X1 = nc.dram_tensor("x1_rows", [NP, D], FP32).ap()
    X3 = nc.dram_tensor("x3_rows", [NP, D], FP32).ap()
    HP = nc.dram_tensor("h_rows", [NP, D], FP32).ap()
    DIS_D = nc.dram_tensor("dis_rows", [NP, 1], FP32).ap()
    by_src = nc.dram_tensor("by_src", [EP, 2], FP32).ap()
    sorted_key = [nc.dram_tensor(f"sorted_{n}", [EP, 1], FP32).ap() for n in ("src", "dst")]
    by_dst = nc.dram_tensor("by_dst", [EP, 2], FP32).ap()
    T_half = T.rearrange("n (h c) -> (n h) c", h=2)

    keep = ExitStack()
    used = []

    def maker(ctx):
        def sb(name, shape, dt=FP32):
            return ctx.enter_context(nc.sbuf_tensor(name, shape, dt))

        def ps(name, shape, dt=FP32):
            return ctx.enter_context(nc.psum_tensor(name, shape, dt))

        def sem(name):
            used.append(ctx.enter_context(nc.semaphore(name)))
            return used[-1]
        return sb, ps, sem

    def clear_used():
        with nc.Block() as block:
            @block.sync
            def _(sp):
                numbers = sorted(s.num for s in used)
                assert numbers == list(range(numbers[0], numbers[-1] + 1))
                sp.sem_clear(range(numbers[0], numbers[-1] + 1))
        used.clear()

    def rows(ap, i, b, width):
        return ap[bass.ds(i * (2 * BLK) + b * BLK, BLK), 0:width].rearrange("(j p) d -> p j d", p=P)

    with keep:
        sbk, _, _ = maker(keep)
        s_scat, s_sct, s_de, *more = [keep.enter_context(nc.semaphore(n)) for n in (
            "scattered", "rows_scattered", "e_dis", "edge_rows0", "edge_rows1", *(f"e_rows{t}" for t in range(4)),
            *(f"e_scattered{t}" for t in range(4)))]
        s_gat, s_ge, s_sce = more[0:2], more[2:6], more[6:10]
        ident = sbk("ident", [P, P])
        identb = sbk("identb", [P, P], BF16)
        dis = sbk("dis", [P, NT])
        e127 = sbk("e127", [P, 1])
        scal = sbk("scal", [P, 16])
        w1q = sbk("w1q", [P, KT, FFN1], BF16)
        w2q = sbk("w2q", [FFN1 + 3, D], BF16)
        b1c = sbk("b1c", [FFN1, 2])

        with ExitStack() as ctx:
            sb, ps, sem = maker(ctx)
            SORT_FIRST, SORT_PER, HOT_PER = 4, 3, 5
            SORT_BLOCKS = (ET - SORT_FIRST) // SORT_PER
            assert SORT_BLOCKS % 2 == 0 and HOT_PER * (NB - SORT_BLOCKS) == ET
            scratch = sb("scratch", [P, EP], I32)
            junk = scratch[:, 0:EP // 2].bitcast(BF16)
            junk_act = scratch[:, EP // 2:EP].bitcast(BF16)
            key = [sb(f"key{k}", [P, EP]) for k in range(2)]
            col_int = [sb(f"col_int{k}", [P, ET], I32) for k in range(2)]
            col = sb("col", [P, ET, 2])
            pair = sb("pair", [P, ET, 2])
            colq = [sb(f"colq{k}", [P, ET]) for k in range(2)]
            junk_diag = sb("junk_diag", [P, P], BF16)
            count = [sb(f"count{k}", [P, ET]) for k in range(2)]
            ties = [sb(f"ties{k}", [P, ET]) for k in range(2)]
            pos = [sb(f"pos{k}", [P, ET], I32) for k in range(2)]
            tri = sb("tri", [P, P])
            iota = sb("iota", [P, P])
            hi_int = sb("hi_int", [P, ET], I32)
            lo_int = sb("lo_int", [P, ET], I32)
            hi = sb("hi", [P, ET])
            lo = sb("lo", [P, ET])
            one_lo = sb("one_lo", [P, HOT_PER, P], BF16)
            one_hi = sb("one_hi", [P, HOT_PER, NT], BF16)
            zero = sb("zero", [P, P], BF16)
            deg = sb("deg", [P, 3, NT])
            w1 = sb("w1", [P, KT, FFN1])
            w2 = sb("w2", [FFN1, D])
            b2r = sb("b2r", [1, 2, D])
            b2p = sb("b2p", [1, 3, D], BF16)
            wmax = sb("wmax", [P, 2])
            wd = sb("wd", [P, KT, HID])
            wlr = sb("wlr", [P, 2, 2 * HID])
            rms = sb("rms", [P, KT])
            mean_of = sb("mean_of", [P, P])
            xt = sb("xt", [P, 2, KT, BLK])
            xb = sb("xb", [P, 2, TPB, D])
            xdT = sb("xdT", [P, 2, 2, BLK])
            lr = sb("lr", [P, 2, TPB, 2 * HID])
            st = sb("st", [P, TPB, 2, 6])
            mv = sb("mv", [P, TPB, 2])
            small = sb("small", [P, 2, 4, TPB])
            hist = ps("hist", [P, NT])
            p_xd = ps("p_xd", [P, 2, 2, BLK])
            p_lr = ps("p_lr", [P, 2, 2 * HID])

            loaded = [sem(f"keys_loaded{k}") for k in range(2)]
            s_conv = sem("src_keys_converted")
            s_w = sem("small_weights")
            s_pw = sem("project_weights")
            s_const = sem("constants")
            s_chain = sem("project_chain")
            s_key = sem("keys_ready")
            s_sign = sem("dst_counted")
            s_shift = sem("dst_shifted")
            s_hot = sem("onehots_ready")
            s_hist = sem("hist_step")
            s_pos = sem("ranks_ready")
            s_deg = sem("degree_ready")
            s_dsd = sem("degree_sqrt")
            s_wmax = sem("weight_max")
            s_wall = sem("weight_max_all")
            s_b2 = sem("b2_parts")
            s_b2in = sem("b2_in")
            s_dis = sem("dis_ready")
            s_end = sem("sort_stores")
            s_wf = sem("wd_folded")
            s_mean = sem("wd_mean")
            s_wc = sem("wd_centred")
            s_xt = [sem(f"xT_loaded{s}") for s in range(2)]
            s_xb = [sem(f"x_loaded{s}") for s in range(2)]
            s_xt_free = sem("xT_used")
            s_xb_free = sem("x_used")
            s_xd = sem("xd_in_psum")
            s_xde = sem("xd_copied")
            s_lr = sem("lr_in_psum")
            s_lre = sem("lr_copied")
            s_var = sem("var_ready")
            s_sd = sem("sd_ready")
            s_r = sem("scale_ready")
            s_lrfree = [sem(f"lr_stored{s}") for s in range(2)]
            leads = (s_xt_free, s_shift, s_hist, s_xde, s_lre, s_lr, s_xd, *s_lrfree)

            def run(eng, part):
                with eng.Fori(0, SORT_BLOCKS // 2) as i:
                    for s in range(2):
                        part(i, s, SORT_PER, 0, True)
                with eng.Fori(SORT_BLOCKS // 2, NB // 2 - 1) as i:
                    for s in range(2):
                        part(i, s, 0, HOT_PER, True)
                for s in range(2):
                    part(NB // 2 - 1, s, 0, HOT_PER, s == 0)

            with nc.Block() as block:
                @block.sync
                def _(sp):
                    for s in leads:
                        sp.sem_inc(s, LEAD)
                    sp.dma_start(wd[:, :, :], W_down.rearrange("(k p) h -> p k h", p=P)).then_inc(s_pw, 16)
                    sp.dma_start(rms[:, :], rms_w).then_inc(s_pw, 16)
                    sp.dma_start(xt[:, 0], xT[:, 0:BLK].rearrange("(k p) n -> p k n", p=P)).then_inc(s_xt[0], 16)
                    for k, w in enumerate((Wl, Wr)):
                        sp.dma_start(wlr[:, :, k * HID:(k + 1) * HID],
                                     w.rearrange("(k p) h -> p k h", p=P)).then_inc(s_pw, 16)
                    for k, (r, c) in enumerate(((src_row, src_col), (dst_row, dst_col))):
                        if k:
                            sp.wait_ge(s_conv, 1)
                        sp.dma_start(scratch[:, :], r.partition_broadcast(P)).then_inc(loaded[k], 16)
                        sp.dma_start(col_int[k][:, :], c).then_inc(loaded[k], 16)
                    for dst, s in ((ident[:, :], ident_in), (w2[:, :], w2T), (b2r[:, 0, :], b2), (b1c[:, 0:1], b1)):
                        sp.dma_start(dst, s).then_inc(s_w, 16)
                    sp.dma_start(w1[:, :, :], w1T.rearrange("(k p) h -> p k h", p=P)).then_inc(s_w, 16)

                    def part(i, s, sorts, hots, more):
                        b = i * 2 + s
                        if more:
                            sp.wait_ge(s_xt_free, LEAD + b)
                            sp.dma_start(xt[:, 1 - s], xT[:, bass.ds((b + 1) * BLK, BLK)].rearrange(
                                "(k p) n -> p k n", p=P)).then_inc(s_xt[1 - s], 16)
                        sp.wait_ge(s_xb_free, b + 1)
                        sp.dma_start(xb[:, s], rows(x, i, s, D)).then_inc(s_xb[s], 16)
                    run(sp, part)
                    sp.wait_ge(s_b2, 1)
                    for k in range(3):
                        sp.dma_start(w2q[FFN1 + k:FFN1 + k + 1, :], b2p[:, k, :]).then_inc(s_b2in, 16)
                    sp.wait_ge(s_dis, 1)
                    with nc.allow_non_contiguous_dma(reason="one value of every node or edge"):
                        sp.dma_start(DIS_D.rearrange("(t p) o -> p (t o)", p=P), dis[:, :]).then_inc(s_end, 16)
                        sp.wait_ge(s_scat, 16 * 2 * ET)
                        for k, table in enumerate((by_src, by_dst)):
                            sp.dma_start(sorted_key[k], table[:, 0:1]).then_inc(s_end, 16)
                    sp.wait_ge(s_b2in, 48)
                    sp.wait_ge(s_end, 48)

                @block.gpsimd
                def _(pool):
                    nc.gpsimd.memset(tri[:, :], 1.0).then_inc(s_const, 1)
                    nc.gpsimd.memset(e127[:, :], 0.0).then_inc(s_const, 1)
                    nc.gpsimd.iota(iota[:, :], [[1, P]], base=0, channel_multiplier=0,
                                   allow_small_or_imprecise_dtypes=True).then_inc(s_const, 1)
                    nc.gpsimd.memset(zero[:, :], 0.0).then_inc(s_const, 1)
                    nc.gpsimd.memset(wmax[:, :], 0.0).then_inc(s_const, 1)
                    pool.wait_ge(s_const, 5)
                    nc.gpsimd.affine_select(tri[:, :], tri[:, :], [[-1, P]], ALU.is_gt, 0.0, base=0,
                                            channel_multiplier=1).then_inc(s_const, 1)
                    nc.gpsimd.affine_select(e127[:, :], e127[:, :], [[0, 1]], ALU.not_equal, 1.0, base=-(P - 1),
                                            channel_multiplier=1).then_inc(s_const, 1)
                    pool.wait_ge(s_wmax, 1)
                    nc.gpsimd.partition_all_reduce(wmax[:, :], wmax[:, :], P, RMAX).then_inc(s_wall, 1)
                    pool.wait_ge(s_pos, 1)
                    for k, (table, rec) in enumerate(((by_src, col), (by_dst, pair))):
                        for t in range(ET):
                            nc.gpsimd.indirect_dma_start(
                                table, bass.IndirectOffsetOnAxis(ap=pos[k][:, t:t + 1], axis=0),
                                rec[:, t, :], None).then_inc(s_scat, 16)
                    pool.wait_ge(s_scat, 16 * 2 * ET)

                @block.tensor
                def _(pe):
                    def down(b, s, count):
                        pe.wait_ge(s_xt[s], count)
                        pe.wait_ge(s_xde, LEAD + b * 2 - 2)
                        for m in range(2):
                            for k in range(KT):
                                last = nc.tensor.matmul(p_xd[:, s, m, :], wd[:, k, m * P:(m + 1) * P],
                                                        xt[:, s, k, :], start=(k == 0), stop=(k == KT - 1))
                            last.then_inc(s_xd, 1)

                    pe.wait_ge(s_wf, 1)
                    for k in range(KT):
                        last = nc.tensor.matmul(p_lr[:, 0, 0:HID], mean_of[:, :], wd[:, k, :], start=(k == 0),
                                                stop=(k == KT - 1))
                    last.then_inc(s_mean, 1)
                    pe.wait_ge(s_const, 7)
                    nc.tensor.matmul(hist[:, :], zero[:, :], zero[:, 0:NT], start=True, stop=False)
                    pe.wait_ge(s_wc, 1)
                    down(0, 0, 16)

                    def part(i, s, sorts, hots, more):
                        b = i * 2 + s
                        if more:
                            down(b + 1, 1 - s, (i + s) * 16 + 16)
                        pe.wait_ge(s_xde, LEAD + b * 2 + 2)
                        for j in range(TPB):
                            pe.wait_ge(s_lre, LEAD + b * TPB + j - 1)
                            for m in range(2):
                                last = nc.tensor.matmul(p_lr[:, j % 2, :], xdT[:, s, m, j * P:(j + 1) * P],
                                                        wlr[:, m, :], start=(m == 0), stop=(m == 1))
                            last.then_inc(s_lr, 1)
                        for u in range(hots):
                            pe.wait_ge(s_hot, (b - SORT_BLOCKS) * HOT_PER + u + 1)
                            nc.tensor.matmul(hist[:, :], one_lo[:, u, :], one_hi[:, u, :], start=False,
                                             stop=False).then_inc(s_hist, 1)
                    run(pe, part)
                    nc.tensor.matmul(hist[:, :], zero[:, :], zero[:, 0:NT], start=False, stop=True).then_inc(s_hist, 1)

                @block.scalar
                def _(act):
                    def sign(t):
                        act.wait_ge(s_shift, LEAD + t)
                        nc.scalar.activation(junk_act, key[1][:, :], ACT.Sign, bias=col[:, bass.ds(t, 1), 1:2].rearrange(
                            "p a b -> p (a b)"), scale=-1.0, accum_out=count[1][:, bass.ds(t, 1)]).then_inc(s_sign, 1)

                    def copy_xd(b, s):
                        for m in range(2):
                            act.wait_ge(s_xd, LEAD + b * 2 + m + 1)
                            act.wait_ge(s_lr, LEAD + b * TPB - TPB)
                            nc.scalar.activation(xdT[:, s, m, :], p_xd[:, s, m, :], ACT.Copy).then_inc(s_xde, 1)
                        act.sem_inc(s_xt_free, 1)

                    act.wait_ge(s_key, 1)
                    for t in range(SORT_FIRST):
                        sign(t)
                    copy_xd(0, 0)

                    def part(i, s, sorts, hots, more):
                        b = i * 2 + s
                        if sorts:
                            sign(b * SORT_PER + SORT_FIRST)
                        act.wait_ge(s_var, b + 1)
                        nc.scalar.activation(small[:, s, 1, :], small[:, s, 0, :], ACT.Sqrt).then_inc(s_sd, 1)
                        if sorts:
                            sign(b * SORT_PER + SORT_FIRST + 1)
                        if more:
                            copy_xd(b + 1, 1 - s)
                        act.wait_ge(s_r, b + 1)
                        act.wait_ge(s_lrfree[s], LEAD + i * 16)
                        for j in range(TPB):
                            act.wait_ge(s_lr, LEAD + b * TPB + j + 1)
                            nc.scalar.activation(lr[:, s, j, :], p_lr[:, j % 2, :], ACT.Copy,
                                                 scale=small[:, s, 2, j:j + 1]).then_inc(s_lre, 1)
                            if sorts and j == 1:
                                sign(b * SORT_PER + SORT_FIRST + 2)
                        act.wait_ge(s_lre, LEAD + b * TPB + TPB)
                        act.dma_start(rows(T, i, s, 2 * HID), lr[:, s]).then_inc(s_lrfree[s], 16)
                    run(act, part)
                    act.wait_ge(s_deg, 1)
                    nc.scalar.activation(deg[:, 1, :], deg[:, 0, :], ACT.Sqrt).then_inc(s_dsd, 1)
                    for s in range(2):
                        act.wait_ge(s_lrfree[s], LEAD + NB // 2 * 16)

                @block.vector
                def _(dve):
                    ch = Chain(dve, s_chain)
                    nc.vector.memset(mean_of[:, :], 1.0 / D)
                    dve.wait_ge(s_pw, 64)
                    for k in range(KT):
                        last = nc.vector.tensor_scalar(wd[:, k, :], wd[:, k, :], rms[:, k:k + 1], None, ALU.mult)
                    ch.link(last)
                    dve.sem_inc(s_wf, 1)
                    dve.wait_ge(loaded[0], 32)
                    ch.link(nc.vector.tensor_scalar(key[0][:, :], scratch[:, :], 0.25, None, ALU.add))
                    dve.sem_inc(s_conv, 1)
                    dve.wait_ge(s_mean, 1)
                    for k in range(KT):
                        last = nc.vector.tensor_tensor(wd[:, k, :], wd[:, k, :], p_lr[:, 0, 0:HID], ALU.subtract)
                    ch.link(last)
                    dve.sem_inc(s_wc, 1)
                    dve.wait_ge(loaded[1], 32)
                    ch.link(nc.vector.tensor_scalar(key[1][:, :], scratch[:, :], 0.25, None, ALU.add))
                    for k in range(2):
                        ch.link(nc.vector.tensor_copy(col[:, :, k], col_int[k][:, :]))
                        ch.link(nc.vector.tensor_copy(pair[:, :, 1 - k], col_int[k][:, :]))
                        ch.link(nc.vector.tensor_scalar(colq[k][:, :], col_int[k][:, :], 0.25, None, ALU.add))
                    dve.wait_ge(s_const, 7)
                    dve.sem_inc(s_key, 1)
                    ch.link(nc.vector.tensor_scalar(lo_int[:, :], col_int[0][:, :], P - 1, None, ALU.bitwise_and))
                    ch.link(nc.vector.tensor_scalar(hi_int[:, :], col_int[0][:, :], 7, None, ALU.arith_shift_right))
                    ch.link(nc.vector.tensor_copy(lo[:, :], lo_int[:, :]))
                    ch.link(nc.vector.tensor_copy(hi[:, :], hi_int[:, :]))
                    dve.sem_inc(s_xb_free, 2)
                    dve.wait_ge(s_w, 16 * 5)
                    ch.link(nc.vector.tensor_reduce(wmax[:, 0:1], w1[:, :, :], AX.XY, ALU.max, apply_absolute_value=True))
                    nc.vector.tensor_reduce(wmax[0:FFN1, 1:2], w2[:, :], AX.X, ALU.max,
                                            apply_absolute_value=True).then_inc(s_wmax, 1)
                    SORT_STEPS = 5
                    STEPS = 8
                    base = ch.n

                    def rank(t, ch):
                        c1 = bass.ds(t, 1)
                        here = bass.ds(t * P, P)
                        n = ch.n
                        ch.link(nc.vector.tensor_scalar(junk, key[0][:, :], col[:, c1, 0:1].rearrange(
                            "p a b -> p (a b)"), None, ALU.is_lt, ALU.add, accum_out=count[0][:, c1]))
                        for k in range(2):
                            ch.link(nc.vector.scalar_tensor_tensor(
                                junk_diag[:, :], key[k][:, here], colq[k][:, c1], tri[:, :], ALU.is_equal,
                                ALU.mult, accum_out=ties[k][:, c1]))
                        ch.link(nc.vector.tensor_scalar(key[0][:, here], key[0][:, here], -0.5, None, ALU.add))
                        dve.wait_ge(s_sign, t + 1)
                        ch.link(nc.vector.tensor_scalar(key[1][:, here], key[1][:, here], -0.5, None, ALU.add))
                        dve.sem_inc(s_shift, 1)
                        assert ch.n == n + SORT_STEPS

                    for t in range(SORT_FIRST):
                        rank(t, ch)
                    base += SORT_FIRST * SORT_STEPS
                    per_sort = STEPS + SORT_PER * SORT_STEPS

                    def finish_ranks(ch):
                        ch.link(nc.vector.tensor_scalar(count[1][:, :], count[1][:, :], float(EP), 0.5, ALU.add,
                                                        ALU.mult))
                        for k in range(2):
                            ch.link(nc.vector.tensor_tensor(ties[k][:, :], ties[k][:, :], count[k][:, :], ALU.add))
                            ch.link(nc.vector.tensor_copy(pos[k][:, :], ties[k][:, :]))
                        dve.sem_inc(s_pos, 1)
                        ch.link(nc.vector.tensor_copy(identb[:, :], ident[:, :]))
                        dve.wait_ge(s_wall, 1)
                        ch.link(nc.vector.tensor_scalar(scal[:, 0:2], wmax[:, :], MIN_RANGE, 1.0 / QP, ALU.max, ALU.mult))
                        ch.link(nc.vector.reciprocal(scal[:, 2:4], scal[:, 0:2]))
                        ch.link(nc.vector.tensor_scalar(w1[:, :, :], w1[:, :, :], scal[:, 2:3], MAGIC, ALU.mult, ALU.add))
                        ch.link(nc.vector.tensor_scalar(w1q[:, :, :], w1[:, :, :], -MAGIC, None, ALU.add))
                        ch.link(nc.vector.tensor_scalar(w2[:, :], w2[:, :], scal[0:FFN1, 3:4], MAGIC, ALU.mult, ALU.add))
                        ch.link(nc.vector.tensor_scalar(w2q[0:FFN1, :], w2[:, :], -MAGIC, None, ALU.add))
                        for k in range(3):
                            ch.link(nc.vector.tensor_copy(b2p[:, k, :], b2r[:, k % 2, :]))
                            if k < 2:
                                ch.link(nc.vector.tensor_tensor(b2r[:, (k + 1) % 2, :], b2r[:, k % 2, :],
                                                                b2p[:, k, :], ALU.subtract))
                        dve.sem_inc(s_b2, 1)

                    FINISH = 5 + 7 + 5
                    after = base + SORT_BLOCKS * per_sort + FINISH

                    def part(i, s, sorts, hots, more):
                        b = i * 2 + s
                        if sorts:
                            ch = Chain(dve, s_chain, b * per_sort + base)
                        else:
                            ch = Chain(dve, s_chain, (b - SORT_BLOCKS) * STEPS + after)
                        dve.wait_ge(s_xb[s], i * 16 + 16)
                        for j in range(TPB):
                            for h in range(2):
                                last = nc.vector.bn_stats(st[:, j, h, :], xb[:, s, j, h * 512:(h + 1) * 512])
                        ch.link(last)
                        dve.sem_inc(s_xb_free, 1)
                        dve.wait_ge(s_lre, LEAD + b * TPB - TPB)
                        nc.vector.memset(small[:, s, 3, :], 0.0)
                        for j in range(TPB):
                            last = nc.vector.bn_aggr(mv[:, j, :], st[:, j])
                        ch.link(last)
                        ch.link(nc.vector.tensor_scalar(small[:, s, 0, :], mv[:, :, 1], 1.0 + RMS_EPS,
                                                        LN_EPS * RMS_EPS, ALU.mult, ALU.add))
                        dve.sem_inc(s_var, 1)
                        if sorts:
                            rank(b * SORT_PER + SORT_FIRST, ch)
                        dve.wait_ge(s_sd, b + 1)
                        rsqrt_rest(nc, ch, small[:, s, 0, :], small[:, s, 1, :], small[:, s, 2, :],
                                   small[:, s, 3, :])
                        dve.sem_inc(s_r, 1)
                        for u in range(1, sorts):
                            rank(b * SORT_PER + SORT_FIRST + u, ch)
                        if hots:
                            dve.wait_ge(s_hist, LEAD + (b - SORT_BLOCKS) * HOT_PER)
                            for u in range(hots):
                                c1 = bass.ds((b - SORT_BLOCKS) * HOT_PER + u, 1)
                                nc.vector.tensor_scalar(one_lo[:, u, :], iota[:, :], lo[:, c1], None, ALU.is_equal)
                                nc.vector.tensor_scalar(one_hi[:, u, :], iota[:, 0:NT], hi[:, c1], None,
                                                        ALU.is_equal).then_inc(s_hot, 1)
                        assert ch.n == (per_sort if sorts else STEPS), ch.n

                    with dve.Fori(0, SORT_BLOCKS // 2) as i:
                        for s in range(2):
                            part(i, s, SORT_PER, 0, True)
                    ch = Chain(dve, s_chain, base + SORT_BLOCKS * per_sort)
                    finish_ranks(ch)
                    assert ch.n == FINISH, ch.n
                    with dve.Fori(SORT_BLOCKS // 2, NB // 2) as i:
                        for s in range(2):
                            part(i, s, 0, HOT_PER, True)
                    ch = Chain(dve, s_chain, after + (NB - SORT_BLOCKS) * STEPS)
                    dve.wait_ge(s_hist, LEAD + ET + 1)
                    nc.vector.tensor_scalar(deg[:, 0, :], hist[:, :], 1.0, None, ALU.add).then_inc(s_deg, 1)
                    dve.wait_ge(s_dsd, 1)
                    rsqrt_rest(nc, ch, deg[:, 0, :], deg[:, 1, :], dis[:, :], deg[:, 2, :])
                    dve.sem_inc(s_dis, 1)

        with ExitStack() as ctx:
            sb, ps, sem = maker(ctx)
            XS = sb("XS", [P, ET, HID])
            XLD = sb("XLD", [P, ET, HID])
            KB = sb("KB", [P, EP])
            a_row = sb("a_row", [P, HID])
            lg = [sb(f"lg{k}", [HEADS, EP]) for k in range(4)]
            step = sb("step", [HEADS, EP + 1], BF16)
            cols = sb("cols", [P, 4, ET])
            prev = sb("prev", [P, 1 + ET])
            idx = sb("idx", [P, 4, ET], I32)
            msg = sb("msg", [P, 2, 2 * HID])
            lgc = sb("lgc", [P, 2, 2 * HEADS])
            pw = sb("pw", [P, 3, ET * HEADS])
            SM = sb("SM", [P, 2, 2, P])
            OS = sb("OS", [P, 2, HID])
            p_lg = ps("p_lg", [HEADS, 2, 4, P])
            p_w = ps("p_w", [P, 3, ET * HEADS])
            p_o = ps("p_o", [P, 2, 512])
            s_in = sem("edges_loaded")
            s_chain = sem("attend_chain")
            s_idx = sem("attend_indices")
            s_g = s_gat
            s_lgc = sem("logits_ready")
            s_lgt = sem("logits_turned")
            s_lge = sem("logits_copied")
            s_dif = sem("shifted_logits")
            s_exp = sem("exps_ready")
            s_sc = sem("scans_ready")
            s_pt = sem("weights_turned")
            s_v = sem("weighted_rows")
            s_o = sem("sums_in_psum")
            s_oe = sem("sums_copied")
            s_res = sem("rows_ready")
            NE = ET // 2
            with nc.Block() as block:
                @block.sync
                def _(sp):
                    for s in (s_lgt, s_lge, s_oe, s_res, s_o):
                        sp.sem_inc(s, LEAD)
                    sp.dma_start(KB[:, :], sorted_key[1][:, 0].partition_broadcast(P)).then_inc(s_in, 16)
                    with nc.allow_non_contiguous_dma(reason="one value of every edge"):
                        sp.dma_start(cols[:, 0, :], sorted_key[1].rearrange("(t p) o -> p (t o)", p=P)).then_inc(s_in, 16)
                        sp.dma_start(cols[:, 1, :], by_dst.rearrange("(t p) o -> p t o", p=P)[:, :, 1]).then_inc(s_in, 16)
                        sp.dma_start(cols[:, 2, 0:ET - 1], sorted_key[1][1:EP - P + 1].rearrange(
                            "(t p) o -> p (t o)", p=P)).then_inc(s_in, 16)
                        sp.dma_start(cols[0:P - 1, 2, ET - 1:ET], sorted_key[1][EP - P + 1:EP]).then_inc(s_in, 16)
                        sp.dma_start(cols[P - 1:P, 2, ET - 1:ET], sorted_key[1][0:1]).then_inc(s_in, 16)
                    sp.dma_start(a_row[:, :], att.partition_broadcast(P)).then_inc(s_in, 16)

                @block.gpsimd
                def _(pool):
                    pool.wait_ge(s_idx, 1)
                    for t in range(ET):
                        s = t % 2
                        if t >= 2:
                            pool.wait_ge(s_lgc, t - 1)
                        nc.gpsimd.indirect_dma_start(XS[:, t, :], None, T_half, bass.IndirectOffsetOnAxis(
                            ap=idx[:, 1, t:t + 1], axis=0)).then_inc(s_g[s], 16)
                        nc.gpsimd.indirect_dma_start(XLD[:, t, :], None, T_half, bass.IndirectOffsetOnAxis(
                            ap=idx[:, 0, t:t + 1], axis=0)).then_inc(s_g[s], 16)
                        nc.gpsimd.indirect_dma_start(msg[:, s, HID:2 * HID], None, T_half, bass.IndirectOffsetOnAxis(
                            ap=idx[:, 2, t:t + 1], axis=0)).then_inc(s_g[s], 16)
                    for t in range(ET):
                        pool.wait_ge(s_res, LEAD + t + 1)
                        nc.gpsimd.indirect_dma_start(
                            T_half, bass.IndirectOffsetOnAxis(ap=idx[:, 3, t:t + 1], axis=0),
                            XLD[:, t, :], None, bounds_check=2 * NP - 1, oob_is_err=False).then_inc(s_sct, 16)
                    pool.wait_ge(s_sct, 16 * ET)

                @block.scalar
                def _(act):
                    for k in range(2):
                        act.wait_ge(s_dif, k + 1)
                        nc.scalar.activation(lg[k][:, :], lg[k][:, :], ACT.Exp).then_inc(s_exp, 1)
                    with act.Fori(0, NE) as i:
                        for s in range(2):
                            act.wait_ge(s_o, LEAD + i * 2 + s + 1)
                            act.wait_ge(s_res, LEAD + i * 2 + s)
                            nc.scalar.activation(OS[:, s, :], p_o[:, s, 0:HID], ACT.Copy).then_inc(s_oe, 1)

                @block.vector
                def _(dve):
                    ch = Chain(dve, s_chain)
                    dve.wait_ge(s_in, 16 * 7)
                    ch.link(nc.vector.tensor_scalar(idx[:, 0, :], cols[:, 0, :], 2.0, None, ALU.mult))
                    ch.link(nc.vector.tensor_scalar(idx[:, 1, :], cols[:, 1, :], 2.0, None, ALU.mult))
                    ch.link(nc.vector.tensor_scalar(idx[:, 2, :], cols[:, 0, :], 2.0, 1.0, ALU.mult, ALU.add))
                    dve.sem_inc(s_idx, 1)
                    ch.link(nc.vector.memset(prev[:, 0:1], -1.0))
                    ch.link(nc.vector.tensor_copy(prev[:, 1:1 + ET], cols[:, 0, :]))
                    ch.link(nc.vector.memset(OS[:, :, :], 0.0))
                    ch.link(nc.vector.tensor_tensor(cols[:, 3, :], cols[:, 0, :], cols[:, 2, :], ALU.is_equal))
                    ch.link(nc.vector.tensor_scalar(cols[:, 3, :], cols[:, 3, :], SKIP, None, ALU.mult))
                    ch.link(nc.vector.tensor_tensor(cols[:, 3, :], cols[:, 3, :], cols[:, 0, :], ALU.add))
                    ch.link(nc.vector.tensor_scalar(idx[:, 3, :], cols[:, 3, :], 2.0, None, ALU.mult))
                    ch.link(nc.vector.memset(step[:, :], 0.0))
                    ch.link(nc.vector.tensor_tensor(step[:, 1:EP], KB[0:HEADS, 1:EP], KB[0:HEADS, 0:EP - 1],
                                                    ALU.is_equal))
                    ch.link(nc.vector.tensor_scalar(step[:, :], step[:, :], -FAR, FAR, ALU.mult, ALU.add))
                    base = ch.n
                    STEPS = 4
                    with dve.Fori(0, NE) as i:
                        for s in range(2):
                            t = i * 2 + s
                            ch = Chain(dve, s_chain, t * STEPS + base)
                            dve.wait_ge(s_g[s], i * 48 + 48)
                            ch.link(nc.vector.tensor_tensor(
                                msg[:, s, 0:HID], XS[:, bass.ds(t, 1), :].rearrange("p o c -> p (o c)"),
                                msg[:, s, HID:2 * HID], ALU.add))
                            ch.link(nc.vector.tensor_tensor(
                                msg[:, s, HID:2 * HID], XLD[:, bass.ds(t, 1), :].rearrange("p o c -> p (o c)"),
                                msg[:, s, HID:2 * HID], ALU.add))
                            ch.link(nc.vector.scalar_tensor_tensor(msg[:, s, :], msg[:, s, :], SLOPE, msg[:, s, :],
                                                                   ALU.mult, ALU.max))
                            ch.link(nc.vector.tensor_tensor(
                                msg[:, s, :].rearrange("p (a c) -> p a c", a=2),
                                msg[:, s, :].rearrange("p (a c) -> p a c", a=2),
                                a_row[:, None, :].broadcast_to([P, 2, HID]), ALU.mult))
                            dve.wait_ge(s_lgt, LEAD + t)
                            nc.vector.tensor_reduce(lgc[:, s, :], msg[:, s, :].rearrange("p (a c) -> p a c", c=HD),
                                                    AX.X, ALU.add).then_inc(s_lgc, 1)
                            if s == 1:
                                dve.wait_ge(s_lgt, LEAD + t + 1)
                                for k in range(2):
                                    last = nc.vector.tensor_copy(
                                        lg[k][:, bass.ds(i * 2 * P, 2 * P)],
                                        p_lg[:, k, 0:2, :].rearrange("h a e -> h (a e)"))
                                last.then_inc(s_lge, 1)
                    ch = Chain(dve, s_chain, base + STEPS * ET)
                    dve.wait_ge(s_lge, LEAD + NE)
                    ch.link(nc.vector.tensor_tensor_scan(lg[2][:, :], step[:, 0:EP], lg[0][:, :], FAR, ALU.add, ALU.max))
                    ch.link(nc.vector.tensor_tensor_scan(lg[3][:, ::-1], step[:, 1:EP + 1][:, ::-1], lg[0][:, ::-1],
                                                         FAR, ALU.add, ALU.max))
                    ch.link(nc.vector.tensor_tensor(lg[2][:, :], lg[2][:, :], lg[3][:, :], ALU.max))
                    ch.link(nc.vector.tensor_tensor(lg[2][:, :], lg[2][:, :], lg[1][:, :], ALU.max))
                    for k in range(2):
                        nc.vector.tensor_tensor(lg[k][:, :], lg[k][:, :], lg[2][:, :],
                                                ALU.subtract).then_inc(s_dif, 1)
                    ch.link(nc.vector.tensor_scalar(step[:, :], step[:, :], 0.0, None, ALU.is_ge))
                    dve.wait_ge(s_exp, 2)
                    ch.link(nc.vector.tensor_tensor_scan(lg[3][:, :], step[:, 0:EP], lg[0][:, :], 0.0, ALU.mult, ALU.add))
                    ch.link(nc.vector.tensor_tensor(lg[3][:, :], lg[3][:, :], lg[1][:, :], ALU.add))
                    ch.link(nc.vector.tensor_scalar(lg[3][:, :], lg[3][:, :], DEN_EPS, None, ALU.add))
                    ch.link(nc.vector.reciprocal(lg[3][:, :], lg[3][:, :]))
                    dve.sem_inc(s_sc, 1)
                    dve.wait_ge(s_pt, 1)
                    ch.link(nc.vector.tensor_copy(pw[:, :, :], p_w[:, :, :]))
                    base2 = ch.n + base + STEPS * ET
                    STEPS2 = 3

                    def per_head(k, t):
                        return pw[:, k, bass.ds(t * HEADS, HEADS)].unsqueeze(2).broadcast_to([P, HEADS, HD])

                    def heads(ap):
                        return ap.rearrange("p (h c) -> p h c", h=HEADS)

                    with dve.Fori(0, NE) as i:
                        for s in range(2):
                            t = i * 2 + s
                            ch = Chain(dve, s_chain, t * STEPS2 + base2)
                            xs = XS[:, bass.ds(t, 1), :].rearrange("p o c -> p (o c)")
                            xld = XLD[:, bass.ds(t, 1), :].rearrange("p o c -> p (o c)")
                            kb = KB[:, bass.ds(t * P, P)]
                            ch.link(nc.vector.tensor_tensor(heads(xs), heads(xs), per_head(0, t), ALU.mult))
                            dve.wait_ge(s_o, LEAD + t)
                            nc.vector.tensor_scalar(SM[:, s, 0, :], kb, cols[:, 0, bass.ds(t, 1)], None, ALU.is_equal)
                            nc.vector.tensor_scalar(SM[:, s, 1, :], kb, prev[:, bass.ds(t, 1)], e127[:, 0:1],
                                                    ALU.is_equal, ALU.mult).then_inc(s_v, 1)
                            ch.link(nc.vector.tensor_tensor(heads(xld), heads(xld), per_head(1, t), ALU.mult))
                            dve.wait_ge(s_oe, LEAD + t + 1)
                            ch.link(nc.vector.tensor_tensor(xld, xld, OS[:, s, :], ALU.add))
                            nc.vector.tensor_tensor(heads(xld), heads(xld), per_head(2, t), ALU.mult).then_inc(s_res, 1)

                @block.tensor
                def _(pe):
                    with pe.Fori(0, NE) as i:
                        for s in range(2):
                            pe.wait_ge(s_lgc, i * 2 + s + 1)
                            pe.wait_ge(s_lge, LEAD + i)
                            for k in range(2):
                                last = nc.tensor.transpose(p_lg[:, k, s, :], lgc[:, s, k * HEADS:(k + 1) * HEADS],
                                                           ident[:, :])
                            last.then_inc(s_lgt, 1)
                    pe.wait_ge(s_sc, 1)
                    for t in range(ET):
                        for j, k in enumerate((0, 1, 3)):
                            last = nc.tensor.transpose(p_w[:, j, t * HEADS:(t + 1) * HEADS],
                                                       lg[k][:, t * P:(t + 1) * P], ident[0:HEADS, 0:HEADS])
                    last.then_inc(s_pt, 1)
                    with pe.Fori(0, NE) as i:
                        for s in range(2):
                            t = i * 2 + s
                            pe.wait_ge(s_v, t + 1)
                            nc.tensor.matmul(p_o[:, s, 0:HID], SM[:, s, 0, :],
                                             XS[:, bass.ds(t, 1), :].rearrange("p o c -> p (o c)"),
                                             start=True, stop=False)
                            pe.wait_ge(s_oe, LEAD + t)
                            nc.tensor.matmul(p_o[:, s, 0:HID], SM[:, s, 1, :], OS[:, 1 - s, :],
                                             start=False, stop=True).then_inc(s_o, 1)

        clear_used()

        with ExitStack() as node_ctx:
            sbn, _, _ = maker(node_ctx)
            mean1 = sbn("mean1", [P, NT])
            r1 = sbn("r1", [P, NT])
            far1 = sbn("far1", [P, 2, NT])
            hT = sbn("hT", [FFN1, NP])
            hmax = sbn("hmax", [P, NB])
            whi = sbn("whi", [P, KT, D], FP16)
            wlo = sbn("wlo", [P, KT, D], FP16)
            gscale = sbn("gscale", [P, 2])
            with ExitStack() as ctx:
                mix(nc, maker(ctx), T, x, X1, W_up, gcnT, whi, wlo, gscale, ident, mean1, r1, far1)
            with ExitStack() as ctx:
                quant1(nc, maker(ctx), X1, identb, w1q, b1c, scal, mean1, r1, far1, hT, hmax)
            with ExitStack() as ctx:
                conv(nc, maker(ctx), rows, X1, X3, HP, gcn_b, whi, wlo, gscale, w2q, ident, dis, scal, hT, hmax)
        with ExitStack() as ctx:
            edges(nc, maker(ctx), s_de, s_ge, s_sce, X3, HP, DIS_D, by_src, sorted_key[0], e127)
        with ExitStack() as ctx:
            gated(nc, maker(ctx), X3, w_gateT, w_upT, w_downT, ident, out)


def block_stats(nc, ch, xs, st, mv, small, s_var, s_sd, want, dve, x_ready=None):
    for j in range(TPB):
        if x_ready is not None:
            dve.wait_ge(*x_ready(j))
        for h in range(2):
            last = nc.vector.bn_stats(st[:, j, h, :], xs[:, j, h * 512:(h + 1) * 512])
    ch.link(last)
    nc.vector.memset(small[:, 4, :], 0.0)
    for j in range(TPB):
        last = nc.vector.bn_aggr(mv[:, j, :], st[:, j])
    ch.link(last)
    ch.link(nc.vector.tensor_scalar(small[:, 0, :], mv[:, :, 1], LN_EPS, None, ALU.add))
    dve.sem_inc(s_var, 1)
    ch.link(nc.vector.tensor_scalar(small[:, 3, :], mv[:, :, 0], -1.0, None, ALU.mult))
    dve.wait_ge(s_sd, want)
    rsqrt_rest(nc, ch, small[:, 0, :], small[:, 1, :], small[:, 2, :], small[:, 4, :])


STAT_STEPS = 9


def run_blocks(eng, part, slots):
    with eng.Fori(0, NB // slots - 1) as i:
        for s in range(slots):
            part(i * slots + s, s, slots)
    for s in range(slots):
        part(NB - slots + s, s, slots - 1 - s)


def block_rows(ap, b, width):
    return ap[bass.ds(b * BLK, BLK), 0:width].rearrange("(j p) d -> p j d", p=P)


def mix(nc, made, T, x, X1, W_up, gcnT, whi, wlo, gscale, ident, mean1, r1, far1):
    sb, ps, sem = made
    wu = sb("wu", [P, 2, D])
    wst = sb("wst", [P, KT, D])
    wtop = sb("wtop", [P, 1])
    g = sb("g", [P, 2, TPB, HID])
    gT = sb("gT", [P, 2, 2, BLK])
    xb = sb("xb_mix", [P, 2, TPB, D])
    x1 = sb("x1_mix", [P, 2, TPB, D])
    st = sb("st_mix", [P, TPB, 2, 6])
    mv = sb("mv_mix", [P, TPB, 2])
    small = sb("small_mix", [P, 4, TPB])
    most = sb("most_mix", [P, TPB])
    carry = sb("carry_mix", [P, TPB])
    p_t = ps("p_t_mix", [P, 2, BLK])
    p_x = ps("p_x_mix", [P, 2, D])
    s_w = sem("mix_weights")
    s_gw = sem("gcn_weights")
    s_gtop = sem("gcn_top")
    s_gall = sem("gcn_top_all")
    s_gsc = sem("gcn_scale")
    s_pool = sem("gcn_split")
    s_chain = sem("mix_chain")
    s_g = [sem(f"g_loaded{s}") for s in range(2)]
    s_x = [sem(f"mix_x_loaded{s}") for s in range(2)]
    s_x_free = sem("mix_x_used")
    s_t = sem("g_turned")
    s_te = sem("g_copied")
    s_p = sem("update_in_psum")
    s_x1 = sem("x1_ready")
    s_var = sem("mix_var")
    s_sd = sem("mix_sd")
    s_out = [sem(f"x1_stored{s}") for s in range(2)]
    leads = (s_te, s_x1, s_t, s_p, *s_out)
    with nc.Block() as block:
        @block.sync
        def _(sp):
            for s in leads:
                sp.sem_inc(s, LEAD)
            sp.dma_start(g[:, 0], block_rows(T, 0, HID)).then_inc(s_g[0], 16)
            sp.dma_start(wu[:, :, :], W_up.rearrange("(k p) n -> p k n", p=P)).then_inc(s_w, 16)

            def part(b, s, left):
                if left:
                    sp.wait_ge(s_t, LEAD + b * 2)
                    sp.dma_start(g[:, 1 - s], block_rows(T, b + 1, HID)).then_inc(s_g[1 - s], 16)
                sp.wait_ge(s_x_free, b + 1)
                sp.dma_start(xb[:, s], block_rows(x, b, D)).then_inc(s_x[s], 16)

            run_blocks(sp, part, 2)

        @block.gpsimd
        def _(pool):
            pool.dma_start(wst[:, :, :], gcnT.rearrange("(k p) n -> p k n", p=P)).then_inc(s_gw, 16)
            pool.wait_ge(s_gtop, 1)
            nc.gpsimd.partition_all_reduce(wtop[:, :], wtop[:, :], P, RMAX).then_inc(s_gall, 1)
            pool.wait_ge(s_gsc, 1)
            for k in range(KT):
                nc.gpsimd.tensor_scalar(wst[:, k, :], wst[:, k, :], gscale[:, 0:1], 1.0, ALU.mult,
                                        ALU.mult).then_inc(s_pool, 1)
                pool.wait_ge(s_pool, 3 * k + 1)
                nc.gpsimd.tensor_copy(whi[:, k, :], wst[:, k, :]).then_inc(s_pool, 1)
                pool.wait_ge(s_pool, 3 * k + 2)
                nc.gpsimd.tensor_tensor(wlo[:, k, :], wst[:, k, :], whi[:, k, :], ALU.subtract).then_inc(s_pool, 1)
            pool.wait_ge(s_pool, 3 * KT)

        @block.tensor
        def _(pe):
            def turn(b, s, loads):
                pe.wait_ge(s_g[s], loads)
                pe.wait_ge(s_te, LEAD + b * 2)
                for m in range(2):
                    for j in range(TPB):
                        last = nc.tensor.transpose(p_t[:, m, j * P:(j + 1) * P], g[:, s, j, m * P:(m + 1) * P],
                                                   ident[:, :])
                    last.then_inc(s_t, 1)

            turn(0, 0, 16)
            pe.wait_ge(s_w, 16)

            def part(b, s, left):
                if left:
                    turn(b + 1, 1 - s, (b + s) * 8 + 16)
                pe.wait_ge(s_te, LEAD + b * 2 + 2)
                for j in range(TPB):
                    pe.wait_ge(s_x1, LEAD + b * TPB + j - 1)
                    for h in range(2):
                        for m in range(2):
                            last = nc.tensor.matmul(p_x[:, j % 2, h * 512:(h + 1) * 512],
                                                    gT[:, s, m, j * P:(j + 1) * P],
                                                    wu[:, m, h * 512:(h + 1) * 512], start=(m == 0), stop=(m == 1))
                    last.then_inc(s_p, 1)
            run_blocks(pe, part, 2)

        @block.scalar
        def _(act):
            def copy(b, s):
                for m in range(2):
                    act.wait_ge(s_t, LEAD + b * 2 + m + 1)
                    act.wait_ge(s_p, LEAD + b * TPB - TPB)
                    nc.scalar.activation(gT[:, s, m, :], p_t[:, m, :], ACT.Copy).then_inc(s_te, 1)

            copy(0, 0)

            def part(b, s, left):
                if left:
                    copy(b + 1, 1 - s)
                act.wait_ge(s_var, b + 1)
                nc.scalar.activation(small[:, 1, :], small[:, 0, :], ACT.Sqrt).then_inc(s_sd, 1)
                act.wait_ge(s_x1, LEAD + b * TPB + TPB)
                act.dma_start(block_rows(X1, b, D), x1[:, s]).then_inc(s_out[s], 16)
            run_blocks(act, part, 2)
            for s in range(2):
                act.wait_ge(s_out[s], LEAD + NB // 2 * 16)

        @block.vector
        def _(dve):
            dve.sem_inc(s_x_free, 2)
            STEPS = STAT_STEPS + 3
            OFFSET = 3

            def part(b, s, left):
                ch = Chain(dve, s_chain, b * STEPS + OFFSET)
                dve.wait_ge(s_x[s], (b - s) * 8 + 16)
                dve.wait_ge(s_out[s], LEAD + (b - s) * 8)
                for j in range(TPB):
                    dve.wait_ge(s_p, LEAD + b * TPB + j + 1)
                    nc.vector.memset(carry[:, j:j + 1], 0.0)
                    nc.vector.tensor_tensor_reduce(out=x1[:, s, j, :], in0=p_x[:, j % 2, :], in1=xb[:, s, j, :],
                                                   scale=1.0, scalar=FAR, op0=ALU.add, op1=ALU.max,
                                                   accum_out=most[:, j:j + 1]).then_inc(s_x1, 1)
                    dve.wait_ge(s_x1, LEAD + b * TPB + j + 1)
                    for h in range(2):
                        last = nc.vector.bn_stats(st[:, j, h, :], x1[:, s, j, h * 512:(h + 1) * 512])
                dve.sem_inc(s_x_free, 1)
                ch.link(last)
                nc.vector.memset(small[:, 3, :], 0.0)
                for j in range(TPB):
                    last = nc.vector.bn_aggr(mv[:, j, :], st[:, j])
                ch.link(last)
                ch.link(nc.vector.tensor_scalar(small[:, 0, :], mv[:, :, 1], LN_EPS, None, ALU.add))
                dve.sem_inc(s_var, 1)
                ch.link(nc.vector.tensor_scalar(mean1[:, bass.ds(b * TPB, TPB)], mv[:, :, 0], -1.0, None, ALU.mult))
                ch.link(nc.vector.tensor_reduce(far1[:, 1, bass.ds(b * TPB, TPB)], x1[:, s], AX.X, ALU.min))
                dve.wait_ge(s_sd, b + 1)
                rsqrt_rest(nc, ch, small[:, 0, :], small[:, 1, :], small[:, 2, :], small[:, 3, :])
                ch.link(nc.vector.tensor_copy(r1[:, bass.ds(b * TPB, TPB)], small[:, 2, :]))
                ch.link(nc.vector.tensor_copy(far1[:, 0, bass.ds(b * TPB, TPB)], most[:, :]))
                assert ch.n == STEPS, ch.n

            ch = Chain(dve, s_chain)
            dve.wait_ge(s_gw, 16)
            nc.vector.tensor_reduce(wtop[:, :], wst[:, :, :], AX.XY, ALU.max,
                                    apply_absolute_value=True).then_inc(s_gtop, 1)
            dve.wait_ge(s_gall, 1)
            ch.link(nc.vector.tensor_scalar(wtop[:, :], wtop[:, :], 1e-30, 1.0 / WMAX, ALU.max, ALU.mult))
            ch.link(nc.vector.reciprocal(gscale[:, 0:1], wtop[:, :]))
            ch.link(nc.vector.tensor_scalar(gscale[:, 1:2], wtop[:, :], 1.0 / YSCALE, None, ALU.mult))
            dve.sem_inc(s_gsc, 1)
            assert ch.n == OFFSET
            run_blocks(dve, part, 2)


def quant1(nc, made, X1, identb, w1q, b1c, scal, mean1, r1, far1, hT, hmax):
    sb, ps, sem = made
    SLOTS = 4
    top = sb("top", [P, 1])
    a = sb("scale1", [P, NT])
    c = sb("shift1", [P, NT])
    xb = sb("xb_q", [P, SLOTS, TPB, D])
    y = sb("y_q", [P, 2, D])
    yq = sb("yq", [P, 2, D], BF16)
    yT = sb("yT_q", [P, 2, KT, BLK], BF16)
    p_t = ps("p_t_q", [P, 2, D], BF16)
    p_h = ps("p_h_q", [P, 2, BLK])
    s_chain = sem("quant_chain")
    s_top = sem("top_ready")
    s_topall = sem("top_all")
    s_x = [sem(f"q_x1_loaded{s}") for s in range(SLOTS)]
    s_x_free = sem("q_x1_used")
    s_y = sem("scaled")
    s_yq = sem("rounded")
    s_t = sem("q_turned")
    s_te = sem("q_copied")
    s_h = sem("h_in_psum")
    s_hg = sem("h_gelu")
    s_hmax = sem("h_max")
    leads = (s_yq, s_te, s_t, s_hg, s_h, s_x_free)
    with nc.Block() as block:
        @block.sync
        def _(sp):
            for s in leads:
                sp.sem_inc(s, LEAD)
            for s in range(SLOTS - 1):
                sp.dma_start(xb[:, s], block_rows(X1, s, D)).then_inc(s_x[s], 16)

            def part(b, s, left):
                if left >= SLOTS - 1:
                    n = (s - 1) % SLOTS
                    sp.wait_ge(s_x_free, LEAD + b)
                    sp.dma_start(xb[:, n], block_rows(X1, b + SLOTS - 1, D)).then_inc(s_x[n], 16)
            run_blocks(sp, part, SLOTS)

        @block.gpsimd
        def _(pool):
            pool.wait_ge(s_top, 1)
            nc.gpsimd.partition_all_reduce(top[:, :], top[:, :], P, RMAX).then_inc(s_topall, 1)

        @block.tensor
        def _(pe):
            def turn(b, j):
                t = b * TPB + j
                pe.wait_ge(s_yq, LEAD + t + 1)
                pe.wait_ge(s_te, LEAD + t - 1)
                for k in range(KT):
                    last = nc.tensor.transpose(p_t[:, j % 2, k * P:(k + 1) * P], yq[:, j % 2, k * P:(k + 1) * P],
                                               identb[:, :])
                last.then_inc(s_t, 1)

            for j in range(TPB):
                turn(0, j)

            def part(b, s, left):
                if left:
                    for j in range(TPB):
                        turn(b + 1, j)
                pe.wait_ge(s_te, LEAD + b * TPB + TPB)
                pe.wait_ge(s_hg, LEAD + b - 1)
                for k in range(KT):
                    last = nc.tensor.matmul(p_h[0:FFN1, s % 2, :], w1q[:, k, :], yT[:, s % 2, k, :], start=(k == 0),
                                            stop=(k == KT - 1))
                last.then_inc(s_h, 1)
            run_blocks(pe, part, SLOTS)

        @block.scalar
        def _(act):
            def copy(b, u):
                act.wait_ge(s_h, LEAD + b - 1)
                for j in range(TPB):
                    act.wait_ge(s_t, LEAD + b * TPB + j + 1)
                    nc.scalar.activation(yT[:, u, :, j * P:(j + 1) * P],
                                         p_t[:, j % 2, :].rearrange("p (k n) -> p k n", k=KT),
                                         ACT.Copy).then_inc(s_te, 1)

            copy(0, 0)

            def part(b, s, left):
                if left:
                    copy(b + 1, (s + 1) % 2)
                act.wait_ge(s_h, LEAD + b + 1)
                nc.scalar.activation(hT[:, bass.ds(b * BLK, BLK)], p_h[0:FFN1, s % 2, :], ACT.Gelu,
                                     bias=b1c[:, 1:2], scale=scal[0:FFN1, 5:6]).then_inc(s_hg, 1)
            run_blocks(act, part, SLOTS)

        @block.vector
        def _(dve):
            ch = Chain(dve, s_chain)
            ch.link(nc.vector.tensor_tensor(a[:, :], far1[:, 0, :], mean1[:, :], ALU.add))
            ch.link(nc.vector.tensor_tensor(c[:, :], far1[:, 1, :], mean1[:, :], ALU.add))
            ch.link(nc.vector.tensor_scalar(c[:, :], c[:, :], -1.0, None, ALU.mult))
            ch.link(nc.vector.tensor_tensor(a[:, :], a[:, :], c[:, :], ALU.max))
            ch.link(nc.vector.tensor_tensor(a[:, :], a[:, :], r1[:, :], ALU.mult))
            nc.vector.tensor_reduce(top[:, :], a[:, :], AX.X, ALU.max).then_inc(s_top, 1)
            dve.wait_ge(s_topall, 1)
            ch.link(nc.vector.tensor_scalar(scal[:, 4:5], top[:, :], MIN_RANGE, 1.0 / QP, ALU.max, ALU.mult))
            ch.link(nc.vector.tensor_tensor(scal[:, 5:6], scal[:, 4:5], scal[:, 0:1], ALU.mult))
            ch.link(nc.vector.reciprocal(scal[:, 6:7], scal[:, 4:5]))
            ch.link(nc.vector.tensor_tensor(b1c[:, 1:2], b1c[:, 0:1], scal[0:FFN1, 5:6], ALU.mult))
            ch.link(nc.vector.tensor_scalar(a[:, :], r1[:, :], scal[:, 6:7], None, ALU.mult))
            ch.link(nc.vector.tensor_tensor(c[:, :], a[:, :], mean1[:, :], ALU.mult))
            ch.link(nc.vector.memset(hmax[:, :], 0.0))
            base = ch.n

            def quantise(b, slot, loads):
                dve.wait_ge(s_x[slot], loads)
                for j in range(TPB):
                    t = b * TPB + j
                    t1 = bass.ds(t, 1)
                    ch = Chain(dve, s_chain, t + base)
                    dve.wait_ge(s_yq, LEAD + t - 1)
                    ch.link(nc.vector.tensor_scalar(y[:, j % 2, :], xb[:, slot, j, :], a[:, t1], c[:, t1], ALU.mult,
                                                    ALU.add))
                    dve.wait_ge(s_t, LEAD + t - 1)
                    nc.vector.tensor_scalar(yq[:, j % 2, :], y[:, j % 2, :], MAGIC, -MAGIC, ALU.add,
                                            ALU.add).then_inc(s_yq, 1)
                dve.sem_inc(s_x_free, 1)

            def largest(b):
                dve.wait_ge(s_hg, LEAD + b + 1)
                nc.vector.tensor_reduce(hmax[0:FFN1, bass.ds(b, 1)], hT[:, bass.ds(b * BLK, BLK)], AX.X, ALU.max,
                                        apply_absolute_value=True).then_inc(s_hmax, 1)

            quantise(0, 0, 16)

            def part(b, s, left):
                if left:
                    quantise(b + 1, (s + 1) % SLOTS, (b - s) * 4 + (32 if s == SLOTS - 1 else 16))
                largest(b)
            run_blocks(dve, part, SLOTS)
            dve.wait_ge(s_hmax, NB)
            nc.vector.tensor_reduce(hmax[0:FFN1, NB - 1:NB], hT[:, (NB - 1) * BLK:N], AX.X, ALU.max,
                                    apply_absolute_value=True)


def conv(nc, made, rows, X1, X3, HP, gcn_b, whi, wlo, gscale, w2q, ident, dis, scal, hT, hmax):
    sb, ps, sem = made
    brow = sb("b_gcn", [P, D])
    top = sb("top_c", [P, 1])
    hs = sb("hs", [FFN1, BLK])
    hq = sb("hq", [FFN1 + 3, 2, BLK], BF16)
    ones = sb("ones3", [3, BLK], BF16)
    xb = sb("xb_c", [P, 2, TPB, D])
    y = sb("y_c", [P, 2, D])
    yhi = sb("yhi", [P, 2, D], FP16)
    ylo = sb("ylo", [P, 2, D], FP16)
    hb = sb("hb_c", [P, TPB, D])
    st = sb("st_c", [P, TPB, 2, 6])
    mv = sb("mv_c", [P, TPB, 2])
    small = sb("small_c", [P, 2, 5, TPB])
    p_u = ps("p_u", [P, D])
    p_t = ps("p_t_c", [P, D])
    p_h = ps("p_h_c", [P, 2, D])
    s_w = sem("conv_bias")
    s_ones = sem("conv_ones")
    s_onesin = sem("conv_ones_in")
    s_chain = sem("conv_chain")
    s_top = sem("hmax_ready")
    s_topall = sem("hmax_all")
    s_x = [sem(f"c_x1_loaded{s}") for s in range(2)]
    s_x3 = [sem(f"x3_stored{s}") for s in range(2)]
    s_hp = [sem(f"h_stored{s}") for s in range(TPB)]
    s_hq = sem("hq_ready")
    s_hqc = sem("hq_scaled")
    s_u = sem("ffn_in_psum")
    s_x2 = sem("x2_ready")
    s_var = sem("c_var")
    s_sd = sem("c_sd")
    s_mean = sem("c_mean")
    s_y = sem("c_normed")
    s_t = sem("c_turned")
    s_hi = sem("c_high_ready")
    s_lo = sem("c_low_ready")
    s_h = sem("c_h_in_psum")
    s_hb = sem("c_bias_added")
    s_hd = sem("c_h_scaled")
    s_fin = sem("x3_ready")
    leads = (s_x2, s_hq, s_hqc, s_hi, s_lo, s_hb, s_h, s_t, *s_x3, *s_hp)
    PAIRS = NB // 2
    CHAIN = STAT_STEPS + 1

    def run(eng, part):
        with eng.Fori(0, PAIRS - 1) as i:
            part(i, 0, True, True)
            part(i, 1, True, True)
        part(PAIRS - 1, 0, True, False)
        part(PAIRS - 1, 1, False, False)

    with nc.Block() as block:
        @block.sync
        def _(sp):
            for s in leads:
                sp.sem_inc(s, LEAD)
            sp.dma_start(brow[:, :], gcn_b.partition_broadcast(P)).then_inc(s_w, 16)
            sp.dma_start(xb[:, 0], rows(X1, 0, 0, D)).then_inc(s_x[0], 16)
            sp.wait_ge(s_ones, 1)
            for s in range(2):
                sp.dma_start(hq[FFN1:FFN1 + 3, s, :], ones[:, :]).then_inc(s_onesin, 16)

            def part(i, s, front, _):
                b = i * 2 + s
                if front:
                    sp.wait_ge(s_x3[1 - s], LEAD + (i + s) * 16 * TPB)
                    sp.dma_start(xb[:, 1 - s], rows(X1, i + s, 1 - s, D)).then_inc(s_x[1 - s], 16)
                for j in range(TPB):
                    t = b * TPB + j
                    sp.wait_ge(s_fin, t + 1)
                    sp.dma_start(X3[bass.ds(t * P, P), :], xb[:, s, j, :]).then_inc(s_x3[s], 16)
            run(sp, part)
            for s in range(2):
                sp.wait_ge(s_x3[s], LEAD + PAIRS * 16 * TPB)

        @block.gpsimd
        def _(pool):
            nc.gpsimd.memset(ones[:, :], 1.0).then_inc(s_ones, 1)
            pool.wait_ge(s_top, 1)
            nc.gpsimd.partition_all_reduce(top[:, :], top[:, :], P, RMAX).then_inc(s_topall, 1)

        @block.tensor
        def _(pe):
            def ffn(bb, slot, j):
                pe.wait_ge(s_hq, LEAD + bb + 1)
                pe.wait_ge(s_x2, LEAD + bb * TPB + j)
                for h in range(2):
                    last = nc.tensor.matmul(p_u[:, h * 512:(h + 1) * 512], hq[:, slot, j * P:(j + 1) * P],
                                            w2q[:, h * 512:(h + 1) * 512], start=True, stop=True)
                last.then_inc(s_u, 1)

            def turn(t, u):
                pe.wait_ge(s_y, t + 1)
                pe.wait_ge(s_lo, LEAD + t)
                for k in range(KT):
                    last = nc.tensor.transpose(p_t[:, k * P:(k + 1) * P], y[:, u, k * P:(k + 1) * P], ident[:, :])
                last.then_inc(s_t, 1)

            def product(u, h):
                c = slice(h * 512, (h + 1) * 512)
                for n, (yy, ww) in enumerate(((yhi, whi), (yhi, wlo), (ylo, whi))):
                    for k in range(KT):
                        last = nc.tensor.matmul(p_h[:, u, c], yy[:, u, k * P:(k + 1) * P], ww[:, k, c],
                                                start=(n == 0 and k == 0), stop=(n == 2 and k == KT - 1))
                return last

            pe.wait_ge(s_onesin, 32)
            for j in range(TPB):
                ffn(0, 0, j)
            turn(0, 0)

            def part(i, s, front, _):
                b = i * 2 + s
                for j in range(TPB):
                    t = b * TPB + j
                    if front and j in (1, 2):
                        ffn(b + 1, 1 - s, 2 * j - 1)
                    if j < TPB - 1 or front:
                        turn(t + 1, (j + 1) % 2)
                    pe.wait_ge(s_lo, LEAD + t + 1)
                    pe.wait_ge(s_hb, LEAD + t - 1)
                    product(j % 2, 0)
                    if front and j in (0, 1):
                        ffn(b + 1, 1 - s, 2 * j)
                    product(j % 2, 1).then_inc(s_h, 1)
            run(pe, part)

        @block.scalar
        def _(act):
            def deviation(bb, slot):
                act.wait_ge(s_var, bb + 1)
                nc.scalar.activation(small[:, slot, 1, :], small[:, slot, 0, :], ACT.Sqrt).then_inc(s_sd, 1)

            def norm(bb, slot, j):
                act.wait_ge(s_mean, bb + 1)
                act.wait_ge(s_t, LEAD + bb * TPB + j - 1)
                nc.scalar.activation(y[:, j % 2, :], xb[:, slot, j, :], ACT.Identity, bias=small[:, slot, 3, j:j + 1],
                                     scale=small[:, slot, 2, j:j + 1]).then_inc(s_y, 1)

            def high(t, u):
                act.wait_ge(s_t, LEAD + t + 1)
                act.wait_ge(s_h, LEAD + t - 1)
                nc.scalar.activation(yhi[:, u, :], p_t[:, :], ACT.Copy).then_inc(s_hi, 1)

            deviation(0, 0)
            norm(0, 0, 0)
            norm(0, 0, 1)
            high(0, 0)

            def part(i, s, front, _):
                b = i * 2 + s
                for j in range(TPB):
                    t = b * TPB + j
                    if j < TPB - 1 or front:
                        high(t + 1, (j + 1) % 2)
                    if j < 2:
                        norm(b, s, j + 2)
                    elif front:
                        if j == 2:
                            deviation(b + 1, 1 - s)
                        norm(b + 1, 1 - s, j - 2)
                    act.wait_ge(s_hb, LEAD + t + 1)
                    nc.scalar.activation(hb[:, j, :], hb[:, j, :], ACT.Copy,
                                         scale=dis[:, bass.ds(t, 1)]).then_inc(s_hd, 1)
                    act.wait_ge(s_hd, t + 1)
                    act.dma_start(HP[bass.ds(t * P, P), :], hb[:, j, :]).then_inc(s_hp[j], 16)
            run(act, part)
            for j in range(TPB):
                act.wait_ge(s_hp[j], LEAD + NB * 16)

        @block.vector
        def _(dve):
            ch = Chain(dve, s_chain)
            nc.vector.tensor_reduce(top[:, :], hmax[:, :], AX.X, ALU.max).then_inc(s_top, 1)
            dve.wait_ge(s_topall, 1)
            ch.link(nc.vector.tensor_scalar(scal[:, 7:8], top[:, :], MIN_RANGE, 1.0 / QP, ALU.max, ALU.mult))
            ch.link(nc.vector.tensor_tensor(scal[:, 8:9], scal[:, 7:8], scal[:, 1:2], ALU.mult))
            ch.link(nc.vector.reciprocal(scal[:, 9:10], scal[:, 7:8]))
            base = ch.n

            def quantise(bb, slot):
                dve.wait_ge(s_hq, LEAD + bb)
                nc.vector.tensor_scalar(hs[:, :], hT[:, bass.ds(bb * BLK, BLK)], scal[0:FFN1, 9:10], MAGIC,
                                        ALU.mult, ALU.add).then_inc(s_hqc, 1)
                dve.wait_ge(s_hqc, LEAD + bb + 1)
                nc.vector.tensor_scalar(hq[0:FFN1, slot, :], hs[:, :], -MAGIC, None, ALU.add).then_inc(s_hq, 1)

            def second(bb, slot, js, n):
                if n == 0:
                    dve.wait_ge(s_x[slot], s_x_count(bb, slot))
                for j in js:
                    dve.wait_ge(s_u, bb * TPB + j + 1)
                    nc.vector.scalar_tensor_tensor(xb[:, slot, j, :], p_u[:, :], scal[:, 8:9], xb[:, slot, j, :],
                                                   ALU.mult, ALU.add).then_inc(s_x2, 1)
                    dve.wait_ge(s_x2, LEAD + bb * TPB + j + 1)
                    for h in range(2):
                        last = nc.vector.bn_stats(st[:, j, h, :], xb[:, slot, j, h * 512:(h + 1) * 512])
                return last

            def s_x_count(bb, slot):
                return (bb - slot) * 8 + 16

            def moments(bb, slot, last):
                ch = Chain(dve, s_chain, bb * CHAIN + base)
                sm = small[:, slot]
                ch.link(last)
                nc.vector.memset(sm[:, 4, :], 0.0)
                for j in range(TPB):
                    last = nc.vector.bn_aggr(mv[:, j, :], st[:, j])
                ch.link(last)
                ch.link(nc.vector.tensor_scalar(sm[:, 0, :], mv[:, :, 1], LN_EPS, None, ALU.add))
                dve.sem_inc(s_var, 1)
                ch.link(nc.vector.tensor_scalar(sm[:, 3, :], mv[:, :, 0], -YSCALE, None, ALU.mult))
                dve.wait_ge(s_sd, bb + 1)
                rsqrt_rest(nc, ch, sm[:, 0, :], sm[:, 1, :], sm[:, 2, :], sm[:, 4, :])
                ch.link(nc.vector.tensor_tensor(sm[:, 3, :], sm[:, 3, :], sm[:, 2, :], ALU.mult))
                nc.vector.tensor_scalar(sm[:, 2, :], sm[:, 2, :], YSCALE, None, ALU.mult).then_inc(s_mean, 1)
                assert ch.n == CHAIN, ch.n

            def low(t, u):
                dve.wait_ge(s_hi, LEAD + t + 1)
                nc.vector.tensor_tensor(ylo[:, u, :], p_t[:, :], yhi[:, u, :], ALU.subtract).then_inc(s_lo, 1)

            quantise(0, 0)
            quantise(1, 1)
            moments(0, 0, second(0, 0, range(TPB), 0))
            low(0, 0)
            dve.wait_ge(s_w, 16)

            def part(i, s, front, more):
                b = i * 2 + s
                for j in range(TPB):
                    t = b * TPB + j
                    if j < TPB - 1 or front:
                        low(t + 1, (j + 1) % 2)
                    if front and j < TPB - 1:
                        last = second(b + 1, 1 - s, ((0,), (1, 2), (3,))[j], j)
                        if j == 2:
                            moments(b + 1, 1 - s, last)
                    if more and j == TPB - 1:
                        quantise(b + 2, s)
                    dve.wait_ge(s_h, LEAD + t + 1)
                    dve.wait_ge(s_hp[j], LEAD + b * 16)
                    nc.vector.scalar_tensor_tensor(hb[:, j, :], p_h[:, j % 2, :], gscale[:, 1:2], brow[:, :],
                                                   ALU.mult, ALU.add).then_inc(s_hb, 1)
                    dve.wait_ge(s_hd, t + 1)
                    nc.vector.scalar_tensor_tensor(xb[:, s, j, :], hb[:, j, :], dis[:, bass.ds(t, 1)],
                                                   xb[:, s, j, :], ALU.mult, ALU.add).then_inc(s_fin, 1)
            run(dve, part)


def edges(nc, made, s_de, s_g, s_sct, X3, HP, DIS_D, by_src, sorted_src, e127):
    sb, ps, sem = made
    KB = sb("KB_e", [P, EP])
    cols = sb("cols_e", [P, 4, ET])
    prev = sb("prev_e", [P, 1 + ET])
    idx = sb("idx_e", [P, 3, ET], I32)
    de = sb("dis_e", [P, ET])
    H = sb("H_e", [P, 4, D])
    X = sb("X_e", [P, 4, D])
    OS = sb("OS_e", [P, 2, D])
    SM = sb("SM_e", [P, 2, 2, P])
    p_o = ps("p_o_e", [P, 2, D])
    s_in = sem("e_loaded")
    s_chain = sem("e_chain")
    s_idx = sem("e_indices")
    s_sm = sem("e_masks")
    s_o = sem("e_sums")
    s_oe = sem("e_sums_copied")
    s_res = sem("e_rows_ready")
    with nc.Block() as block:
        @block.sync
        def _(sp):
            for s in (s_oe, s_res):
                sp.sem_inc(s, LEAD)
            sp.dma_start(KB[:, :], sorted_src[:, 0].partition_broadcast(P)).then_inc(s_in, 16)
            with nc.allow_non_contiguous_dma(reason="one value of every edge"):
                sp.dma_start(cols[:, 0, :], sorted_src.rearrange("(t p) o -> p (t o)", p=P)).then_inc(s_in, 16)
                sp.dma_start(cols[:, 1, :], by_src.rearrange("(t p) o -> p t o", p=P)[:, :, 1]).then_inc(s_in, 16)
                sp.dma_start(cols[:, 2, 0:ET - 1], sorted_src[1:EP - P + 1].rearrange(
                    "(t p) o -> p (t o)", p=P)).then_inc(s_in, 16)
                sp.dma_start(cols[0:P - 1, 2, ET - 1:ET], sorted_src[EP - P + 1:EP]).then_inc(s_in, 16)
                sp.dma_start(cols[P - 1:P, 2, ET - 1:ET], sorted_src[0:1]).then_inc(s_in, 16)

        @block.gpsimd
        def _(pool):
            def scatter(t):
                s = t % 4
                pool.wait_ge(s_res, LEAD + t + 1)
                nc.gpsimd.indirect_dma_start(X3, bass.IndirectOffsetOnAxis(ap=idx[:, 2, t:t + 1], axis=0),
                                             X[:, s, :], None, bounds_check=NP - 1, oob_is_err=False
                                             ).then_inc(s_sct[s], 16)

            pool.wait_ge(s_idx, 1)
            for t in range(ET):
                nc.gpsimd.indirect_dma_start(de[:, t:t + 1], None, DIS_D, bass.IndirectOffsetOnAxis(
                    ap=idx[:, 0, t:t + 1], axis=0)).then_inc(s_de, 16)
            for t in range(ET):
                s = t % 4
                if t >= 4:
                    pool.wait_ge(s_o, t - 3)
                    pool.wait_ge(s_sct[s], t // 4 * 16)
                nc.gpsimd.indirect_dma_start(H[:, s, :], None, HP, bass.IndirectOffsetOnAxis(
                    ap=idx[:, 1, t:t + 1], axis=0)).then_inc(s_g[s], 16)
                nc.gpsimd.indirect_dma_start(X[:, s, :], None, X3, bass.IndirectOffsetOnAxis(
                    ap=idx[:, 0, t:t + 1], axis=0)).then_inc(s_g[s], 16)
                if t >= 2:
                    scatter(t - 2)
            for t in range(ET - 2, ET):
                scatter(t)
            for s in range(4):
                pool.wait_ge(s_sct[s], ET // 4 * 16)

        @block.vector
        def _(dve):
            ch = Chain(dve, s_chain)
            dve.wait_ge(s_in, 16 * 6)
            ch.link(nc.vector.tensor_copy(idx[:, 0, :], cols[:, 0, :]))
            ch.link(nc.vector.tensor_copy(idx[:, 1, :], cols[:, 1, :]))
            ch.link(nc.vector.tensor_tensor(cols[:, 3, :], cols[:, 0, :], cols[:, 2, :], ALU.is_equal))
            ch.link(nc.vector.tensor_scalar(cols[:, 3, :], cols[:, 3, :], SKIP, None, ALU.mult))
            ch.link(nc.vector.tensor_tensor(cols[:, 3, :], cols[:, 3, :], cols[:, 0, :], ALU.add))
            ch.link(nc.vector.tensor_copy(idx[:, 2, :], cols[:, 3, :]))
            ch.link(nc.vector.memset(prev[:, 0:1], -1.0))
            ch.link(nc.vector.tensor_copy(prev[:, 1:1 + ET], cols[:, 0, :]))
            ch.link(nc.vector.memset(OS[:, :, :], 0.0))
            dve.sem_inc(s_idx, 1)
            dve.wait_ge(s_de, 16 * ET)

            def masks(t, s):
                kb = KB[:, bass.ds(t * P, P)]
                nc.vector.tensor_scalar(SM[:, s, 0, :], kb, cols[:, 0, bass.ds(t, 1)], None, ALU.is_equal)
                nc.vector.tensor_scalar(SM[:, s, 1, :], kb, prev[:, bass.ds(t, 1)], e127[:, 0:1],
                                        ALU.is_equal, ALU.mult).then_inc(s_sm, 1)

            with dve.Fori(0, ET // 4) as i:
                for s in range(4):
                    t = i * 4 + s
                    masks(t, s % 2)
                    dve.wait_ge(s_g[s], i * 32 + 32)
                    dve.wait_ge(s_oe, LEAD + t + 1)
                    nc.vector.scalar_tensor_tensor(X[:, s, :], OS[:, s % 2, :], de[:, bass.ds(t, 1)], X[:, s, :],
                                                   ALU.mult, ALU.add).then_inc(s_res, 1)

        @block.scalar
        def _(act):
            with act.Fori(0, ET // 4) as i:
                for s in range(4):
                    t = i * 4 + s
                    act.wait_ge(s_o, t + 1)
                    act.wait_ge(s_res, LEAD + t)
                    nc.scalar.activation(OS[:, s % 2, :], p_o[:, s % 2, :], ACT.Copy).then_inc(s_oe, 1)

        @block.tensor
        def _(pe):
            pe.wait_ge(s_idx, 1)
            with pe.Fori(0, ET // 4) as i:
                for s in range(4):
                    t = i * 4 + s
                    pe.wait_ge(s_sm, t + 1)
                    pe.wait_ge(s_g[s], i * 32 + 32)
                    pe.wait_ge(s_oe, LEAD + t)
                    for h in range(2):
                        c = slice(h * 512, (h + 1) * 512)
                        nc.tensor.matmul(p_o[:, s % 2, c], SM[:, s % 2, 0, :], H[:, s, c], start=True, stop=False)
                        last = nc.tensor.matmul(p_o[:, s % 2, c], SM[:, s % 2, 1, :], OS[:, 1 - s % 2, c],
                                                start=False, stop=True)
                    last.then_inc(s_o, 1)


def gated(nc, made, X3, w_gateT, w_upT, w_downT, ident, out):
    sb, ps, sem = made
    M = UPROW + FFN2
    SLOTS = 4
    wi = sb("wi", [P, KT, M], I32)
    wf = sb("wf", [P, KT, M])
    wh = sb("wh_g", [P, KT, M], FP16)
    wl = sb("wl_g", [P, KT, M], FP16)
    top = sb("top_g", [P, 1])
    unscale = sb("unscale_g", [P, 2])
    di = sb("di", [FFN2, D], I32)
    wd = sb("wd_g", [FFN2, D])
    xb = sb("xb_g", [P, SLOTS, TPB, D])
    y = sb("y_g", [P, 2, D])
    yhi = sb("yhi_g", [P, 2, KT, BLK], FP16)
    ylo = sb("ylo_g", [P, 2, KT, BLK], FP16)
    hh = sb("hh_g", [FFN2, 2, BLK])
    st = sb("st_g", [P, TPB, 2, 6])
    mv = sb("mv_g", [P, TPB, 2])
    small = sb("small_g", [P, 2, 5, TPB])
    p_t = ps("p_t_g", [P, 2, D])
    p_g = ps("p_g", [P, 2, BLK])
    p_o = ps("p_o_g", [P, D])
    s_w = sem("gated_weights")
    s_wz = sem("gated_zeros")
    s_top = sem("gated_top")
    s_topall = sem("gated_top_all")
    s_wf = sem("gated_weights_ready")
    s_chain = sem("gated_chain")
    s_x = [sem(f"g_x3_loaded{s}") for s in range(SLOTS)]
    s_out = [sem(f"out_stored{s}") for s in range(SLOTS)]
    s_var = sem("g_var")
    s_sd = sem("g_sd")
    s_mean = sem("g_mean")
    s_y = sem("g_normed")
    s_t = sem("g_y_turned")
    s_hi = sem("g_high_ready")
    s_lo = sem("g_low_ready")
    s_gu = sem("gate_up_in_psum")
    s_si = sem("silu_ready")
    s_hh = sem("hidden_ready")
    s_o = sem("g_out_in_psum")
    s_fin = sem("g_out_ready")
    leads = (*s_out, s_t, s_lo, s_hh, s_fin, s_gu)
    CHAIN = STAT_STEPS + 1

    def run(eng, part):
        with eng.Fori(0, NB // SLOTS - 1) as i:
            for s in range(SLOTS):
                part(i * SLOTS + s, s, SLOTS)
        for s in range(SLOTS):
            part(NB - SLOTS + s, s, SLOTS - 1 - s)

    def xrows(ap, b):
        return ap[bass.ds(b * BLK, BLK), :].rearrange("(j p) d -> p j d", p=P)

    with nc.Block() as block:
        @block.sync
        def _(sp):
            for s in leads:
                sp.sem_inc(s, LEAD)
            for b in range(SLOTS - 1):
                sp.dma_start(xb[:, b], xrows(X3, b)).then_inc(s_x[b], 16)
            sp.wait_ge(s_wz, 1)
            sp.dma_start(wi[:, :, 0:FFN2], w_gateT.rearrange("(k p) h -> p k h", p=P)).then_inc(s_w, 16)
            sp.dma_start(wi[:, :, UPROW:M], w_upT.rearrange("(k p) h -> p k h", p=P)).then_inc(s_w, 16)
            sp.dma_start(di[:, :], w_downT).then_inc(s_w, 16)

            def part(b, s, left):
                if left >= SLOTS - 1:
                    n = (s - 1) % SLOTS
                    sp.wait_ge(s_out[n], LEAD + (b - s) * 4 + (16 if s else 0))
                    sp.dma_start(xb[:, n], xrows(X3, b + SLOTS - 1)).then_inc(s_x[n], 16)
                sp.wait_ge(s_fin, LEAD + b * TPB + TPB)
                sp.dma_start(xrows(out, b), xb[:, s]).then_inc(s_out[s], 16)
            run(sp, part)
            for s in range(SLOTS):
                sp.wait_ge(s_out[s], LEAD + NB // SLOTS * 16)

        @block.gpsimd
        def _(pool):
            nc.gpsimd.memset(wi[:, :, :], 0).then_inc(s_wz, 1)
            pool.wait_ge(s_top, 1)
            nc.gpsimd.partition_all_reduce(top[:, :], top[:, :], P, RMAX).then_inc(s_topall, 1)

        @block.tensor
        def _(pe):
            def turn(t, j):
                pe.wait_ge(s_y, t + 1)
                pe.wait_ge(s_lo, LEAD + t - 1)
                for k in range(KT):
                    last = nc.tensor.transpose(p_t[:, j % 2, k * P:(k + 1) * P], y[:, j % 2, k * P:(k + 1) * P],
                                               ident[:, :])
                last.then_inc(s_t, 1)

            def gate_up(b, u):
                pe.wait_ge(s_lo, LEAD + b * TPB + TPB)
                pe.wait_ge(s_hh, LEAD + b - 1)
                for n, (yy, ww) in enumerate(((yhi, wh), (yhi, wl), (ylo, wh))):
                    for k in range(KT):
                        last = nc.tensor.matmul(p_g[0:M, u, :], ww[:, k, :], yy[:, u, k, :],
                                                start=(n == 0 and k == 0), stop=(n == 2 and k == KT - 1))
                last.then_inc(s_gu, 1)

            def down(b, j, u):
                pe.wait_ge(s_hh, LEAD + b + 1)
                pe.wait_ge(s_fin, LEAD + b * TPB + j)
                for h in range(2):
                    last = nc.tensor.matmul(p_o[:, h * 512:(h + 1) * 512], hh[:, u, j * P:(j + 1) * P],
                                            wd[:, h * 512:(h + 1) * 512], start=True, stop=True)
                last.then_inc(s_o, 1)

            for j in range(TPB):
                turn(j, j)
            pe.wait_ge(s_wf, 1)
            gate_up(0, 0)

            def part(b, s, left):
                for j in range(TPB):
                    if left:
                        turn(b * TPB + TPB + j, j)
                    down(b, j, s % 2)
                if left:
                    gate_up(b + 1, (s + 1) % 2)
            run(pe, part)

        @block.scalar
        def _(act):
            def deviation(b, u):
                act.wait_ge(s_var, b + 1)
                nc.scalar.activation(small[:, u, 1, :], small[:, u, 0, :], ACT.Sqrt).then_inc(s_sd, 1)

            def norm(b, slot, j):
                act.wait_ge(s_mean, b + 1)
                act.wait_ge(s_t, LEAD + b * TPB + j - 1)
                nc.scalar.activation(y[:, j % 2, :], xb[:, slot, j, :], ACT.Identity,
                                     bias=small[:, slot % 2, 3, j:j + 1],
                                     scale=small[:, slot % 2, 2, j:j + 1]).then_inc(s_y, 1)

            def high(b, u, j):
                act.wait_ge(s_t, LEAD + b * TPB + j + 1)
                if j == 0:
                    act.wait_ge(s_gu, LEAD + b - 1)
                nc.scalar.activation(yhi[:, u, :, j * P:(j + 1) * P],
                                     p_t[:, j % 2, :].rearrange("p (k n) -> p k n", k=KT), ACT.Copy).then_inc(s_hi, 1)

            def front(b, slot):
                for j in range(TPB):
                    high(b, slot % 2, j)
                    if j < 2:
                        norm(b, slot, j + 2)

            deviation(0, 0)
            norm(0, 0, 0)
            norm(0, 0, 1)
            deviation(1, 1)
            front(0, 0)

            def part(b, s, left):
                if left:
                    norm(b + 1, (s + 1) % SLOTS, 0)
                    norm(b + 1, (s + 1) % SLOTS, 1)
                act.wait_ge(s_gu, LEAD + b + 1)
                nc.scalar.activation(hh[:, s % 2, :], p_g[0:FFN2, s % 2, :], ACT.Silu,
                                     scale=unscale[0:FFN2, 1:2]).then_inc(s_si, 1)
                if left:
                    front(b + 1, (s + 1) % SLOTS)
                if left > 1:
                    deviation(b + 2, s % 2)
            run(act, part)

        @block.vector
        def _(dve):
            ch = Chain(dve, s_chain)

            def stats(b, slot, j):
                if j == 0:
                    dve.wait_ge(s_x[slot], (b - slot) * 4 + 16)
                for h in range(2):
                    last = nc.vector.bn_stats(st[:, j, h, :], xb[:, slot, j, h * 512:(h + 1) * 512])
                return last

            def moments(b, slot, last, base):
                ch = Chain(dve, s_chain, b * CHAIN + base)
                sm = small[:, slot % 2]
                ch.link(last)
                nc.vector.memset(sm[:, 4, :], 0.0)
                for j in range(TPB):
                    last = nc.vector.bn_aggr(mv[:, j, :], st[:, j])
                ch.link(last)
                dve.wait_ge(s_y, b * TPB - TPB) if type(b) is not int or b > 1 else None
                ch.link(nc.vector.tensor_scalar(sm[:, 0, :], mv[:, :, 1], LN_EPS, None, ALU.add))
                dve.sem_inc(s_var, 1)
                ch.link(nc.vector.tensor_scalar(sm[:, 3, :], mv[:, :, 0], -YSCALE, None, ALU.mult))
                dve.wait_ge(s_sd, b + 1)
                rsqrt_rest(nc, ch, sm[:, 0, :], sm[:, 1, :], sm[:, 2, :], sm[:, 4, :])
                ch.link(nc.vector.tensor_tensor(sm[:, 3, :], sm[:, 3, :], sm[:, 2, :], ALU.mult))
                nc.vector.tensor_scalar(sm[:, 2, :], sm[:, 2, :], YSCALE, None, ALU.mult).then_inc(s_mean, 1)
                assert ch.n == CHAIN, ch.n

            def low(b, u, j):
                dve.wait_ge(s_hi, b * TPB + j + 1)
                c = slice(j * P, (j + 1) * P)
                nc.vector.tensor_tensor(ylo[:, u, :, c], p_t[:, j % 2, :].rearrange("p (k n) -> p k n", k=KT),
                                        yhi[:, u, :, c], ALU.subtract).then_inc(s_lo, 1)

            def finish(b, s, j):
                dve.wait_ge(s_o, b * TPB + j + 1)
                nc.vector.tensor_tensor(xb[:, s, j, :], xb[:, s, j, :], p_o[:, :], ALU.add).then_inc(s_fin, 1)

            for b in range(2):
                for j in range(TPB):
                    last = stats(b, b, j)
                moments(b, b, last, 0)
            low(0, 0, 0)
            base = 2 * CHAIN
            ch = Chain(dve, s_chain, base)
            dve.wait_ge(s_w, 48)
            ch.link(nc.vector.tensor_copy(wf[:, :, :], wi[:, :, :]))
            low(0, 0, 1)
            ch.link(nc.vector.tensor_scalar(wf[:, :, :], wf[:, :, :], 1.0 / QP, None, ALU.mult))
            nc.vector.tensor_reduce(top[:, :], wf[:, :, :], AX.XY, ALU.max,
                                    apply_absolute_value=True).then_inc(s_top, 1)
            low(0, 0, 2)
            low(0, 0, 3)
            ch.link(nc.vector.tensor_copy(wd[:, :], di[:, :]))
            ch.link(nc.vector.tensor_scalar(wd[:, :], wd[:, :], 1.0 / QP, None, ALU.mult))
            dve.wait_ge(s_topall, 1)
            ch.link(nc.vector.tensor_scalar(top[:, :], top[:, :], 1e-30, 1.0 / WMAX, ALU.max, ALU.mult))
            ch.link(nc.vector.reciprocal(unscale[:, 0:1], top[:, :]))
            ch.link(nc.vector.tensor_scalar(unscale[:, 1:2], top[:, :], 1.0 / YSCALE, None, ALU.mult))
            ch.link(nc.vector.tensor_scalar(wf[:, :, :], wf[:, :, :], unscale[:, 0:1], None, ALU.mult))
            ch.link(nc.vector.tensor_copy(wh[:, :, :], wf[:, :, :]))
            ch.link(nc.vector.tensor_tensor(wl[:, :, :], wf[:, :, :], wh[:, :, :], ALU.subtract))
            dve.sem_inc(s_wf, 1)
            base2 = ch.n

            def part(b, s, left):
                dve.wait_ge(s_si, b + 1)
                nc.vector.scalar_tensor_tensor(hh[:, s % 2, :], p_g[UPROW:M, s % 2, :], unscale[0:FFN2, 1:2],
                                               hh[:, s % 2, :], ALU.mult, ALU.mult).then_inc(s_hh, 1)
                for j in range(TPB):
                    if left:
                        low(b + 1, (s + 1) % 2, j)
                    if left > 1:
                        last = stats(b + 2, (s + 2) % SLOTS, j)
                    finish(b, s, j)
                if left > 1:
                    moments(b + 2, (s + 2) % SLOTS, last, base2)
            run(dve, part)


def kernel(x, src, dst, L0_gnn_rms_w, L0_gnn_W_down, L0_gnn_Wl, L0_gnn_Wr, L0_gnn_att, L0_gnn_W_up, L0_ffn_w1,
           L0_ffn_b1, L0_ffn_w2, L0_ffn_b2, L1_gnn_W, L1_gnn_b, L1_ffn_w_gate, L1_ffn_w_up, L1_ffn_w_down):
    import numpy as np
    import concourse.bacc as bacc
    from concourse import mybir as mb
    from concourse.bass_utils import run_bass_kernel_spmd

    def lay(a):
        return np.ascontiguousarray(np.asarray(a))

    xp = np.zeros((NP, D), np.float32)
    xp[:N] = np.asarray(x)
    ends = []
    for e in (src, dst):
        p = np.full((EP,), NP - 1, np.int32)
        p[:E] = np.asarray(e)
        ends.append(p)
    arrays = {
        "x": xp, "xT": lay(xp.T),
        "src_row": ends[0], "dst_row": ends[1],
        "src_col": lay(ends[0].reshape(ET, P).T), "dst_col": lay(ends[1].reshape(ET, P).T),
        "rms_w": lay(np.asarray(L0_gnn_rms_w).reshape(KT, P).T),
        "W_down": lay(L0_gnn_W_down), "Wl": lay(L0_gnn_Wl), "Wr": lay(L0_gnn_Wr),
        "att": lay(L0_gnn_att).reshape(HID), "W_up": lay(L0_gnn_W_up),
        "w1T": lay(np.asarray(L0_ffn_w1).T), "b1": lay(L0_ffn_b1).reshape(FFN1, 1),
        "w2T": lay(np.asarray(L0_ffn_w2).T), "b2": lay(L0_ffn_b2).reshape(1, D),
        "gcnT": lay(np.asarray(L1_gnn_W).T), "gcn_b": lay(L1_gnn_b).reshape(D),
        "w_gateT": lay(np.asarray(L1_ffn_w_gate).T), "w_upT": lay(np.asarray(L1_ffn_w_up).T),
        "w_downT": lay(np.asarray(L1_ffn_w_down).T),
        "ident_in": np.eye(P, dtype=np.float32),
    }
    nc = bacc.Bacc("TRN2", target_bir_lowering=False, num_devices=1)
    feeds, args = {}, {}
    for name, a in arrays.items():
        feeds[f"in_{name}"] = a
        args[name] = nc.dram_tensor(f"in_{name}", a.shape, mb.dt.from_np(a.dtype), kind="ExternalInput").ap()
    args["out"] = nc.dram_tensor("out_rows", [NP, D], mb.dt.float32, kind="ExternalOutput").ap()
    build(nc, **args)
    r = run_bass_kernel_spmd(nc, [feeds], core_ids=[0])
    return r.results[0]["out_rows"][:N]
```

```python
from contextlib import ExitStack

import concourse.bass as bass
from concourse import mybir

FP32 = mybir.dt.float32
BF16 = mybir.dt.bfloat16
FP16 = mybir.dt.float16
I32 = mybir.dt.int32
ALU = mybir.AluOpType
ACT = mybir.ActivationFunctionType
AX = mybir.AxisListType
RMAX = bass.bass_isa.ReduceOp.absmax

P = 128
N, D, E = 10000, 1024, 5000
HID, HEADS, FFN1, FFN2 = 256, 4, 64, 48
HD = HID // HEADS
KT = D // P
TPB = 4
BLK = TPB * P
NB = -(-N // BLK)
NP = NB * BLK
NT = NP // P
ET = -(-E // P)
EP = ET * P
UPROW = 64
LN_EPS, RMS_EPS, DEN_EPS = 1e-5, 1e-6, 1e-16
SLOPE, QP, MIN_RANGE = 0.2, 127.0, 1e-6
MAGIC = 1.5 * 2.0 ** 23
SKIP = float(2 ** 20)
FAR = -1.0e30
YSCALE, WMAX = 2.0 ** 10, 2.0 ** 12
ESLOTS = 8
LEAD = 16


class Chain:

    def __init__(self, eng, sem, base=0):
        self.eng, self.sem, self.base, self.n = eng, sem, base, 0

    def link(self, ins):
        self.n += 1
        ins.then_inc(self.sem, 1)
        self.eng.wait_ge(self.sem, self.base + self.n)


def rsqrt_rest(nc, ch, var, sd, r, tmp):
    ch.link(nc.vector.reciprocal(r, sd))
    ch.link(nc.vector.tensor_tensor(tmp, r, r, ALU.mult))
    ch.link(nc.vector.tensor_tensor(tmp, tmp, var, ALU.mult))
    ch.link(nc.vector.tensor_scalar(tmp, tmp, -0.5, 1.5, ALU.mult, ALU.add))
    ch.link(nc.vector.tensor_tensor(r, r, tmp, ALU.mult))


class Edges:
    pass


def build(nc, x, xT, src_row, dst_row, src_col, dst_col, rms_w, W_down, Wl, Wr, att, W_up,
          w1T, b1, w2T, b2, gcnT, gcn_b, w_gateT, w_upT, w_downT, ident_in, out):
    T = nc.dram_tensor("node_rows", [NP, 2 * HID], FP32).ap()
    X1 = nc.dram_tensor("x1_rows", [NP, D], FP32).ap()
    X3 = nc.dram_tensor("x3_rows", [NP, D], FP32).ap()
    HP = nc.dram_tensor("h_rows", [NP, D], FP32).ap()
    DIS_D = nc.dram_tensor("dis_rows", [NP, 1], FP32).ap()
    by_src = nc.dram_tensor("by_src", [EP, 2], FP32).ap()
    sorted_key = [nc.dram_tensor(f"sorted_{n}", [EP, 1], FP32).ap() for n in ("src", "dst")]
    by_dst = nc.dram_tensor("by_dst", [EP, 2], FP32).ap()
    T_half = T.rearrange("n (h c) -> (n h) c", h=2)

    keep = ExitStack()
    used = []

    def maker(ctx):
        def sb(name, shape, dt=FP32):
            return ctx.enter_context(nc.sbuf_tensor(name, shape, dt))

        def ps(name, shape, dt=FP32):
            return ctx.enter_context(nc.psum_tensor(name, shape, dt))

        def sem(name):
            used.append(ctx.enter_context(nc.semaphore(name)))
            return used[-1]
        return sb, ps, sem

    def clear_used():
        with nc.Block() as block:
            @block.sync
            def _(sp):
                numbers = sorted(s.num for s in used)
                assert numbers == list(range(numbers[0], numbers[-1] + 1))
                sp.sem_clear(range(numbers[0], numbers[-1] + 1))
        used.clear()

    def rows(ap, i, b, width):
        return ap[bass.ds(i * (2 * BLK) + b * BLK, BLK), 0:width].rearrange("(j p) d -> p j d", p=P)

    with keep:
        sbk, _, _ = maker(keep)
        s_scat, s_sct, s_de, *more = [keep.enter_context(nc.semaphore(n)) for n in (
            "scattered", "rows_scattered", "e_dis", *(f"edge_rows{t}" for t in range(4)), *(f"e_rows{t}" for t in range(ESLOTS)),
            *(f"e_scattered{t}" for t in range(ESLOTS)))]
        s_gat, s_ge, s_sce = more[0:4], more[4:4 + ESLOTS], more[4 + ESLOTS:]
        ident = sbk("ident", [P, P])
        identb = sbk("identb", [P, P], BF16)
        dis = sbk("dis", [P, NT])
        e127 = sbk("e127", [P, 1])
        scal = sbk("scal", [P, 16])
        w1q = sbk("w1q", [P, KT, FFN1], BF16)
        w2q = sbk("w2q", [FFN1 + 3, D], BF16)
        b1c = sbk("b1c", [FFN1, 2])
        by = Edges()
        by.cols = sbk("e_cols", [P, 4, ET])
        by.prev = sbk("e_prev", [P, 1 + ET])
        by.idx = sbk("e_idx", [P, 3, ET], I32)
        by.dis = sbk("e_dis_src", [P, ET])

        with ExitStack() as ctx:
            sb, ps, sem = maker(ctx)
            SORT_FIRST, SORT_PER, HOT_PER = 4, 3, 5
            SORT_BLOCKS = (ET - SORT_FIRST) // SORT_PER
            assert SORT_BLOCKS % 2 == 0 and HOT_PER * (NB - SORT_BLOCKS) == ET
            scratch = sb("scratch", [P, EP], I32)
            junk = scratch[:, 0:EP // 2].bitcast(BF16)
            junk_act = scratch[:, EP // 2:EP].bitcast(BF16)
            key = [sb(f"key{k}", [P, EP]) for k in range(2)]
            col_int = [sb(f"col_int{k}", [P, ET], I32) for k in range(2)]
            col = sb("col", [P, ET, 2])
            pair = sb("pair", [P, ET, 2])
            colq = [sb(f"colq{k}", [P, ET]) for k in range(2)]
            junk_diag = sb("junk_diag", [P, P], BF16)
            count = [sb(f"count{k}", [P, ET]) for k in range(2)]
            ties = [sb(f"ties{k}", [P, ET]) for k in range(2)]
            pos = [sb(f"pos{k}", [P, ET], I32) for k in range(2)]
            tri = sb("tri", [P, P])
            iota = sb("iota", [P, P])
            hi_int = sb("hi_int", [P, ET], I32)
            lo_int = sb("lo_int", [P, ET], I32)
            hi = sb("hi", [P, ET])
            lo = sb("lo", [P, ET])
            one_lo = sb("one_lo", [P, HOT_PER, P], BF16)
            one_hi = sb("one_hi", [P, HOT_PER, NT], BF16)
            zero = sb("zero", [P, P], BF16)
            deg = sb("deg", [P, 3, NT])
            w1 = sb("w1", [P, KT, FFN1])
            w2 = sb("w2", [FFN1, D])
            b2r = sb("b2r", [1, 2, D])
            b2p = sb("b2p", [1, 3, D], BF16)
            wmax = sb("wmax", [P, 2])
            wd = sb("wd", [P, KT, HID])
            wlr = sb("wlr", [P, 2, 2 * HID])
            rms = sb("rms", [P, KT])
            mean_of = sb("mean_of", [P, P])
            xt = sb("xt", [P, 2, KT, BLK])
            xb = sb("xb", [P, 2, TPB, D])
            xdT = sb("xdT", [P, 2, 2, BLK])
            lr = sb("lr", [P, 2, TPB, 2 * HID])
            st = sb("st", [P, TPB, 2, 6])
            mv = sb("mv", [P, TPB, 2])
            small = sb("small", [P, 2, 4, TPB])
            hist = ps("hist", [P, NT])
            p_xd = ps("p_xd", [P, 2, 2, BLK])
            p_lr = ps("p_lr", [P, 2, 2 * HID])

            loaded = [sem(f"keys_loaded{k}") for k in range(2)]
            s_conv = sem("src_keys_converted")
            s_w = sem("small_weights")
            s_pw = sem("project_weights")
            s_const = sem("constants")
            s_chain = sem("project_chain")
            s_key = sem("keys_ready")
            s_sign = sem("dst_counted")
            s_shift = sem("dst_shifted")
            s_hot = sem("onehots_ready")
            s_hist = sem("hist_step")
            s_pos = sem("ranks_ready")
            s_deg = sem("degree_ready")
            s_dsd = sem("degree_sqrt")
            s_wmax = sem("weight_max")
            s_wall = sem("weight_max_all")
            s_b2 = sem("b2_parts")
            s_b2in = sem("b2_in")
            s_dis = sem("dis_ready")
            s_end = sem("sort_stores")
            s_wf = sem("wd_folded")
            s_mean = sem("wd_mean")
            s_wc = sem("wd_centred")
            s_xt = [sem(f"xT_loaded{s}") for s in range(2)]
            s_xb = [sem(f"x_loaded{s}") for s in range(2)]
            s_xt_free = sem("xT_used")
            s_xb_free = sem("x_used")
            s_xd = sem("xd_in_psum")
            s_xde = sem("xd_copied")
            s_lr = sem("lr_in_psum")
            s_lre = sem("lr_copied")
            s_var = sem("var_ready")
            s_sd = sem("sd_ready")
            s_r = sem("scale_ready")
            s_lrfree = [sem(f"lr_stored{s}") for s in range(2)]
            leads = (s_xt_free, s_shift, s_hist, s_xde, s_lre, s_lr, s_xd, *s_lrfree)

            def run(eng, part):
                with eng.Fori(0, SORT_BLOCKS // 2) as i:
                    for s in range(2):
                        part(i, s, SORT_PER, 0, True)
                with eng.Fori(SORT_BLOCKS // 2, NB // 2 - 1) as i:
                    for s in range(2):
                        part(i, s, 0, HOT_PER, True)
                for s in range(2):
                    part(NB // 2 - 1, s, 0, HOT_PER, s == 0)

            with nc.Block() as block:
                @block.sync
                def _(sp):
                    for s in leads:
                        sp.sem_inc(s, LEAD)
                    sp.dma_start(wd[:, :, :], W_down.rearrange("(k p) h -> p k h", p=P)).then_inc(s_pw, 16)
                    sp.dma_start(rms[:, :], rms_w).then_inc(s_pw, 16)
                    sp.dma_start(xt[:, 0], xT[:, 0:BLK].rearrange("(k p) n -> p k n", p=P)).then_inc(s_xt[0], 16)
                    for k, w in enumerate((Wl, Wr)):
                        sp.dma_start(wlr[:, :, k * HID:(k + 1) * HID],
                                     w.rearrange("(k p) h -> p k h", p=P)).then_inc(s_pw, 16)
                    for k, (r, c) in enumerate(((src_row, src_col), (dst_row, dst_col))):
                        if k:
                            sp.wait_ge(s_conv, 1)
                        sp.dma_start(scratch[:, :], r.partition_broadcast(P)).then_inc(loaded[k], 16)
                        sp.dma_start(col_int[k][:, :], c).then_inc(loaded[k], 16)
                    for dst, s in ((ident[:, :], ident_in), (w2[:, :], w2T), (b2r[:, 0, :], b2), (b1c[:, 0:1], b1)):
                        sp.dma_start(dst, s).then_inc(s_w, 16)
                    sp.dma_start(w1[:, :, :], w1T.rearrange("(k p) h -> p k h", p=P)).then_inc(s_w, 16)

                    def part(i, s, sorts, hots, more):
                        b = i * 2 + s
                        if more:
                            sp.wait_ge(s_xt_free, LEAD + b)
                            sp.dma_start(xt[:, 1 - s], xT[:, bass.ds((b + 1) * BLK, BLK)].rearrange(
                                "(k p) n -> p k n", p=P)).then_inc(s_xt[1 - s], 16)
                        sp.wait_ge(s_xb_free, b + 1)
                        sp.dma_start(xb[:, s], rows(x, i, s, D)).then_inc(s_xb[s], 16)
                    run(sp, part)
                    sp.wait_ge(s_b2, 1)
                    for k in range(3):
                        sp.dma_start(w2q[FFN1 + k:FFN1 + k + 1, :], b2p[:, k, :]).then_inc(s_b2in, 16)
                    sp.wait_ge(s_dis, 1)
                    with nc.allow_non_contiguous_dma(reason="one value of every node or edge"):
                        sp.dma_start(DIS_D.rearrange("(t p) o -> p (t o)", p=P), dis[:, :]).then_inc(s_end, 16)
                        sp.wait_ge(s_scat, 16 * 2 * ET)
                        for k, table in enumerate((by_src, by_dst)):
                            sp.dma_start(sorted_key[k], table[:, 0:1]).then_inc(s_end, 16)
                    sp.wait_ge(s_b2in, 48)
                    sp.wait_ge(s_end, 48)

                @block.gpsimd
                def _(pool):
                    nc.gpsimd.memset(tri[:, :], 1.0).then_inc(s_const, 1)
                    nc.gpsimd.memset(e127[:, :], 0.0).then_inc(s_const, 1)
                    nc.gpsimd.iota(iota[:, :], [[1, P]], base=0, channel_multiplier=0,
                                   allow_small_or_imprecise_dtypes=True).then_inc(s_const, 1)
                    nc.gpsimd.memset(zero[:, :], 0.0).then_inc(s_const, 1)
                    nc.gpsimd.memset(wmax[:, :], 0.0).then_inc(s_const, 1)
                    pool.wait_ge(s_const, 5)
                    nc.gpsimd.affine_select(tri[:, :], tri[:, :], [[-1, P]], ALU.is_gt, 0.0, base=0,
                                            channel_multiplier=1).then_inc(s_const, 1)
                    nc.gpsimd.affine_select(e127[:, :], e127[:, :], [[0, 1]], ALU.not_equal, 1.0, base=-(P - 1),
                                            channel_multiplier=1).then_inc(s_const, 1)
                    pool.wait_ge(s_wmax, 1)
                    nc.gpsimd.partition_all_reduce(wmax[:, :], wmax[:, :], P, RMAX).then_inc(s_wall, 1)
                    pool.wait_ge(s_pos, 1)
                    for k, (table, rec) in enumerate(((by_src, col), (by_dst, pair))):
                        for t in range(ET):
                            nc.gpsimd.indirect_dma_start(
                                table, bass.IndirectOffsetOnAxis(ap=pos[k][:, t:t + 1], axis=0),
                                rec[:, t, :], None).then_inc(s_scat, 16)
                    pool.wait_ge(s_scat, 16 * 2 * ET)

                @block.tensor
                def _(pe):
                    def down(b, s, count):
                        pe.wait_ge(s_xt[s], count)
                        pe.wait_ge(s_xde, LEAD + b * 2 - 2)
                        for m in range(2):
                            for k in range(KT):
                                last = nc.tensor.matmul(p_xd[:, s, m, :], wd[:, k, m * P:(m + 1) * P],
                                                        xt[:, s, k, :], start=(k == 0), stop=(k == KT - 1))
                            last.then_inc(s_xd, 1)

                    pe.wait_ge(s_wf, 1)
                    for k in range(KT):
                        last = nc.tensor.matmul(p_lr[:, 0, 0:HID], mean_of[:, :], wd[:, k, :], start=(k == 0),
                                                stop=(k == KT - 1))
                    last.then_inc(s_mean, 1)
                    pe.wait_ge(s_const, 7)
                    nc.tensor.matmul(hist[:, :], zero[:, :], zero[:, 0:NT], start=True, stop=False)
                    pe.wait_ge(s_wc, 1)
                    down(0, 0, 16)

                    def part(i, s, sorts, hots, more):
                        b = i * 2 + s
                        if more:
                            down(b + 1, 1 - s, (i + s) * 16 + 16)
                        pe.wait_ge(s_xde, LEAD + b * 2 + 2)
                        for j in range(TPB):
                            pe.wait_ge(s_lre, LEAD + b * TPB + j - 1)
                            for m in range(2):
                                last = nc.tensor.matmul(p_lr[:, j % 2, :], xdT[:, s, m, j * P:(j + 1) * P],
                                                        wlr[:, m, :], start=(m == 0), stop=(m == 1))
                            last.then_inc(s_lr, 1)
                        for u in range(hots):
                            pe.wait_ge(s_hot, (b - SORT_BLOCKS) * HOT_PER + u + 1)
                            nc.tensor.matmul(hist[:, :], one_lo[:, u, :], one_hi[:, u, :], start=False,
                                             stop=False).then_inc(s_hist, 1)
                    run(pe, part)
                    nc.tensor.matmul(hist[:, :], zero[:, :], zero[:, 0:NT], start=False, stop=True).then_inc(s_hist, 1)

                @block.scalar
                def _(act):
                    def sign(t):
                        act.wait_ge(s_shift, LEAD + t)
                        nc.scalar.activation(junk_act, key[1][:, :], ACT.Sign, bias=col[:, bass.ds(t, 1), 1:2].rearrange(
                            "p a b -> p (a b)"), scale=-1.0, accum_out=count[1][:, bass.ds(t, 1)]).then_inc(s_sign, 1)

                    def copy_xd(b, s):
                        for m in range(2):
                            act.wait_ge(s_xd, LEAD + b * 2 + m + 1)
                            act.wait_ge(s_lr, LEAD + b * TPB - TPB)
                            nc.scalar.activation(xdT[:, s, m, :], p_xd[:, s, m, :], ACT.Copy).then_inc(s_xde, 1)
                        act.sem_inc(s_xt_free, 1)

                    act.wait_ge(s_key, 1)
                    for t in range(SORT_FIRST):
                        sign(t)
                    copy_xd(0, 0)

                    def part(i, s, sorts, hots, more):
                        b = i * 2 + s
                        if sorts:
                            sign(b * SORT_PER + SORT_FIRST)
                        act.wait_ge(s_var, b + 1)
                        nc.scalar.activation(small[:, s, 1, :], small[:, s, 0, :], ACT.Sqrt).then_inc(s_sd, 1)
                        if sorts:
                            sign(b * SORT_PER + SORT_FIRST + 1)
                        if more:
                            copy_xd(b + 1, 1 - s)
                        act.wait_ge(s_r, b + 1)
                        act.wait_ge(s_lrfree[s], LEAD + i * 16)
                        for j in range(TPB):
                            act.wait_ge(s_lr, LEAD + b * TPB + j + 1)
                            nc.scalar.activation(lr[:, s, j, :], p_lr[:, j % 2, :], ACT.Copy,
                                                 scale=small[:, s, 2, j:j + 1]).then_inc(s_lre, 1)
                            if sorts and j == 1:
                                sign(b * SORT_PER + SORT_FIRST + 2)
                        act.wait_ge(s_lre, LEAD + b * TPB + TPB)
                        act.dma_start(rows(T, i, s, 2 * HID), lr[:, s]).then_inc(s_lrfree[s], 16)
                    run(act, part)
                    act.wait_ge(s_deg, 1)
                    nc.scalar.activation(deg[:, 1, :], deg[:, 0, :], ACT.Sqrt).then_inc(s_dsd, 1)
                    for s in range(2):
                        act.wait_ge(s_lrfree[s], LEAD + NB // 2 * 16)

                @block.vector
                def _(dve):
                    ch = Chain(dve, s_chain)
                    nc.vector.memset(mean_of[:, :], 1.0 / D)
                    dve.wait_ge(s_pw, 64)
                    for k in range(KT):
                        last = nc.vector.tensor_scalar(wd[:, k, :], wd[:, k, :], rms[:, k:k + 1], None, ALU.mult)
                    ch.link(last)
                    dve.sem_inc(s_wf, 1)
                    dve.wait_ge(loaded[0], 32)
                    ch.link(nc.vector.tensor_scalar(key[0][:, :], scratch[:, :], 0.25, None, ALU.add))
                    dve.sem_inc(s_conv, 1)
                    dve.wait_ge(s_mean, 1)
                    for k in range(KT):
                        last = nc.vector.tensor_tensor(wd[:, k, :], wd[:, k, :], p_lr[:, 0, 0:HID], ALU.subtract)
                    ch.link(last)
                    dve.sem_inc(s_wc, 1)
                    dve.wait_ge(loaded[1], 32)
                    ch.link(nc.vector.tensor_scalar(key[1][:, :], scratch[:, :], 0.25, None, ALU.add))
                    for k in range(2):
                        ch.link(nc.vector.tensor_copy(col[:, :, k], col_int[k][:, :]))
                        ch.link(nc.vector.tensor_copy(pair[:, :, 1 - k], col_int[k][:, :]))
                        ch.link(nc.vector.tensor_scalar(colq[k][:, :], col_int[k][:, :], 0.25, None, ALU.add))
                    dve.wait_ge(s_const, 7)
                    dve.sem_inc(s_key, 1)
                    ch.link(nc.vector.tensor_scalar(lo_int[:, :], col_int[0][:, :], P - 1, None, ALU.bitwise_and))
                    ch.link(nc.vector.tensor_scalar(hi_int[:, :], col_int[0][:, :], 7, None, ALU.arith_shift_right))
                    ch.link(nc.vector.tensor_copy(lo[:, :], lo_int[:, :]))
                    ch.link(nc.vector.tensor_copy(hi[:, :], hi_int[:, :]))
                    dve.sem_inc(s_xb_free, 2)
                    dve.wait_ge(s_w, 16 * 5)
                    ch.link(nc.vector.tensor_reduce(wmax[:, 0:1], w1[:, :, :], AX.XY, ALU.max, apply_absolute_value=True))
                    nc.vector.tensor_reduce(wmax[0:FFN1, 1:2], w2[:, :], AX.X, ALU.max,
                                            apply_absolute_value=True).then_inc(s_wmax, 1)
                    SORT_STEPS = 5
                    STEPS = 8
                    base = ch.n

                    def rank(t, ch):
                        c1 = bass.ds(t, 1)
                        here = bass.ds(t * P, P)
                        n = ch.n
                        ch.link(nc.vector.tensor_scalar(junk, key[0][:, :], col[:, c1, 0:1].rearrange(
                            "p a b -> p (a b)"), None, ALU.is_lt, ALU.add, accum_out=count[0][:, c1]))
                        for k in range(2):
                            ch.link(nc.vector.scalar_tensor_tensor(
                                junk_diag[:, :], key[k][:, here], colq[k][:, c1], tri[:, :], ALU.is_equal,
                                ALU.mult, accum_out=ties[k][:, c1]))
                        ch.link(nc.vector.tensor_scalar(key[0][:, here], key[0][:, here], -0.5, None, ALU.add))
                        dve.wait_ge(s_sign, t + 1)
                        ch.link(nc.vector.tensor_scalar(key[1][:, here], key[1][:, here], -0.5, None, ALU.add))
                        dve.sem_inc(s_shift, 1)
                        assert ch.n == n + SORT_STEPS

                    for t in range(SORT_FIRST):
                        rank(t, ch)
                    base += SORT_FIRST * SORT_STEPS
                    per_sort = STEPS + SORT_PER * SORT_STEPS

                    def finish_ranks(ch):
                        ch.link(nc.vector.tensor_scalar(count[1][:, :], count[1][:, :], float(EP), 0.5, ALU.add,
                                                        ALU.mult))
                        for k in range(2):
                            ch.link(nc.vector.tensor_tensor(ties[k][:, :], ties[k][:, :], count[k][:, :], ALU.add))
                            ch.link(nc.vector.tensor_copy(pos[k][:, :], ties[k][:, :]))
                        dve.sem_inc(s_pos, 1)
                        ch.link(nc.vector.tensor_copy(identb[:, :], ident[:, :]))
                        dve.wait_ge(s_wall, 1)
                        ch.link(nc.vector.tensor_scalar(scal[:, 0:2], wmax[:, :], MIN_RANGE, 1.0 / QP, ALU.max, ALU.mult))
                        ch.link(nc.vector.reciprocal(scal[:, 2:4], scal[:, 0:2]))
                        ch.link(nc.vector.tensor_scalar(w1[:, :, :], w1[:, :, :], scal[:, 2:3], MAGIC, ALU.mult, ALU.add))
                        ch.link(nc.vector.tensor_scalar(w1q[:, :, :], w1[:, :, :], -MAGIC, None, ALU.add))
                        ch.link(nc.vector.tensor_scalar(w2[:, :], w2[:, :], scal[0:FFN1, 3:4], MAGIC, ALU.mult, ALU.add))
                        ch.link(nc.vector.tensor_scalar(w2q[0:FFN1, :], w2[:, :], -MAGIC, None, ALU.add))
                        for k in range(3):
                            ch.link(nc.vector.tensor_copy(b2p[:, k, :], b2r[:, k % 2, :]))
                            if k < 2:
                                ch.link(nc.vector.tensor_tensor(b2r[:, (k + 1) % 2, :], b2r[:, k % 2, :],
                                                                b2p[:, k, :], ALU.subtract))
                        dve.sem_inc(s_b2, 1)

                    FINISH = 5 + 7 + 5
                    after = base + SORT_BLOCKS * per_sort + FINISH

                    def part(i, s, sorts, hots, more):
                        b = i * 2 + s
                        if sorts:
                            ch = Chain(dve, s_chain, b * per_sort + base)
                        else:
                            ch = Chain(dve, s_chain, (b - SORT_BLOCKS) * STEPS + after)
                        dve.wait_ge(s_xb[s], i * 16 + 16)
                        for j in range(TPB):
                            for h in range(2):
                                last = nc.vector.bn_stats(st[:, j, h, :], xb[:, s, j, h * 512:(h + 1) * 512])
                        ch.link(last)
                        dve.sem_inc(s_xb_free, 1)
                        dve.wait_ge(s_lre, LEAD + b * TPB - TPB)
                        nc.vector.memset(small[:, s, 3, :], 0.0)
                        for j in range(TPB):
                            last = nc.vector.bn_aggr(mv[:, j, :], st[:, j])
                        ch.link(last)
                        ch.link(nc.vector.tensor_scalar(small[:, s, 0, :], mv[:, :, 1], 1.0 + RMS_EPS,
                                                        LN_EPS * RMS_EPS, ALU.mult, ALU.add))
                        dve.sem_inc(s_var, 1)
                        if sorts:
                            rank(b * SORT_PER + SORT_FIRST, ch)
                        dve.wait_ge(s_sd, b + 1)
                        rsqrt_rest(nc, ch, small[:, s, 0, :], small[:, s, 1, :], small[:, s, 2, :],
                                   small[:, s, 3, :])
                        dve.sem_inc(s_r, 1)
                        for u in range(1, sorts):
                            rank(b * SORT_PER + SORT_FIRST + u, ch)
                        if hots:
                            dve.wait_ge(s_hist, LEAD + (b - SORT_BLOCKS) * HOT_PER)
                            for u in range(hots):
                                c1 = bass.ds((b - SORT_BLOCKS) * HOT_PER + u, 1)
                                nc.vector.tensor_scalar(one_lo[:, u, :], iota[:, :], lo[:, c1], None, ALU.is_equal)
                                nc.vector.tensor_scalar(one_hi[:, u, :], iota[:, 0:NT], hi[:, c1], None,
                                                        ALU.is_equal).then_inc(s_hot, 1)
                        assert ch.n == (per_sort if sorts else STEPS), ch.n

                    with dve.Fori(0, SORT_BLOCKS // 2) as i:
                        for s in range(2):
                            part(i, s, SORT_PER, 0, True)
                    ch = Chain(dve, s_chain, base + SORT_BLOCKS * per_sort)
                    finish_ranks(ch)
                    assert ch.n == FINISH, ch.n
                    with dve.Fori(SORT_BLOCKS // 2, NB // 2) as i:
                        for s in range(2):
                            part(i, s, 0, HOT_PER, True)
                    ch = Chain(dve, s_chain, after + (NB - SORT_BLOCKS) * STEPS)
                    dve.wait_ge(s_hist, LEAD + ET + 1)
                    nc.vector.tensor_scalar(deg[:, 0, :], hist[:, :], 1.0, None, ALU.add).then_inc(s_deg, 1)
                    dve.wait_ge(s_dsd, 1)
                    rsqrt_rest(nc, ch, deg[:, 0, :], deg[:, 1, :], dis[:, :], deg[:, 2, :])
                    dve.sem_inc(s_dis, 1)

        with ExitStack() as ctx:
            attend(nc, maker(ctx), T, T_half, by_dst, sorted_key[1], att, ident, e127, s_gat, s_sct)

        clear_used()

        with ExitStack() as node_ctx:
            sbn, _, _ = maker(node_ctx)
            mean1 = sbn("mean1", [P, NT])
            r1 = sbn("r1", [P, NT])
            far1 = sbn("far1", [P, 2, NT])
            hT = sbn("hT", [FFN1, NP])
            hmax = sbn("hmax", [P, NB])
            whi = sbn("whi", [P, KT, D], FP16)
            wlo = sbn("wlo", [P, KT, D], FP16)
            gscale = sbn("gscale", [P, 2])
            with ExitStack() as ctx:
                mix(nc, maker(ctx), T, x, X1, W_up, gcnT, whi, wlo, gscale, ident, mean1, r1, far1)
            with ExitStack() as ctx:
                quant1(nc, maker(ctx), X1, identb, w1q, b1c, scal, mean1, r1, far1, hT, hmax)
            with ExitStack() as ctx:
                conv(nc, maker(ctx), rows, X1, X3, HP, gcn_b, whi, wlo, gscale, w2q, ident, dis, scal, hT, hmax,
                     by, by_src, sorted_key[0], DIS_D, s_de, e127)
        with ExitStack() as ctx:
            edges(nc, maker(ctx), s_ge, s_sce, X3, HP, sorted_key[0], by)
        with ExitStack() as ctx:
            gated(nc, maker(ctx), X3, w_gateT, w_upT, w_downT, ident, out)


def attend(nc, made, T, T_half, by_dst, sorted_dst, att, ident, e127, s_g, s_sct):
    sb, ps, sem = made
    SLOTS = len(s_g)
    NE = ET // 2
    W = HID + HEADS
    XS = sb("XS", [P, ET, W])
    XLD = sb("XLD", [P, ET, HID])
    R = sb("R", [P, SLOTS, 2, 2 * HID])
    KB = sb("KB", [P, EP])
    a_row = sb("a_row", [P, HID])
    lg = [sb(f"lg{k}", [HEADS, EP]) for k in range(2)]
    step = sb("step", [HEADS, EP + 1], BF16)
    cols = sb("cols", [P, 4, ET])
    prev = sb("prev", [P, 1 + ET])
    idx = sb("idx", [P, 3, ET], I32)
    msg = sb("msg", [P, 2, 2, HID])
    lgc = sb("lgc", [P, SLOTS, 2, 2, HEADS])
    LC = sb("LC", [P, ET, 2, HEADS])
    PX = sb("PX", [P, ET, 2, HEADS])
    peak = sb("peak", [P, ET, HEADS])
    selfden = sb("selfden", [P, ET, HEADS])
    den = sb("den", [P, 2, 2, HEADS])
    SM = sb("SM", [P, 2, 2, 2, P])
    OS = sb("OS", [P, 2, W])
    p_lg = ps("p_lg", [HEADS, 2, 4, P])
    p_w = ps("p_w", [P, 2, 512])
    p_o = ps("p_o", [P, 4, 512])
    s_in = sem("edge_ends_loaded")
    s_in2 = sem("targets_loaded")
    s_chain = sem("attend_chain")
    s_idx = sem("attend_indices")
    s_add = sem("messages_ready")
    s_xc = sem("target_rows_kept")
    s_lgc = sem("logits_ready")
    s_lgt = sem("logits_turned")
    s_lge = sem("logits_copied")
    s_dif = sem("shifted_logits")
    s_exp = sem("exps_ready")
    s_sc = sem("scans_ready")
    s_pt = sem("peaks_turned")
    s_v = sem("weighted_rows")
    s_o = sem("sums_in_psum")
    s_oe = sem("sums_copied")
    s_res = sem("rows_ready")

    def tiles(ap, q):
        return ap[:, bass.ds(q * 2, 2)]

    def heads(ap):
        return ap.rearrange("p a (h c) -> p a h c", h=HEADS)

    def to_heads(ap):
        return ap.unsqueeze(3).broadcast_to([P, 2, HEADS, HD])

    with nc.Block() as block:
        @block.sync
        def _(sp):
            for s in (s_lge, s_oe, s_res, s_o):
                sp.sem_inc(s, LEAD)
            with nc.allow_non_contiguous_dma(reason="one value of every edge"):
                sp.dma_start(cols[:, 0, :], sorted_dst.rearrange("(t p) o -> p (t o)", p=P)).then_inc(s_in, 16)
                sp.dma_start(cols[:, 1, :], by_dst.rearrange("(t p) o -> p t o", p=P)[:, :, 1]).then_inc(s_in, 16)
                sp.dma_start(a_row[:, :], att.partition_broadcast(P)).then_inc(s_in2, 16)
                sp.dma_start(KB[:, :], sorted_dst[:, 0].partition_broadcast(P)).then_inc(s_in2, 16)
                sp.dma_start(cols[:, 2, 0:ET - 1], sorted_dst[1:EP - P + 1].rearrange(
                    "(t p) o -> p (t o)", p=P)).then_inc(s_in2, 16)
                sp.dma_start(cols[0:P - 1, 2, ET - 1:ET], sorted_dst[EP - P + 1:EP]).then_inc(s_in2, 16)
                sp.dma_start(cols[P - 1:P, 2, ET - 1:ET], sorted_dst[0:1]).then_inc(s_in2, 16)

        @block.gpsimd
        def _(pool):
            pool.wait_ge(s_idx, 1)
            for q in range(NE):
                r = q % SLOTS
                if q >= SLOTS:
                    pool.wait_ge(s_add, q - SLOTS + 1)
                    pool.wait_ge(s_xc, q - SLOTS + 1)
                for u in range(2):
                    t = q * 2 + u
                    nc.gpsimd.indirect_dma_start(XS[:, t, 0:HID], None, T_half, bass.IndirectOffsetOnAxis(
                        ap=idx[:, 1, t:t + 1], axis=0)).then_inc(s_g[r], 16)
                    nc.gpsimd.indirect_dma_start(R[:, r, u, :], None, T, bass.IndirectOffsetOnAxis(
                        ap=idx[:, 0, t:t + 1], axis=0)).then_inc(s_g[r], 16)
            for t in range(ET):
                if t % 2 == 0:
                    pool.wait_ge(s_res, LEAD + t // 2 + 1)
                nc.gpsimd.indirect_dma_start(
                    T_half, bass.IndirectOffsetOnAxis(ap=idx[:, 2, t:t + 1], axis=0),
                    XLD[:, t, :], None, bounds_check=2 * NP - 1, oob_is_err=False).then_inc(s_sct, 16)
            pool.wait_ge(s_sct, 16 * ET)

        @block.scalar
        def _(act):
            with act.Fori(0, NE // SLOTS) as i:
                for r in range(SLOTS):
                    q = i * SLOTS + r
                    act.wait_ge(s_g[r], i * 64 + 64)
                    nc.scalar.activation(tiles(XLD, q), R[:, r, :, 0:HID], ACT.Copy).then_inc(s_xc, 1)
                    act.wait_ge(s_lgc, q + 1)
                    nc.scalar.activation(tiles(LC, q), lgc[:, r], ACT.Copy)
                    act.wait_ge(s_lgt, q + 1)
                    nc.scalar.activation(lg[0][:, bass.ds(q * 2 * P, 2 * P)],
                                         p_lg[:, r % 2, 0:2, :].rearrange("h a e -> h (a e)"), ACT.Copy).then_inc(s_lge, 1)
            act.wait_ge(s_dif, 1)
            nc.scalar.activation(PX[:, :, :, :], LC[:, :, :, :], ACT.Exp).then_inc(s_exp, 1)
            with act.Fori(0, NE // 2) as i:
                for s in range(4):
                    t = i * 4 + s
                    act.wait_ge(s_o, LEAD + t + 1)
                    nc.scalar.activation(OS[:, s % 2, :], p_o[:, s, 0:W], ACT.Copy).then_inc(s_oe, 1)

        @block.vector
        def _(dve):
            ch = Chain(dve, s_chain)
            dve.wait_ge(s_in, 32)
            nc.vector.tensor_copy(idx[:, 0, :], cols[:, 0, :])
            ch.link(nc.vector.tensor_scalar(idx[:, 1, :], cols[:, 1, :], 2.0, None, ALU.mult))
            dve.sem_inc(s_idx, 1)
            ch.link(nc.vector.memset(prev[:, 0:1], 0.0))
            ch.link(nc.vector.tensor_scalar(prev[:, 1:1 + ET], cols[:, 0, :], 1.0, None, ALU.add))
            ch.link(nc.vector.tensor_scalar(prev[:, :], prev[:, :], e127[:, 0:1], -1.0, ALU.mult, ALU.add))
            ch.link(nc.vector.memset(OS[:, :, :], 0.0))
            dve.wait_ge(s_in2, 16 * 5)
            ch.link(nc.vector.tensor_tensor(cols[:, 3, :], cols[:, 0, :], cols[:, 2, :], ALU.is_equal))
            ch.link(nc.vector.tensor_scalar(cols[:, 3, :], cols[:, 3, :], SKIP, None, ALU.mult))
            ch.link(nc.vector.tensor_tensor(cols[:, 3, :], cols[:, 3, :], cols[:, 0, :], ALU.add))
            ch.link(nc.vector.tensor_scalar(idx[:, 2, :], cols[:, 3, :], 2.0, None, ALU.mult))
            ch.link(nc.vector.memset(step[:, :], 0.0))
            ch.link(nc.vector.tensor_tensor(step[:, 1:EP], KB[0:HEADS, 1:EP], KB[0:HEADS, 0:EP - 1], ALU.is_equal))
            ch.link(nc.vector.tensor_scalar(step[:, :], step[:, :], -FAR, FAR, ALU.mult, ALU.add))
            base = ch.n
            STEPS = 4
            with dve.Fori(0, NE // SLOTS) as i:
                for r in range(SLOTS):
                    q = i * SLOTS + r
                    ch = Chain(dve, s_chain, q * STEPS + base)
                    dve.wait_ge(s_g[r], i * 64 + 64)
                    nc.vector.tensor_tensor(msg[:, :, 0, :], tiles(XS, q)[:, :, 0:HID], R[:, r, :, HID:2 * HID],
                                            ALU.add)
                    ch.link(nc.vector.tensor_tensor(msg[:, :, 1, :], R[:, r, :, 0:HID], R[:, r, :, HID:2 * HID],
                                                    ALU.add))
                    dve.sem_inc(s_add, 1)
                    ch.link(nc.vector.scalar_tensor_tensor(msg[:, :, :, :], msg[:, :, :, :], SLOPE, msg[:, :, :, :],
                                                           ALU.mult, ALU.max))
                    ch.link(nc.vector.tensor_tensor(
                        msg[:, :, :, :].rearrange("p a k c -> p (a k) c"),
                        msg[:, :, :, :].rearrange("p a k c -> p (a k) c"),
                        a_row[:, None, :].broadcast_to([P, 4, HID]), ALU.mult))
                    dve.wait_ge(s_lge, LEAD + q - SLOTS + 1)
                    ch.link(nc.vector.tensor_reduce(
                        lgc[:, r].rearrange("p a k h -> p (a k h)"),
                        msg[:, :, :, :].rearrange("p a k (h c) -> p (a k h) c", c=HD), AX.X, ALU.add))
                    dve.sem_inc(s_lgc, 1)
            ch = Chain(dve, s_chain, base + STEPS * NE)
            dve.wait_ge(s_lge, LEAD + NE)
            ch.link(nc.vector.tensor_tensor_scan(lg[1][:, :], step[:, 0:EP], lg[0][:, :], FAR, ALU.add, ALU.max))
            dve.sem_inc(s_sc, 1)
            nc.vector.tensor_tensor_scan(lg[0][:, ::-1], step[:, 1:EP + 1][:, ::-1], lg[0][:, ::-1],
                                         FAR, ALU.add, ALU.max).then_inc(s_sc, 1)
            dve.wait_ge(s_pt, 2)

            def turned(k):
                return p_w[:, k, 0:ET * HEADS].rearrange("p (t h) -> p t h", h=HEADS)

            ch.link(nc.vector.tensor_copy(peak[:, :, :], turned(0)))
            ch.link(nc.vector.tensor_tensor(peak[:, :, :], peak[:, :, :], turned(1), ALU.max))
            ch.link(nc.vector.tensor_tensor(peak[:, :, :], peak[:, :, :], LC[:, :, 1, :], ALU.max))
            for k in range(2):
                last = nc.vector.tensor_tensor(LC[:, :, k, :], LC[:, :, k, :], peak[:, :, :], ALU.subtract)
            last.then_inc(s_dif, 1)
            dve.wait_ge(s_exp, 1)
            nc.vector.tensor_copy(XS[:, :, HID:W], PX[:, :, 0, :])
            ch.link(nc.vector.tensor_scalar(selfden[:, :, :], PX[:, :, 1, :], DEN_EPS, None, ALU.add))

            def front(q, s):
                xs = heads(tiles(XS, q)[:, :, 0:HID])
                xld = heads(tiles(XLD, q))
                nc.vector.tensor_tensor(xs, xs, to_heads(tiles(PX, q)[:, :, 0, :]), ALU.mult)
                kb = KB[:, bass.ds(q * 2 * P, 2 * P)].rearrange("p (a e) -> p a e", a=2)
                dve.wait_ge(s_o, LEAD + q * 2 - 2)
                nc.vector.tensor_tensor(SM[:, s, 0], kb, cols[:, 0, bass.ds(q * 2, 2)].unsqueeze(2).broadcast_to(
                    [P, 2, P]), ALU.is_equal)
                nc.vector.tensor_tensor(SM[:, s, 1], kb, prev[:, bass.ds(q * 2, 2)].unsqueeze(2).broadcast_to(
                    [P, 2, P]), ALU.is_equal).then_inc(s_v, 1)
                nc.vector.tensor_tensor(xld, xld, to_heads(tiles(PX, q)[:, :, 1, :]), ALU.mult)

            STEPS2 = 2
            base2 = base + STEPS * NE + ch.n

            def back(q, s):
                ch = Chain(dve, s_chain, q * STEPS2 + base2)
                xld = heads(tiles(XLD, q))
                sums = p_o[:, 2 * s:2 * s + 2, 0:HID]
                dve.wait_ge(s_oe, LEAD + q * 2 + 2)
                nc.vector.tensor_tensor(den[:, s], tiles(selfden, q), p_o[:, 2 * s:2 * s + 2, HID:W], ALU.add)
                ch.link(nc.vector.tensor_tensor(tiles(XLD, q), tiles(XLD, q), sums, ALU.add))
                ch.link(nc.vector.reciprocal(den[:, s], den[:, s]))
                nc.vector.tensor_tensor(xld, xld, to_heads(den[:, s]), ALU.mult).then_inc(s_res, 1)

            front(0, 0)
            with dve.Fori(0, NE // 2 - 1) as i:
                for s in range(2):
                    front(i * 2 + s + 1, 1 - s)
                    back(i * 2 + s, s)
            front(NE - 1, 1)
            back(NE - 2, 0)
            back(NE - 1, 1)

        @block.tensor
        def _(pe):
            with pe.Fori(0, NE // SLOTS) as i:
                for r in range(SLOTS):
                    q = i * SLOTS + r
                    pe.wait_ge(s_lgc, q + 1)
                    pe.wait_ge(s_lge, LEAD + q - 1)
                    for u in range(2):
                        last = nc.tensor.transpose(p_lg[:, r % 2, u, :], lgc[:, r, u, 0, :], ident[:, :])
                    last.then_inc(s_lgt, 1)
            for k in range(2):
                pe.wait_ge(s_sc, k + 1)
                for t in range(ET):
                    last = nc.tensor.transpose(p_w[:, k, t * HEADS:(t + 1) * HEADS],
                                               lg[1 - k][:, t * P:(t + 1) * P], ident[0:HEADS, 0:HEADS])
                last.then_inc(s_pt, 1)

            def within(t, s):
                nc.tensor.matmul(p_o[:, s, 0:W], SM[:, s // 2, 0, s % 2, :],
                                 XS[:, bass.ds(t, 1), :].rearrange("p o c -> p (o c)"), start=True, stop=False)

            def carry(t, s):
                pe.wait_ge(s_oe, LEAD + t)
                nc.tensor.matmul(p_o[:, s, 0:W], SM[:, s // 2, 1, s % 2, :], OS[:, 1 - s % 2, :],
                                 start=False, stop=True).then_inc(s_o, 1)

            def part(q, s, more):
                for u in range(2):
                    carry(q * 2 + u, 2 * s + u)
                    if more:
                        if u == 0:
                            pe.wait_ge(s_v, q + 2)
                            pe.wait_ge(s_res, LEAD + q)
                        within(q * 2 + 2 + u, 2 - 2 * s + u)

            pe.wait_ge(s_v, 1)
            within(0, 0)
            within(1, 1)
            with pe.Fori(0, NE // 2 - 1) as i:
                for s in range(2):
                    part(i * 2 + s, s, True)
            part(NE - 2, 0, True)
            part(NE - 1, 1, False)


def block_stats(nc, ch, xs, st, mv, small, s_var, s_sd, want, dve, x_ready=None):
    for j in range(TPB):
        if x_ready is not None:
            dve.wait_ge(*x_ready(j))
        for h in range(2):
            last = nc.vector.bn_stats(st[:, j, h, :], xs[:, j, h * 512:(h + 1) * 512])
    ch.link(last)
    nc.vector.memset(small[:, 4, :], 0.0)
    for j in range(TPB):
        last = nc.vector.bn_aggr(mv[:, j, :], st[:, j])
    ch.link(last)
    ch.link(nc.vector.tensor_scalar(small[:, 0, :], mv[:, :, 1], LN_EPS, None, ALU.add))
    dve.sem_inc(s_var, 1)
    ch.link(nc.vector.tensor_scalar(small[:, 3, :], mv[:, :, 0], -1.0, None, ALU.mult))
    dve.wait_ge(s_sd, want)
    rsqrt_rest(nc, ch, small[:, 0, :], small[:, 1, :], small[:, 2, :], small[:, 4, :])


STAT_STEPS = 9


def run_blocks(eng, part, slots, first=0):
    for b in range(first * slots):
        part(b, b % slots, slots)
    with eng.Fori(first, NB // slots - 1) as i:
        for s in range(slots):
            part(i * slots + s, s, slots)
    for s in range(slots):
        part(NB - slots + s, s, slots - 1 - s)


def block_rows(ap, b, width):
    return ap[bass.ds(b * BLK, BLK), 0:width].rearrange("(j p) d -> p j d", p=P)


def mix(nc, made, T, x, X1, W_up, gcnT, whi, wlo, gscale, ident, mean1, r1, far1):
    sb, ps, sem = made
    wu = sb("wu", [P, 2, D])
    wst = sb("wst", [P, KT, D])
    wtop = sb("wtop", [P, 1])
    g = sb("g", [P, 2, TPB, HID])
    gT = sb("gT", [P, 2, 2, BLK])
    xb = sb("xb_mix", [P, 2, TPB, D])
    x1 = sb("x1_mix", [P, 2, TPB, D])
    st = sb("st_mix", [P, TPB, 2, 6])
    mv = sb("mv_mix", [P, TPB, 2])
    small = sb("small_mix", [P, 4, TPB])
    most = sb("most_mix", [P, TPB])
    least = sb("least_mix", [P, TPB])
    carry = sb("carry_mix", [P, TPB])
    p_t = ps("p_t_mix", [P, 2, BLK])
    p_x = ps("p_x_mix", [P, 2, D])
    s_w = sem("mix_weights")
    s_gw = sem("gcn_weights")
    s_gtop = sem("gcn_top")
    s_gall = sem("gcn_top_all")
    s_gsc = sem("gcn_scale_steps")
    s_pool = sem("gcn_split")
    s_chain = sem("mix_chain")
    s_g = [sem(f"g_loaded{s}") for s in range(2)]
    s_x = [sem(f"mix_x_loaded{s}") for s in range(2)]
    s_x_free = sem("mix_x_used")
    s_t = sem("g_turned")
    s_te = sem("g_copied")
    s_p = sem("update_in_psum")
    s_x1 = sem("x1_ready")
    s_var = sem("mix_var")
    s_sd = sem("mix_sd")
    s_out = [sem(f"x1_stored{s}") for s in range(2)]
    leads = (s_te, s_x1, s_t, s_p, *s_out)
    with nc.Block() as block:
        @block.sync
        def _(sp):
            for s in leads:
                sp.sem_inc(s, LEAD)
            sp.dma_start(g[:, 0], block_rows(T, 0, HID)).then_inc(s_g[0], 16)
            sp.dma_start(wu[:, :, :], W_up.rearrange("(k p) n -> p k n", p=P)).then_inc(s_w, 16)

            def part(b, s, left):
                if left:
                    sp.wait_ge(s_t, LEAD + b * 2)
                    sp.dma_start(g[:, 1 - s], block_rows(T, b + 1, HID)).then_inc(s_g[1 - s], 16)
                sp.wait_ge(s_x_free, b + 1)
                sp.dma_start(xb[:, s], block_rows(x, b, D)).then_inc(s_x[s], 16)

            run_blocks(sp, part, 2)

        @block.gpsimd
        def _(pool):
            pool.dma_start(wst[:, :, :], gcnT.rearrange("(k p) n -> p k n", p=P)).then_inc(s_gw, 16)
            pool.wait_ge(s_gtop, 1)
            nc.gpsimd.partition_all_reduce(wtop[:, :], wtop[:, :], P, RMAX).then_inc(s_gall, 1)
            pool.wait_ge(s_gsc, 3)
            for k in range(KT):
                nc.gpsimd.tensor_scalar(wst[:, k, :], wst[:, k, :], gscale[:, 0:1], 1.0, ALU.mult,
                                        ALU.mult).then_inc(s_pool, 1)
                pool.wait_ge(s_pool, 3 * k + 1)
                nc.gpsimd.tensor_copy(whi[:, k, :], wst[:, k, :]).then_inc(s_pool, 1)
                pool.wait_ge(s_pool, 3 * k + 2)
                nc.gpsimd.tensor_tensor(wlo[:, k, :], wst[:, k, :], whi[:, k, :], ALU.subtract).then_inc(s_pool, 1)
            pool.wait_ge(s_pool, 3 * KT)

        @block.tensor
        def _(pe):
            def turn(b, s, loads):
                pe.wait_ge(s_g[s], loads)
                pe.wait_ge(s_te, LEAD + b * 2)
                for m in range(2):
                    for j in range(TPB):
                        last = nc.tensor.transpose(p_t[:, m, j * P:(j + 1) * P], g[:, s, j, m * P:(m + 1) * P],
                                                   ident[:, :])
                    last.then_inc(s_t, 1)

            turn(0, 0, 16)
            pe.wait_ge(s_w, 16)

            def part(b, s, left):
                pe.wait_ge(s_te, LEAD + b * 2 + 2)
                for j in range(TPB):
                    if left and j == 2:
                        turn(b + 1, 1 - s, (b + s) * 8 + 16)
                    pe.wait_ge(s_x1, LEAD + b * TPB + j - 1)
                    for h in range(2):
                        for m in range(2):
                            last = nc.tensor.matmul(p_x[:, j % 2, h * 512:(h + 1) * 512],
                                                    gT[:, s, m, j * P:(j + 1) * P],
                                                    wu[:, m, h * 512:(h + 1) * 512], start=(m == 0), stop=(m == 1))
                    last.then_inc(s_p, 1)
            run_blocks(pe, part, 2)

        @block.scalar
        def _(act):
            def copy(b, s):
                for m in range(2):
                    act.wait_ge(s_t, LEAD + b * 2 + m + 1)
                    act.wait_ge(s_p, LEAD + b * TPB - TPB)
                    nc.scalar.activation(gT[:, s, m, :], p_t[:, m, :], ACT.Copy).then_inc(s_te, 1)

            copy(0, 0)

            def part(b, s, left):
                if left:
                    copy(b + 1, 1 - s)
                act.wait_ge(s_var, b + 1)
                nc.scalar.activation(small[:, 1, :], small[:, 0, :], ACT.Sqrt).then_inc(s_sd, 1)
                act.wait_ge(s_x1, LEAD + b * TPB + TPB)
                act.dma_start(block_rows(X1, b, D), x1[:, s]).then_inc(s_out[s], 16)
            run_blocks(act, part, 2)
            for s in range(2):
                act.wait_ge(s_out[s], LEAD + NB // 2 * 16)

        @block.vector
        def _(dve):
            dve.sem_inc(s_x_free, 2)
            STEPS = STAT_STEPS + 3

            def part(b, s, left):
                ch = Chain(dve, s_chain, b * STEPS)
                dve.wait_ge(s_x[s], (b - s) * 8 + 16)
                dve.wait_ge(s_out[s], LEAD + (b - s) * 8)
                for j in range(TPB):
                    dve.wait_ge(s_p, LEAD + b * TPB + j + 1)
                    nc.vector.memset(carry[:, j:j + 1], 0.0)
                    nc.vector.tensor_tensor_reduce(out=x1[:, s, j, :], in0=p_x[:, j % 2, :], in1=xb[:, s, j, :],
                                                   scale=1.0, scalar=FAR, op0=ALU.add, op1=ALU.max,
                                                   accum_out=most[:, j:j + 1]).then_inc(s_x1, 1)
                    dve.wait_ge(s_x1, LEAD + b * TPB + j + 1)
                    for h in range(2):
                        nc.vector.bn_stats(st[:, j, h, :], x1[:, s, j, h * 512:(h + 1) * 512])
                    last = nc.vector.tensor_reduce(least[:, j:j + 1], x1[:, s, j, :], AX.X, ALU.min)
                dve.sem_inc(s_x_free, 1)
                ch.link(last)
                nc.vector.memset(small[:, 3, :], 0.0)
                for j in range(TPB):
                    last = nc.vector.bn_aggr(mv[:, j, :], st[:, j])
                ch.link(last)
                ch.link(nc.vector.tensor_scalar(small[:, 0, :], mv[:, :, 1], LN_EPS, None, ALU.add))
                dve.sem_inc(s_var, 1)
                ch.link(nc.vector.tensor_scalar(mean1[:, bass.ds(b * TPB, TPB)], mv[:, :, 0], -1.0, None, ALU.mult))
                ch.link(nc.vector.tensor_copy(far1[:, 1, bass.ds(b * TPB, TPB)], least[:, :]))
                dve.wait_ge(s_sd, b + 1)
                rsqrt_rest(nc, ch, small[:, 0, :], small[:, 1, :], small[:, 2, :], small[:, 3, :])
                ch.link(nc.vector.tensor_copy(r1[:, bass.ds(b * TPB, TPB)], small[:, 2, :]))
                ch.link(nc.vector.tensor_copy(far1[:, 0, bass.ds(b * TPB, TPB)], most[:, :]))
                assert ch.n == STEPS, ch.n
                if type(b) is int and b == 1:
                    dve.wait_ge(s_gw, 16)
                    nc.vector.tensor_reduce(wtop[:, :], wst[:, :, :], AX.XY, ALU.max,
                                            apply_absolute_value=True).then_inc(s_gtop, 1)
                    ch = Chain(dve, s_gsc)
                    dve.wait_ge(s_gall, 1)
                    ch.link(nc.vector.tensor_scalar(wtop[:, :], wtop[:, :], 1e-30, 1.0 / WMAX, ALU.max, ALU.mult))
                    ch.link(nc.vector.reciprocal(gscale[:, 0:1], wtop[:, :]))
                    ch.link(nc.vector.tensor_scalar(gscale[:, 1:2], wtop[:, :], 1.0 / YSCALE, None, ALU.mult))

            run_blocks(dve, part, 2, 1)


def quant1(nc, made, X1, identb, w1q, b1c, scal, mean1, r1, far1, hT, hmax):
    sb, ps, sem = made
    SLOTS = 4
    top = sb("top", [P, 1])
    a = sb("scale1", [P, NT])
    c = sb("shift1", [P, NT])
    xb = sb("xb_q", [P, SLOTS, TPB, D])
    y = sb("y_q", [P, 2, D])
    yq = sb("yq", [P, 2, D], BF16)
    yT = sb("yT_q", [P, 2, KT, BLK], BF16)
    p_t = ps("p_t_q", [P, 2, D], BF16)
    p_h = ps("p_h_q", [P, 2, BLK])
    s_chain = sem("quant_chain")
    s_top = sem("top_ready")
    s_topall = sem("top_all")
    s_x = [sem(f"q_x1_loaded{s}") for s in range(SLOTS)]
    s_x_free = sem("q_x1_used")
    s_y = sem("scaled")
    s_yq = sem("rounded")
    s_t = sem("q_turned")
    s_te = sem("q_copied")
    s_h = sem("h_in_psum")
    s_hg = sem("h_gelu")
    s_hmax = sem("h_max")
    leads = (s_yq, s_te, s_t, s_hg, s_h, s_x_free)
    with nc.Block() as block:
        @block.sync
        def _(sp):
            for s in leads:
                sp.sem_inc(s, LEAD)
            for s in range(SLOTS - 1):
                sp.dma_start(xb[:, s], block_rows(X1, s, D)).then_inc(s_x[s], 16)

            def part(b, s, left):
                if left >= SLOTS - 1:
                    n = (s - 1) % SLOTS
                    sp.wait_ge(s_x_free, LEAD + b)
                    sp.dma_start(xb[:, n], block_rows(X1, b + SLOTS - 1, D)).then_inc(s_x[n], 16)
            run_blocks(sp, part, SLOTS)

        @block.gpsimd
        def _(pool):
            pool.wait_ge(s_top, 1)
            nc.gpsimd.partition_all_reduce(top[:, :], top[:, :], P, RMAX).then_inc(s_topall, 1)

        @block.tensor
        def _(pe):
            def turn(b, j):
                t = b * TPB + j
                pe.wait_ge(s_yq, LEAD + t + 1)
                pe.wait_ge(s_te, LEAD + t - 1)
                for k in range(KT):
                    last = nc.tensor.transpose(p_t[:, j % 2, k * P:(k + 1) * P], yq[:, j % 2, k * P:(k + 1) * P],
                                               identb[:, :])
                last.then_inc(s_t, 1)

            for j in range(TPB):
                turn(0, j)

            def part(b, s, left):
                if left:
                    turn(b + 1, 0)
                    turn(b + 1, 1)
                pe.wait_ge(s_te, LEAD + b * TPB + TPB)
                pe.wait_ge(s_hg, LEAD + b - 1)
                for k in range(KT):
                    last = nc.tensor.matmul(p_h[0:FFN1, s % 2, :], w1q[:, k, :], yT[:, s % 2, k, :], start=(k == 0),
                                            stop=(k == KT - 1))
                last.then_inc(s_h, 1)
                if left:
                    turn(b + 1, 2)
                    turn(b + 1, 3)
            run_blocks(pe, part, SLOTS)

        @block.scalar
        def _(act):
            def copy(b, u, js):
                act.wait_ge(s_h, LEAD + b - 1)
                for j in js:
                    act.wait_ge(s_t, LEAD + b * TPB + j + 1)
                    nc.scalar.activation(yT[:, u, :, j * P:(j + 1) * P],
                                         p_t[:, j % 2, :].rearrange("p (k n) -> p k n", k=KT),
                                         ACT.Copy).then_inc(s_te, 1)

            copy(0, 0, range(TPB))

            def part(b, s, left):
                if left:
                    copy(b + 1, (s + 1) % 2, range(TPB - 1))
                act.wait_ge(s_h, LEAD + b + 1)
                nc.scalar.activation(hT[:, bass.ds(b * BLK, BLK)], p_h[0:FFN1, s % 2, :], ACT.Gelu,
                                     bias=b1c[:, 1:2], scale=scal[0:FFN1, 5:6]).then_inc(s_hg, 1)
                if left:
                    copy(b + 1, (s + 1) % 2, (TPB - 1,))
            run_blocks(act, part, SLOTS)

        @block.vector
        def _(dve):
            ch = Chain(dve, s_chain)
            ch.link(nc.vector.tensor_tensor(a[:, :], far1[:, 0, :], mean1[:, :], ALU.add))
            ch.link(nc.vector.tensor_tensor(c[:, :], far1[:, 1, :], mean1[:, :], ALU.add))
            ch.link(nc.vector.tensor_scalar(c[:, :], c[:, :], -1.0, None, ALU.mult))
            ch.link(nc.vector.tensor_tensor(a[:, :], a[:, :], c[:, :], ALU.max))
            ch.link(nc.vector.tensor_tensor(a[:, :], a[:, :], r1[:, :], ALU.mult))
            nc.vector.tensor_reduce(top[:, :], a[:, :], AX.X, ALU.max).then_inc(s_top, 1)
            dve.wait_ge(s_topall, 1)
            ch.link(nc.vector.tensor_scalar(scal[:, 4:5], top[:, :], MIN_RANGE, 1.0 / QP, ALU.max, ALU.mult))
            ch.link(nc.vector.tensor_tensor(scal[:, 5:6], scal[:, 4:5], scal[:, 0:1], ALU.mult))
            ch.link(nc.vector.reciprocal(scal[:, 6:7], scal[:, 4:5]))
            ch.link(nc.vector.tensor_tensor(b1c[:, 1:2], b1c[:, 0:1], scal[0:FFN1, 5:6], ALU.mult))
            ch.link(nc.vector.tensor_scalar(a[:, :], r1[:, :], scal[:, 6:7], None, ALU.mult))
            ch.link(nc.vector.tensor_tensor(c[:, :], a[:, :], mean1[:, :], ALU.mult))
            ch.link(nc.vector.memset(hmax[:, :], 0.0))
            base = ch.n

            def quantise(b, slot, loads, js):
                dve.wait_ge(s_x[slot], loads)
                for j in js:
                    t = b * TPB + j
                    t1 = bass.ds(t, 1)
                    ch = Chain(dve, s_chain, t + base)
                    dve.wait_ge(s_yq, LEAD + t - 1)
                    ch.link(nc.vector.tensor_scalar(y[:, j % 2, :], xb[:, slot, j, :], a[:, t1], c[:, t1], ALU.mult,
                                                    ALU.add))
                    dve.wait_ge(s_t, LEAD + t - 1)
                    nc.vector.tensor_scalar(yq[:, j % 2, :], y[:, j % 2, :], MAGIC, -MAGIC, ALU.add,
                                            ALU.add).then_inc(s_yq, 1)
                if TPB - 1 in js:
                    dve.sem_inc(s_x_free, 1)

            def largest(b):
                dve.wait_ge(s_hg, LEAD + b + 1)
                nc.vector.tensor_reduce(hmax[0:FFN1, bass.ds(b, 1)], hT[:, bass.ds(b * BLK, BLK)], AX.X, ALU.max,
                                        apply_absolute_value=True).then_inc(s_hmax, 1)

            quantise(0, 0, 16, range(TPB))

            def part(b, s, left):
                loads = (b - s) * 4 + (32 if s == SLOTS - 1 else 16)
                if left:
                    quantise(b + 1, (s + 1) % SLOTS, loads, (0, 1))
                if type(b) is not int or b > 0:
                    largest(b - 1)
                if left:
                    quantise(b + 1, (s + 1) % SLOTS, loads, (2, 3))
            run_blocks(dve, part, SLOTS, 1)
            largest(NB - 1)
            dve.wait_ge(s_hmax, NB)
            nc.vector.tensor_reduce(hmax[0:FFN1, NB - 1:NB], hT[:, (NB - 1) * BLK:N], AX.X, ALU.max,
                                    apply_absolute_value=True)


def conv(nc, made, rows, X1, X3, HP, gcn_b, whi, wlo, gscale, w2q, ident, dis, scal, hT, hmax, by, by_src,
         sorted_src, DIS_D, s_de, e127):
    sb, ps, sem = made
    brow = sb("b_gcn", [P, D])
    top = sb("top_c", [P, 1])
    hs = sb("hs", [FFN1, BLK])
    hq = sb("hq", [FFN1 + 3, 2, BLK], BF16)
    ones = sb("ones3", [3, BLK], BF16)
    xb = sb("xb_c", [P, 2, TPB, D])
    y = sb("y_c", [P, 2, D])
    yhi = sb("yhi", [P, 2, D], FP16)
    ylo = sb("ylo", [P, 2, D], FP16)
    hb = sb("hb_c", [P, TPB, D])
    st = sb("st_c", [P, TPB, 2, 6])
    mv = sb("mv_c", [P, TPB, 2])
    small = sb("small_c", [P, 2, 5, TPB])
    p_u = ps("p_u", [P, D])
    p_t = ps("p_t_c", [P, D])
    p_h = ps("p_h_c", [P, 2, D])
    s_w = sem("conv_bias")
    s_ones = sem("conv_ones")
    s_onesin = sem("conv_ones_in")
    s_chain = sem("conv_chain")
    s_top = sem("hmax_ready")
    s_topall = sem("hmax_all")
    s_x = [sem(f"c_x1_loaded{s}") for s in range(2)]
    s_x3 = [sem(f"x3_stored{s}") for s in range(2)]
    s_hp = [sem(f"h_stored{s}") for s in range(TPB)]
    s_hq = sem("hq_ready")
    s_hqc = sem("hq_scaled")
    s_u = sem("ffn_in_psum")
    s_x2 = sem("x2_ready")
    s_var = sem("c_var")
    s_sd = sem("c_sd")
    s_mean = sem("c_mean")
    s_y = sem("c_normed")
    s_t = sem("c_turned")
    s_hi = sem("c_high_ready")
    s_lo = sem("c_low_ready")
    s_h = sem("c_h_in_psum")
    s_hb = sem("c_bias_added")
    s_hd = sem("c_h_scaled")
    s_fin = sem("x3_ready")
    s_ends = sem("edge_ends")
    s_prep = sem("edge_steps")
    s_eidx = sem("edge_indices")
    leads = (s_x2, s_hq, s_hqc, s_hi, s_lo, s_hb, s_h, s_t, *s_x3, *s_hp)
    PAIRS = NB // 2
    CHAIN = STAT_STEPS + 1

    def run(eng, part):
        with eng.Fori(0, PAIRS - 1) as i:
            part(i, 0, True, True)
            part(i, 1, True, True)
        part(PAIRS - 1, 0, True, False)
        part(PAIRS - 1, 1, False, False)

    with nc.Block() as block:
        @block.sync
        def _(sp):
            for s in leads:
                sp.sem_inc(s, LEAD)
            sp.dma_start(brow[:, :], gcn_b.partition_broadcast(P)).then_inc(s_w, 16)
            sp.dma_start(xb[:, 0], rows(X1, 0, 0, D)).then_inc(s_x[0], 16)
            with nc.allow_non_contiguous_dma(reason="one value of every edge"):
                for to, frm in ((by.cols[:, 0, :], sorted_src.rearrange("(t p) o -> p (t o)", p=P)),
                                (by.cols[:, 1, :], by_src.rearrange("(t p) o -> p t o", p=P)[:, :, 1]),
                                (by.cols[:, 2, 0:ET - 1], sorted_src[1:EP - P + 1].rearrange(
                                    "(t p) o -> p (t o)", p=P)),
                                (by.cols[0:P - 1, 2, ET - 1:ET], sorted_src[EP - P + 1:EP]),
                                (by.cols[P - 1:P, 2, ET - 1:ET], sorted_src[0:1])):
                    sp.dma_start(to, frm).then_inc(s_ends, 16)
            sp.wait_ge(s_ones, 1)
            for s in range(2):
                sp.dma_start(hq[FFN1:FFN1 + 3, s, :], ones[:, :]).then_inc(s_onesin, 16)

            def part(i, s, front, _):
                b = i * 2 + s
                if front:
                    sp.wait_ge(s_x3[1 - s], LEAD + (i + s) * 16 * TPB)
                    sp.dma_start(xb[:, 1 - s], rows(X1, i + s, 1 - s, D)).then_inc(s_x[1 - s], 16)
                for j in range(TPB):
                    t = b * TPB + j
                    sp.wait_ge(s_fin, t + 1)
                    sp.dma_start(X3[bass.ds(t * P, P), :], xb[:, s, j, :]).then_inc(s_x3[s], 16)
            run(sp, part)
            for s in range(2):
                sp.wait_ge(s_x3[s], LEAD + PAIRS * 16 * TPB)

        @block.gpsimd
        def _(pool):
            nc.gpsimd.memset(ones[:, :], 1.0).then_inc(s_ones, 1)
            pool.wait_ge(s_top, 1)
            nc.gpsimd.partition_all_reduce(top[:, :], top[:, :], P, RMAX).then_inc(s_topall, 1)
            pool.wait_ge(s_eidx, 1)
            for t in range(ET):
                nc.gpsimd.indirect_dma_start(by.dis[:, t:t + 1], None, DIS_D, bass.IndirectOffsetOnAxis(
                    ap=by.idx[:, 0, t:t + 1], axis=0)).then_inc(s_de, 16)
            pool.wait_ge(s_de, 16 * ET)

        @block.tensor
        def _(pe):
            def ffn(bb, slot, j):
                pe.wait_ge(s_hq, LEAD + bb + 1)
                pe.wait_ge(s_x2, LEAD + bb * TPB + j)
                for h in range(2):
                    last = nc.tensor.matmul(p_u[:, h * 512:(h + 1) * 512], hq[:, slot, j * P:(j + 1) * P],
                                            w2q[:, h * 512:(h + 1) * 512], start=True, stop=True)
                last.then_inc(s_u, 1)

            def turn(t, u):
                pe.wait_ge(s_y, t + 1)
                pe.wait_ge(s_lo, LEAD + t)
                for k in range(KT):
                    last = nc.tensor.transpose(p_t[:, k * P:(k + 1) * P], y[:, u, k * P:(k + 1) * P], ident[:, :])
                last.then_inc(s_t, 1)

            def product(u, h):
                c = slice(h * 512, (h + 1) * 512)
                for n, (yy, ww) in enumerate(((yhi, whi), (yhi, wlo), (ylo, whi))):
                    for k in range(KT):
                        last = nc.tensor.matmul(p_h[:, u, c], yy[:, u, k * P:(k + 1) * P], ww[:, k, c],
                                                start=(n == 0 and k == 0), stop=(n == 2 and k == KT - 1))
                return last

            pe.wait_ge(s_onesin, 32)
            for j in range(TPB):
                ffn(0, 0, j)
            turn(0, 0)

            def part(i, s, front, _):
                b = i * 2 + s
                for j in range(TPB):
                    t = b * TPB + j
                    if front and j in (1, 2):
                        ffn(b + 1, 1 - s, 2 * j - 1)
                    if j < TPB - 1 or front:
                        turn(t + 1, (j + 1) % 2)
                    pe.wait_ge(s_lo, LEAD + t + 1)
                    pe.wait_ge(s_hb, LEAD + t - 1)
                    product(j % 2, 0)
                    if front and j in (0, 1):
                        ffn(b + 1, 1 - s, 2 * j)
                    product(j % 2, 1).then_inc(s_h, 1)
            run(pe, part)

        @block.scalar
        def _(act):
            def deviation(bb, slot):
                act.wait_ge(s_var, bb + 1)
                nc.scalar.activation(small[:, slot, 1, :], small[:, slot, 0, :], ACT.Sqrt).then_inc(s_sd, 1)

            def norm(bb, slot, j):
                act.wait_ge(s_mean, bb + 1)
                act.wait_ge(s_t, LEAD + bb * TPB + j - 1)
                nc.scalar.activation(y[:, j % 2, :], xb[:, slot, j, :], ACT.Identity, bias=small[:, slot, 3, j:j + 1],
                                     scale=small[:, slot, 2, j:j + 1]).then_inc(s_y, 1)

            def high(t, u):
                act.wait_ge(s_t, LEAD + t + 1)
                act.wait_ge(s_h, LEAD + t - 1)
                nc.scalar.activation(yhi[:, u, :], p_t[:, :], ACT.Copy).then_inc(s_hi, 1)

            deviation(0, 0)
            norm(0, 0, 0)
            norm(0, 0, 1)
            high(0, 0)

            def part(i, s, front, _):
                b = i * 2 + s
                for j in range(TPB):
                    t = b * TPB + j
                    if j < TPB - 1 or front:
                        high(t + 1, (j + 1) % 2)
                    if j < 2:
                        norm(b, s, j + 2)
                    elif front:
                        if j == 2:
                            deviation(b + 1, 1 - s)
                        norm(b + 1, 1 - s, j - 2)
                    act.wait_ge(s_hb, LEAD + t + 1)
                    nc.scalar.activation(hb[:, j, :], hb[:, j, :], ACT.Copy,
                                         scale=dis[:, bass.ds(t, 1)]).then_inc(s_hd, 1)
                    act.wait_ge(s_hd, t + 1)
                    act.dma_start(HP[bass.ds(t * P, P), :], hb[:, j, :]).then_inc(s_hp[j], 16)
            run(act, part)
            for j in range(TPB):
                act.wait_ge(s_hp[j], LEAD + NB * 16)

        @block.vector
        def _(dve):
            ch = Chain(dve, s_chain)
            nc.vector.tensor_reduce(top[:, :], hmax[:, :], AX.X, ALU.max).then_inc(s_top, 1)
            dve.wait_ge(s_topall, 1)
            ch.link(nc.vector.tensor_scalar(scal[:, 7:8], top[:, :], MIN_RANGE, 1.0 / QP, ALU.max, ALU.mult))
            ch.link(nc.vector.tensor_tensor(scal[:, 8:9], scal[:, 7:8], scal[:, 1:2], ALU.mult))
            ch.link(nc.vector.reciprocal(scal[:, 9:10], scal[:, 7:8]))
            base = ch.n

            def quantise(bb, slot):
                dve.wait_ge(s_hq, LEAD + bb)
                nc.vector.tensor_scalar(hs[:, :], hT[:, bass.ds(bb * BLK, BLK)], scal[0:FFN1, 9:10], MAGIC,
                                        ALU.mult, ALU.add).then_inc(s_hqc, 1)
                dve.wait_ge(s_hqc, LEAD + bb + 1)
                nc.vector.tensor_scalar(hq[0:FFN1, slot, :], hs[:, :], -MAGIC, None, ALU.add).then_inc(s_hq, 1)

            def second(bb, slot, js, n):
                if n == 0:
                    dve.wait_ge(s_x[slot], s_x_count(bb, slot))
                for j in js:
                    dve.wait_ge(s_u, bb * TPB + j + 1)
                    nc.vector.scalar_tensor_tensor(xb[:, slot, j, :], p_u[:, :], scal[:, 8:9], xb[:, slot, j, :],
                                                   ALU.mult, ALU.add).then_inc(s_x2, 1)
                    dve.wait_ge(s_x2, LEAD + bb * TPB + j + 1)
                    for h in range(2):
                        last = nc.vector.bn_stats(st[:, j, h, :], xb[:, slot, j, h * 512:(h + 1) * 512])
                return last

            def s_x_count(bb, slot):
                return (bb - slot) * 8 + 16

            def moments(bb, slot, last):
                ch = Chain(dve, s_chain, bb * CHAIN + base)
                sm = small[:, slot]
                ch.link(last)
                nc.vector.memset(sm[:, 4, :], 0.0)
                for j in range(TPB):
                    last = nc.vector.bn_aggr(mv[:, j, :], st[:, j])
                ch.link(last)
                ch.link(nc.vector.tensor_scalar(sm[:, 0, :], mv[:, :, 1], LN_EPS, None, ALU.add))
                dve.sem_inc(s_var, 1)
                ch.link(nc.vector.tensor_scalar(sm[:, 3, :], mv[:, :, 0], -YSCALE, None, ALU.mult))
                dve.wait_ge(s_sd, bb + 1)
                rsqrt_rest(nc, ch, sm[:, 0, :], sm[:, 1, :], sm[:, 2, :], sm[:, 4, :])
                ch.link(nc.vector.tensor_tensor(sm[:, 3, :], sm[:, 3, :], sm[:, 2, :], ALU.mult))
                nc.vector.tensor_scalar(sm[:, 2, :], sm[:, 2, :], YSCALE, None, ALU.mult).then_inc(s_mean, 1)
                assert ch.n == CHAIN, ch.n

            def low(t, u):
                dve.wait_ge(s_hi, LEAD + t + 1)
                nc.vector.tensor_tensor(ylo[:, u, :], p_t[:, :], yhi[:, u, :], ALU.subtract).then_inc(s_lo, 1)

            quantise(0, 0)
            quantise(1, 1)
            moments(0, 0, second(0, 0, range(TPB), 0))
            low(0, 0)
            dve.wait_ge(s_w, 16)

            def edge_indices():
                ch = Chain(dve, s_prep)
                cols, prev, idx = by.cols, by.prev, by.idx
                dve.wait_ge(s_ends, 16 * 5)
                ch.link(nc.vector.tensor_copy(idx[:, 0, :], cols[:, 0, :]))
                dve.sem_inc(s_eidx, 1)
                nc.vector.memset(prev[:, 0:1], 0.0)
                nc.vector.tensor_copy(idx[:, 1, :], cols[:, 1, :])
                ch.link(nc.vector.tensor_scalar(prev[:, 1:1 + ET], cols[:, 0, :], 1.0, None, ALU.add))
                nc.vector.tensor_scalar(prev[:, :], prev[:, :], e127[:, 0:1], -1.0, ALU.mult, ALU.add)
                ch.link(nc.vector.tensor_tensor(cols[:, 3, :], cols[:, 0, :], cols[:, 2, :], ALU.is_equal))
                ch.link(nc.vector.tensor_scalar(cols[:, 3, :], cols[:, 3, :], SKIP, None, ALU.mult))
                ch.link(nc.vector.tensor_tensor(cols[:, 3, :], cols[:, 3, :], cols[:, 0, :], ALU.add))
                ch.link(nc.vector.tensor_copy(idx[:, 2, :], cols[:, 3, :]))

            edge_indices()

            def part(i, s, front, more):
                b = i * 2 + s
                for j in range(TPB):
                    t = b * TPB + j
                    if j < TPB - 1 or front:
                        low(t + 1, (j + 1) % 2)
                    if front and j < TPB - 1:
                        last = second(b + 1, 1 - s, ((0,), (1, 2), (3,))[j], j)
                        if j == 2:
                            moments(b + 1, 1 - s, last)
                    if more and j == TPB - 1:
                        quantise(b + 2, s)
                    dve.wait_ge(s_h, LEAD + t + 1)
                    dve.wait_ge(s_hp[j], LEAD + b * 16)
                    nc.vector.scalar_tensor_tensor(hb[:, j, :], p_h[:, j % 2, :], gscale[:, 1:2], brow[:, :],
                                                   ALU.mult, ALU.add).then_inc(s_hb, 1)
                    dve.wait_ge(s_hd, t + 1)
                    nc.vector.scalar_tensor_tensor(xb[:, s, j, :], hb[:, j, :], dis[:, bass.ds(t, 1)],
                                                   xb[:, s, j, :], ALU.mult, ALU.add).then_inc(s_fin, 1)
            run(dve, part)


def edges(nc, made, s_g, s_sct, X3, HP, sorted_src, by):
    sb, ps, sem = made
    LAG = ESLOTS // 2
    MASKS = 4
    KB = sb("KB_e", [P, EP])
    H = sb("H_e", [P, ESLOTS, D])
    X = sb("X_e", [P, ESLOTS, D])
    OS = sb("OS_e", [P, 2, D])
    SM = sb("SM_e", [P, MASKS, 2, P])
    p_o = ps("p_o_e", [P, 2, D])
    s_in = sem("e_loaded")
    s_zero = sem("e_sums_zeroed")
    s_sm = sem("e_masks")
    s_o = sem("e_sums")
    s_oe = sem("e_sums_copied")
    s_res = sem("e_rows_ready")

    def run(eng, part):
        with eng.Fori(0, ET // ESLOTS - 1) as i:
            for s in range(ESLOTS):
                part(i * ESLOTS + s, s, ESLOTS)
        for s in range(ESLOTS):
            part(ET - ESLOTS + s, s, ESLOTS - 1 - s)

    with nc.Block() as block:
        @block.sync
        def _(sp):
            for s in (s_oe, s_res, s_o):
                sp.sem_inc(s, LEAD)
            sp.dma_start(KB[:, :], sorted_src[:, 0].partition_broadcast(P)).then_inc(s_in, 16)

        @block.gpsimd
        def _(pool):
            def scatter(t):
                s = t % ESLOTS
                pool.wait_ge(s_res, LEAD + t + 1)
                nc.gpsimd.indirect_dma_start(X3, bass.IndirectOffsetOnAxis(ap=by.idx[:, 2, t:t + 1], axis=0),
                                             X[:, s, :], None, bounds_check=NP - 1, oob_is_err=False
                                             ).then_inc(s_sct[s], 16)

            for t in range(ET):
                s = t % ESLOTS
                if t >= ESLOTS:
                    pool.wait_ge(s_o, LEAD + t - ESLOTS + 1)
                    pool.wait_ge(s_sct[s], t // ESLOTS * 16)
                nc.gpsimd.indirect_dma_start(H[:, s, :], None, HP, bass.IndirectOffsetOnAxis(
                    ap=by.idx[:, 1, t:t + 1], axis=0)).then_inc(s_g[s], 16)
                nc.gpsimd.indirect_dma_start(X[:, s, :], None, X3, bass.IndirectOffsetOnAxis(
                    ap=by.idx[:, 0, t:t + 1], axis=0)).then_inc(s_g[s], 16)
                if t >= LAG:
                    scatter(t - LAG)
            for t in range(ET - LAG, ET):
                scatter(t)
            for s in range(ESLOTS):
                pool.wait_ge(s_sct[s], ET // ESLOTS * 16)

        @block.vector
        def _(dve):
            nc.vector.memset(OS[:, :, :], 0.0).then_inc(s_zero, 1)
            dve.wait_ge(s_in, 16)

            def masks(t, s):
                kb = KB[:, bass.ds(t * P, P)]
                dve.wait_ge(s_o, LEAD + t - MASKS + 1)
                nc.vector.tensor_scalar(SM[:, s, 0, :], kb, by.cols[:, 0, bass.ds(t, 1)], None, ALU.is_equal)
                nc.vector.tensor_scalar(SM[:, s, 1, :], kb, by.prev[:, bass.ds(t, 1)], None,
                                        ALU.is_equal).then_inc(s_sm, 1)

            masks(0, 0)
            masks(1, 1)

            def part(t, s, left):
                if left > 1:
                    masks(t + 2, (s + 2) % MASKS)
                dve.wait_ge(s_g[s], (t - s) * (32 // ESLOTS) + 32)
                dve.wait_ge(s_oe, LEAD + t + 1)
                nc.vector.scalar_tensor_tensor(X[:, s, :], OS[:, s % 2, :], by.dis[:, bass.ds(t, 1)], X[:, s, :],
                                               ALU.mult, ALU.add).then_inc(s_res, 1)
            run(dve, part)

        @block.scalar
        def _(act):
            def part(t, s, left):
                act.wait_ge(s_o, LEAD + t + 1)
                act.wait_ge(s_res, LEAD + t - 1)
                nc.scalar.activation(OS[:, s % 2, :], p_o[:, s % 2, :], ACT.Copy).then_inc(s_oe, 1)
            act.wait_ge(s_zero, 1)
            run(act, part)

        @block.tensor
        def _(pe):
            def within(t, s):
                pe.wait_ge(s_sm, t + 1)
                pe.wait_ge(s_g[s], (t - s) * (32 // ESLOTS) + 32)
                pe.wait_ge(s_oe, LEAD + t - 1)
                for h in range(2):
                    c = slice(h * 512, (h + 1) * 512)
                    nc.tensor.matmul(p_o[:, s % 2, c], SM[:, s % MASKS, 0, :], H[:, s, c], start=True, stop=False)

            def carry(t, s):
                pe.wait_ge(s_oe, LEAD + t)
                for h in range(2):
                    c = slice(h * 512, (h + 1) * 512)
                    last = nc.tensor.matmul(p_o[:, s % 2, c], SM[:, s % MASKS, 1, :], OS[:, 1 - s % 2, c],
                                            start=False, stop=True)
                last.then_inc(s_o, 1)

            pe.wait_ge(s_zero, 1)
            within(0, 0)

            def part(t, s, left):
                carry(t, s)
                if left:
                    within(t + 1, (s + 1) % ESLOTS)
            run(pe, part)


def gated(nc, made, X3, w_gateT, w_upT, w_downT, ident, out):
    sb, ps, sem = made
    M = UPROW + FFN2
    SLOTS = 4
    HALF = BLK // 2
    LOW = 2.0 ** 11
    HBITS = 14
    HSCALE = 2.0 ** (HBITS - 20)
    wi = sb("wi", [P, KT, M], I32)
    wf = sb("wf", [P, KT, M])
    wh = sb("wh_g", [P, KT, M], FP16)
    wl = sb("wl_g", [P, KT, M], FP16)
    top = sb("top_g", [P, 2])
    unit = sb("unit_g", [P, 2])
    inv = sb("inv_g", [P, 2])
    scale = sb("scale_g", [P, 3])
    di = sb("di", [FFN2, D], I32)
    wd = sb("wd_g", [FFN2, D])
    wdh = sb("wdh_g", [M, D], FP16)
    wdl = sb("wdl_g", [FFN2, D], FP16)
    xb = sb("xb_g", [P, SLOTS, TPB, D])
    y = sb("y_g", [P, 2, D])
    yhi = sb("yhi_g", [P, 2, KT, BLK], FP16)
    ylo = sb("ylo_g", [P, 2, KT, BLK], FP16)
    silu = sb("silu_g", [FFN2, 2, HALF])
    hid = sb("hid_g", [FFN2, 2, HALF])
    hh = sb("hh_g", [M, 2, BLK], FP16)
    st = sb("st_g", [P, TPB, 2, 6])
    mv = sb("mv_g", [P, TPB, 2])
    small = sb("small_g", [P, 2, 5, TPB])
    p_t = ps("p_t_g", [P, 2, D])
    p_g = ps("p_g", [P, 2, 512])
    p_o = ps("p_o_g", [P, D])
    s_w = sem("gated_weights")
    s_wz = sem("gated_zeros")
    s_top = sem("gated_top")
    s_topall = sem("gated_top_all")
    s_wf = sem("gated_weights_ready")
    s_chain = sem("gated_chain")
    s_x = [sem(f"g_x3_loaded{s}") for s in range(SLOTS * TPB)]
    s_out = [sem(f"out_stored{s}") for s in range(2)]
    s_var = sem("g_var")
    s_sd = sem("g_sd")
    s_mean = sem("g_mean")
    s_y = sem("g_normed")
    s_t = sem("g_y_turned")
    s_hi = sem("g_high_ready")
    s_lo = sem("g_low_ready")
    s_gu = sem("gate_up_in_psum")
    s_si = sem("silu_ready")
    s_hid = sem("hidden_ready")
    s_hhi = sem("hidden_high_ready")
    s_hh = sem("hidden_low_ready")
    s_o = sem("g_out_in_psum")
    s_fin = sem("g_out_ready")
    leads = (*s_out, s_t, s_lo, s_hh, s_fin, s_gu, s_o, s_y)
    CHAIN = STAT_STEPS + 1

    def run(eng, part, before=True):
        if before:
            part(-2, -2, NB)
            part(-1, -1, NB)
        with eng.Fori(0, NB // SLOTS - 1) as i:
            for s in range(SLOTS):
                part(i * SLOTS + s, s, NB)
        for s in range(SLOTS):
            part(NB - SLOTS + s, s, SLOTS - 1 - s)

    def tile_rows(ap, t):
        return ap[bass.ds(t * P, P), :] if type(t) is not int else ap[t * P:(t + 1) * P, :]

    with nc.Block() as block:
        @block.sync
        def _(sp):
            for s in leads:
                sp.sem_inc(s, LEAD)
            sp.wait_ge(s_wz, 1)
            for t in range(SLOTS * TPB - 1):
                sp.dma_start(xb[:, t // TPB, t % TPB, :], tile_rows(X3, t)).then_inc(s_x[t], 16)
                if t == TPB - 1:
                    for w, c in ((w_gateT, 0), (w_upT, UPROW)):
                        sp.dma_start(wi[:, :, c:c + FFN2], w.rearrange("(k p) h -> p k h", p=P)).then_inc(s_w, 16)
                    sp.dma_start(di[:, :], w_downT).then_inc(s_w, 16)

            def part(b, s, left):
                for j in range(TPB):
                    sp.wait_ge(s_fin, LEAD + b * TPB + j + 1)
                    sp.dma_start(tile_rows(out, b * TPB + j), xb[:, s, j, :]).then_inc(s_out[j % 2], 16)
                    if left == NB or left == SLOTS - 1 and j == 0:
                        sp.wait_ge(s_out[(j - 1) % 2], LEAD + b * 32 + (j + 1) // 2 * 16)
                        n = (s * TPB + j - 1) % (SLOTS * TPB)
                        sp.dma_start(xb[:, n // TPB, n % TPB, :], tile_rows(X3, b * TPB + j + SLOTS * TPB - 1)
                                     ).then_inc(s_x[n], 16)
                    elif left != NB:
                        sp.wait_ge(s_out[(j - 1) % 2], LEAD + b * 32 + (j + 1) // 2 * 16)
            run(sp, part, False)
            for s in range(2):
                sp.wait_ge(s_out[s], LEAD + NT // 2 * 16)

        @block.gpsimd
        def _(pool):
            nc.gpsimd.memset(wi[:, :, :], 0).then_inc(s_wz, 1)
            pool.wait_ge(s_top, 1)
            nc.gpsimd.partition_all_reduce(top[:, :], top[:, :], P, RMAX).then_inc(s_topall, 1)

        @block.tensor
        def _(pe):
            def turn(b, j):
                t = b * TPB + j
                pe.wait_ge(s_y, LEAD + t + 1)
                pe.wait_ge(s_lo, LEAD + t - 1)
                for k in range(KT):
                    last = nc.tensor.transpose(p_t[:, j % 2, k * P:(k + 1) * P], y[:, j % 2, k * P:(k + 1) * P],
                                               ident[:, :])
                last.then_inc(s_t, 1)

            products = [(yy, ww, k) for yy, ww in ((yhi, wh), (yhi, wl), (ylo, wh)) for k in range(KT)]
            PART = len(products) // 2

            def gate_up(b, u, j):
                h = j // 2
                if j % 2 == 0:
                    pe.wait_ge(s_lo, LEAD + b * TPB + 2 * h + 2)
                    pe.wait_ge(s_hh, LEAD + b * 2 + h - 1)
                c = slice(h * HALF, (h + 1) * HALF)
                for n in range(j % 2 * PART, (j % 2 + 1) * PART):
                    yy, ww, k = products[n]
                    last = nc.tensor.matmul(p_g[0:M, h, 0:HALF], ww[:, k, :], yy[:, u, k, c], start=(n == 0),
                                            stop=(n == 2 * PART - 1))
                if j % 2:
                    last.then_inc(s_gu, 1)

            def down(b, u, j):
                pe.wait_ge(s_hh, LEAD + b * 2 + j // 2 + 1)
                pe.wait_ge(s_fin, LEAD + b * TPB + j)
                c = slice(j * P, (j + 1) * P)
                for h in range(2):
                    half = slice(h * 512, (h + 1) * 512)
                    nc.tensor.matmul(p_o[:, half], hh[:, u, c], wdh[:, half], start=True, stop=False)
                    last = nc.tensor.matmul(p_o[:, half], hh[0:FFN2, u, c], wdl[:, half], start=False, stop=True)
                last.then_inc(s_o, 1)

            def part(b, s, left):
                for j in range(TPB):
                    if s == -1 and j == 0:
                        pe.wait_ge(s_wf, 1)
                    if left > 0 and s != -2:
                        gate_up(b + 1, (s + 1) % 2, j)
                    if s >= 0:
                        down(b, s % 2, j)
                    if left > 1:
                        turn(b + 2, j)
            run(pe, part)

        @block.scalar
        def _(act):
            def deviation(b, u):
                act.wait_ge(s_var, b + 1)
                nc.scalar.activation(small[:, u, 1, :], small[:, u, 0, :], ACT.Sqrt).then_inc(s_sd, 1)

            def norm(b, slot, j):
                act.wait_ge(s_mean, b + 1)
                act.wait_ge(s_t, LEAD + b * TPB + j - 1)
                nc.scalar.activation(y[:, j % 2, :], xb[:, slot, j, :], ACT.Identity,
                                     bias=small[:, slot % 2, 3, j:j + 1],
                                     scale=small[:, slot % 2, 2, j:j + 1]).then_inc(s_y, 1)

            def high(b, u, j):
                act.wait_ge(s_t, LEAD + b * TPB + j + 1)
                if j == 0:
                    act.wait_ge(s_gu, LEAD + b * 2 - 2)
                nc.scalar.activation(yhi[:, u, :, j * P:(j + 1) * P],
                                     p_t[:, j % 2, :].rearrange("p (k n) -> p k n", k=KT), ACT.Copy).then_inc(s_hi, 1)

            def hidden(b, u, h):
                act.wait_ge(s_gu, LEAD + b * 2 + h + 1)
                nc.scalar.activation(silu[:, h, :], p_g[0:FFN2, h, 0:HALF], ACT.Silu,
                                     scale=scale[0:FFN2, 0:1]).then_inc(s_si, 1)
                act.wait_ge(s_hid, b * 2 + h + 1)
                act.wait_ge(s_o, LEAD + b * TPB - TPB)
                nc.scalar.activation(hh[0:FFN2, u, h * HALF:(h + 1) * HALF], hid[:, h, :], ACT.Copy,
                                     scale=1.0 / LOW).then_inc(s_hhi, 1)

            deviation(0, 0)

            def part(b, s, left):
                for j in range(TPB):
                    if left > 1:
                        norm(b + 2, (s + 2) % SLOTS, j)
                    if left > 2 and j == 3:
                        deviation(b + 3, (s + 3) % 2)
                    if left > 0 and s != -2 and j % 2:
                        hidden(b + 1, (s + 1) % 2, j // 2)
                    if left > 1:
                        high(b + 2, s % 2, j)
            run(act, part)

        @block.vector
        def _(dve):
            def stats(b, slot, j):
                dve.wait_ge(s_x[slot * TPB + j], (b - slot) * 4 + 16)
                for h in range(2):
                    last = nc.vector.bn_stats(st[:, j, h, :], xb[:, slot, j, h * 512:(h + 1) * 512])
                return last

            def variance(b, slot, last, base):
                ch = Chain(dve, s_chain, b * CHAIN + base)
                sm = small[:, slot % 2]
                ch.link(last)
                dve.wait_ge(s_y, LEAD + b * TPB - TPB)
                nc.vector.memset(sm[:, 4, :], 0.0)
                for j in range(TPB):
                    last = nc.vector.bn_aggr(mv[:, j, :], st[:, j])
                ch.link(last)
                ch.link(nc.vector.tensor_scalar(sm[:, 0, :], mv[:, :, 1], LN_EPS, None, ALU.add))
                dve.sem_inc(s_var, 1)
                ch.link(nc.vector.tensor_scalar(sm[:, 3, :], mv[:, :, 0], -YSCALE, None, ALU.mult))
                return ch

            def scales(b, slot, base):
                ch = Chain(dve, s_chain, b * CHAIN + base + 4)
                sm = small[:, slot % 2]
                dve.wait_ge(s_sd, b + 1)
                rsqrt_rest(nc, ch, sm[:, 0, :], sm[:, 1, :], sm[:, 2, :], sm[:, 4, :])
                ch.link(nc.vector.tensor_tensor(sm[:, 3, :], sm[:, 3, :], sm[:, 2, :], ALU.mult))
                nc.vector.tensor_scalar(sm[:, 2, :], sm[:, 2, :], YSCALE, None, ALU.mult).then_inc(s_mean, 1)
                assert ch.n + 4 == CHAIN, ch.n

            def low(b, u, j):
                dve.wait_ge(s_hi, b * TPB + j + 1)
                c = slice(j * P, (j + 1) * P)
                nc.vector.tensor_tensor(ylo[:, u, :, c], p_t[:, j % 2, :].rearrange("p (k n) -> p k n", k=KT),
                                        yhi[:, u, :, c], ALU.subtract).then_inc(s_lo, 1)

            def hidden(b, u, h):
                dve.wait_ge(s_si, b * 2 + h + 1)
                nc.vector.scalar_tensor_tensor(hid[:, h, :], p_g[UPROW:M, h, 0:HALF], scale[0:FFN2, 1:2],
                                               silu[:, h, :], ALU.mult, ALU.mult).then_inc(s_hid, 1)
                dve.wait_ge(s_hhi, b * 2 + h + 1)
                c = slice(h * HALF, (h + 1) * HALF)
                nc.vector.scalar_tensor_tensor(hh[UPROW:M, u, c], hh[0:FFN2, u, c], -LOW, hid[:, h, :], ALU.mult,
                                               ALU.add).then_inc(s_hh, 1)

            def finish(b, s, j):
                dve.wait_ge(s_o, LEAD + b * TPB + j + 1)
                nc.vector.scalar_tensor_tensor(xb[:, s, j, :], p_o[:, :], scale[:, 2:3], xb[:, s, j, :], ALU.mult,
                                               ALU.add).then_inc(s_fin, 1)

            for j in range(TPB):
                last = stats(0, 0, j)
            variance(0, 0, last, 0)
            scales(0, 0, 0)
            ch = Chain(dve, s_chain, CHAIN)
            ch.link(nc.vector.memset(top[:, :], 0.0))
            dve.wait_ge(s_w, 48)
            ch.link(nc.vector.tensor_copy(wf[:, :, :], wi[:, :, :]))
            ch.link(nc.vector.tensor_scalar(wf[:, :, :], wf[:, :, :], 1.0 / QP, None, ALU.mult))
            ch.link(nc.vector.tensor_copy(wd[:, :], di[:, :]))
            ch.link(nc.vector.tensor_scalar(wd[:, :], wd[:, :], 1.0 / QP, None, ALU.mult))
            nc.vector.tensor_reduce(top[:, 0:1], wf[:, :, :], AX.XY, ALU.max, apply_absolute_value=True)
            ch.link(nc.vector.tensor_reduce(top[0:FFN2, 1:2], wd[:, :], AX.X, ALU.max, apply_absolute_value=True))
            dve.sem_inc(s_top, 1)
            ch.link(nc.vector.memset(hh[:, :, :], 0.0))
            ch.link(nc.vector.memset(wdh[:, :], 0.0))
            dve.wait_ge(s_topall, 1)
            ch.link(nc.vector.tensor_scalar(unit[:, :], top[:, :], 1.0 / QP, 1.0 / WMAX, ALU.max, ALU.mult))
            ch.link(nc.vector.reciprocal(inv[:, :], unit[:, :]))
            ch.link(nc.vector.tensor_scalar(wf[:, :, :], wf[:, :, :], inv[:, 0:1], None, ALU.mult))
            ch.link(nc.vector.tensor_copy(wh[:, :, :], wf[:, :, :]))
            ch.link(nc.vector.tensor_tensor(wl[:, :, :], wf[:, :, :], wh[:, :, :], ALU.subtract))
            ch.link(nc.vector.tensor_scalar(wd[:, :], wd[:, :], inv[0:FFN2, 1:2], None, ALU.mult))
            ch.link(nc.vector.tensor_copy(wdh[0:FFN2, :], wd[:, :]))
            ch.link(nc.vector.tensor_tensor(wdl[:, :], wd[:, :], wdh[0:FFN2, :], ALU.subtract))
            ch.link(nc.vector.tensor_scalar(wdh[UPROW:M, :], wdh[0:FFN2, :], 1.0 / LOW, None, ALU.mult))
            ch.link(nc.vector.tensor_scalar(scale[:, 0:1], unit[:, 0:1], 1.0 / YSCALE, None, ALU.mult))
            ch.link(nc.vector.tensor_scalar(scale[:, 1:2], inv[:, 0:1], inv[:, 0:1], HSCALE * LOW / WMAX ** 2,
                                            ALU.mult, ALU.mult))
            ch.link(nc.vector.tensor_scalar(scale[:, 1:2], scale[:, 1:2], scale[:, 0:1], None, ALU.mult))
            ch.link(nc.vector.tensor_scalar(scale[:, 2:3], unit[:, 0:1], unit[:, 0:1], WMAX ** 2 / HSCALE,
                                            ALU.mult, ALU.mult))
            ch.link(nc.vector.tensor_scalar(scale[:, 2:3], scale[:, 2:3], unit[:, 1:2], None, ALU.mult))
            dve.sem_inc(s_wf, 1)
            base = ch.n

            def part(b, s, left):
                slot = (s + 3) % SLOTS
                for j in range(TPB):
                    if j == 0:
                        if left > 0 and s != -2:
                            low(b + 1, (s + 1) % 2, TPB - 1)
                    elif left > 1:
                        low(b + 2, s % 2, j - 1)
                    if left > 2 and j == 3:
                        scales(b + 3, slot, base)
                    if left > 0 and s != -2 and j % 2:
                        hidden(b + 1, (s + 1) % 2, j // 2)
                    if s >= 0:
                        finish(b, s, j)
                    if left > 2 and j < 3:
                        for u in ((0, 1), (2,), (3,))[j]:
                            last = stats(b + 3, slot, u)
                        if j == 2:
                            variance(b + 3, slot, last, base)
            run(dve, part)


def kernel(x, src, dst, L0_gnn_rms_w, L0_gnn_W_down, L0_gnn_Wl, L0_gnn_Wr, L0_gnn_att, L0_gnn_W_up, L0_ffn_w1,
           L0_ffn_b1, L0_ffn_w2, L0_ffn_b2, L1_gnn_W, L1_gnn_b, L1_ffn_w_gate, L1_ffn_w_up, L1_ffn_w_down):
    import numpy as np
    import concourse.bacc as bacc
    from concourse import mybir as mb
    from concourse.bass_utils import run_bass_kernel_spmd

    def lay(a):
        return np.ascontiguousarray(np.asarray(a))

    xp = np.zeros((NP, D), np.float32)
    xp[:N] = np.asarray(x)
    ends = []
    for e in (src, dst):
        p = np.full((EP,), NP - 1, np.int32)
        p[:E] = np.asarray(e)
        ends.append(p)
    arrays = {
        "x": xp, "xT": lay(xp.T),
        "src_row": ends[0], "dst_row": ends[1],
        "src_col": lay(ends[0].reshape(ET, P).T), "dst_col": lay(ends[1].reshape(ET, P).T),
        "rms_w": lay(np.asarray(L0_gnn_rms_w).reshape(KT, P).T),
        "W_down": lay(L0_gnn_W_down), "Wl": lay(L0_gnn_Wl), "Wr": lay(L0_gnn_Wr),
        "att": lay(L0_gnn_att).reshape(HID), "W_up": lay(L0_gnn_W_up),
        "w1T": lay(np.asarray(L0_ffn_w1).T), "b1": lay(L0_ffn_b1).reshape(FFN1, 1),
        "w2T": lay(np.asarray(L0_ffn_w2).T), "b2": lay(L0_ffn_b2).reshape(1, D),
        "gcnT": lay(np.asarray(L1_gnn_W).T), "gcn_b": lay(L1_gnn_b).reshape(D),
        "w_gateT": lay(np.asarray(L1_ffn_w_gate).T), "w_upT": lay(np.asarray(L1_ffn_w_up).T),
        "w_downT": lay(np.asarray(L1_ffn_w_down).T),
        "ident_in": np.eye(P, dtype=np.float32),
    }
    nc = bacc.Bacc("TRN2", target_bir_lowering=False, num_devices=1)
    feeds, args = {}, {}
    for name, a in arrays.items():
        feeds[f"in_{name}"] = a
        args[name] = nc.dram_tensor(f"in_{name}", a.shape, mb.dt.from_np(a.dtype), kind="ExternalInput").ap()
    args["out"] = nc.dram_tensor("out_rows", [NP, D], mb.dt.float32, kind="ExternalOutput").ap()
    build(nc, **args)
    r = run_bass_kernel_spmd(nc, [feeds], core_ids=[0])
    return r.results[0]["out_rows"][:N]
```
